# Optimizing a Trainium2 kernel written in Bass

```python
import numpy as np
import jax
import jax.numpy as jnp

def _softmax(x, axis=-1):
    return jax.nn.softmax(x, axis=axis)

def _gelu(x):
    return jax.nn.gelu(x, approximate=True)

def _silu(x):
    return jax.nn.silu(x)

def _sigmoid(x):
    return jax.nn.sigmoid(x)

def _layernorm(x, axis=-1, eps=1e-05):
    m = jnp.mean(x, axis=axis, keepdims=True)
    v = jnp.var(x, axis=axis, keepdims=True)
    return (x - m) / jnp.sqrt(v + eps)

def _scatter_add(tgt, idx, src, axis=0):
    return tgt.at[idx].add(src)

def _segment_sum(src, seg, n):
    return jax.ops.segment_sum(src, seg, n)
kernel_name = 'mk_gnn_resnorm_d2_gnn_r8_b19226'

def setup_inputs(seed: int=0):
    np.random.seed(seed)
    _w = jnp.asarray

    def _rec_inputs():
        import jax
        import jax.numpy as jnp
        _gk = jax.random.key(seed)
        x = -0.0003713 + 1 * jax.random.normal(jax.random.fold_in(_gk, 1), (6250, 128), jnp.float32)
        _s = jax.random.randint(jax.random.fold_in(_gk, 2), (50000,), 0, 6250, jnp.int32)
        _d = jax.random.randint(jax.random.fold_in(_gk, 3), (50000,), 0, 6250, jnp.int32)
        _loop = jnp.arange(6250, dtype=jnp.int32)
        src = jnp.concatenate([_s, _d, _loop])
        dst = jnp.concatenate([_d, _s, _loop])
        _o = jnp.argsort(dst, stable=True)
        src = src[_o]
        dst = dst[_o]
        edge_attr_128 = -5.16925e-05 + 1.00005 * jax.random.normal(jax.random.fold_in(_gk, 11), (106250, 128), jnp.float32)
        return (x, src, dst, edge_attr_128)
    x, src, dst, edge_attr_128 = _rec_inputs()

    def _L0_gnn_setup():
        import jax, jax.numpy as jnp
        import numpy as np
        import math
        N_NODES = 12500
        N_EDGES = 200000
        DIM = 128
        key = jax.random.key(seed)
        ks = jax.random.split(key, 6)
        x = jax.random.normal(ks[0], (N_NODES, DIM), dtype=jnp.float32)
        edge_index = jax.random.randint(ks[1], (2, N_EDGES), 0, N_NODES, dtype=jnp.int64)
        limit = 0.1 * math.sqrt(6.0 / (DIM + DIM))
        Wqk = jax.random.uniform(ks[2], (DIM, DIM), dtype=jnp.float32, minval=-limit, maxval=limit)
        Wv = jax.random.uniform(ks[3], (DIM, DIM), dtype=jnp.float32, minval=-limit, maxval=limit)
        Wo = jax.random.uniform(ks[4], (DIM, DIM), dtype=jnp.float32, minval=-limit, maxval=limit)
        return {'x': x, 'edge_index': edge_index, 'Wqk': Wqk, 'bqk': jnp.zeros((DIM,), jnp.float32), 'Wv': Wv, 'bv': jnp.zeros((DIM,), jnp.float32), 'Wo': Wo, 'bo': jnp.zeros((DIM,), jnp.float32), 'gamma': jnp.ones((DIM,), jnp.float32), 'beta': jnp.zeros((DIM,), jnp.float32)}
    _L0_gnn_all = _L0_gnn_setup()
    _L0_gnn_in = {k: v for k, v in _L0_gnn_all.items() if k in ('Wqk', 'bqk', 'Wv', 'bv', 'Wo', 'bo', 'gamma', 'beta')}
    del _L0_gnn_all

    def _L1_gnn_setup():
        import jax, jax.numpy as jnp
        import numpy as np
        N, E, D, H = (6250, 100000, 128, 8)
        C = D // H
        NEG_SLOPE = 0.2
        EPS = 1e-05

        def _layer_norm(x, w):
            mu = x.mean(-1, keepdims=True)
            var = ((x - mu) ** 2).mean(-1, keepdims=True)
            return (x - mu) / jnp.sqrt(var + EPS) * w
        key = jax.random.key(seed)
        ks = jax.random.split(key, 9)
        s = 0.05
        return {'x': jax.random.normal(ks[0], (N, D), dtype=jnp.float32), 'edge_index': jax.random.randint(ks[1], (2, E), 0, N, dtype=jnp.int32), 'edge_attr': jax.random.normal(ks[2], (E, D), dtype=jnp.float32), 'ln1_w': jnp.ones((D,), jnp.float32), 'lin_l_w': jax.random.normal(ks[3], (D, D), dtype=jnp.float32) * s, 'lin_l_b': jnp.zeros((D,), jnp.float32), 'lin_r_w': jax.random.normal(ks[4], (D, D), dtype=jnp.float32) * s, 'lin_r_b': jnp.zeros((D,), jnp.float32), 'lin_edge_w': jax.random.normal(ks[5], (D, D), dtype=jnp.float32) * s, 'att': jax.random.normal(ks[6], (H, C), dtype=jnp.float32) * s, 'attn_bias': jnp.zeros((D,), jnp.float32), 'ln2_w': jnp.ones((D,), jnp.float32), 'fc_w': jax.random.normal(ks[7], (4 * D, D), dtype=jnp.float32) * s, 'proj_w': jax.random.normal(ks[8], (D, 4 * D), dtype=jnp.float32) * s}
    _L1_gnn_all = _L1_gnn_setup()
    _L1_gnn_in = {k: v for k, v in _L1_gnn_all.items() if k in ('ln1_w', 'lin_l_w', 'lin_l_b', 'lin_r_w', 'lin_r_b', 'lin_edge_w', 'att', 'attn_bias', 'ln2_w', 'fc_w', 'proj_w')}
    del _L1_gnn_all
    return {'x': x, 'src': src, 'dst': dst, 'edge_attr_128': edge_attr_128, 'L0_gnn_Wqk': _L0_gnn_in['Wqk'], 'L0_gnn_bqk': _L0_gnn_in['bqk'], 'L0_gnn_Wv': _L0_gnn_in['Wv'], 'L0_gnn_bv': _L0_gnn_in['bv'], 'L0_gnn_Wo': _L0_gnn_in['Wo'], 'L0_gnn_bo': _L0_gnn_in['bo'], 'L0_gnn_gamma': _L0_gnn_in['gamma'], 'L0_gnn_beta': _L0_gnn_in['beta'], 'L1_gnn_ln1_w': _L1_gnn_in['ln1_w'], 'L1_gnn_lin_l_w': _L1_gnn_in['lin_l_w'], 'L1_gnn_lin_l_b': _L1_gnn_in['lin_l_b'], 'L1_gnn_lin_r_w': _L1_gnn_in['lin_r_w'], 'L1_gnn_lin_r_b': _L1_gnn_in['lin_r_b'], 'L1_gnn_lin_edge_w': _L1_gnn_in['lin_edge_w'], 'L1_gnn_att': _L1_gnn_in['att'], 'L1_gnn_attn_bias': _L1_gnn_in['attn_bias'], 'L1_gnn_ln2_w': _L1_gnn_in['ln2_w'], 'L1_gnn_fc_w': _L1_gnn_in['fc_w'], 'L1_gnn_proj_w': _L1_gnn_in['proj_w']}

def reference(x, src, dst, edge_attr_128, L0_gnn_Wqk, L0_gnn_bqk, L0_gnn_Wv, L0_gnn_bv, L0_gnn_Wo, L0_gnn_bo, L0_gnn_gamma, L0_gnn_beta, L1_gnn_ln1_w, L1_gnn_lin_l_w, L1_gnn_lin_l_b, L1_gnn_lin_r_w, L1_gnn_lin_r_b, L1_gnn_lin_edge_w, L1_gnn_att, L1_gnn_attn_bias, L1_gnn_ln2_w, L1_gnn_fc_w, L1_gnn_proj_w):
    import jax
    import jax.numpy as jnp

    def _L0_gnn_ref(x, edge_index, Wqk, bqk, Wv, bv, Wo, bo, gamma, beta):
        import jax, jax.numpy as jnp
        import numpy as np
        import math
        N_NODES = 12500
        N_EDGES = 200000
        DIM = 128
        N, D = x.shape
        qk = x @ Wqk + bqk
        v = x @ Wv + bv
        src = edge_index[0]
        dst = edge_index[1]
        scores = jnp.sum(qk[dst] * qk[src], axis=-1) / jnp.sqrt(jnp.float32(D))
        scores = jnp.clip(scores, -5.0, 5.0)
        m = jax.ops.segment_max(scores, dst, num_segments=N)
        e = jnp.exp(scores - m[dst])
        s = jax.ops.segment_sum(e, dst, num_segments=N)
        attn = e / s[dst]
        out = jax.ops.segment_sum(attn[:, None] * v[src], dst, num_segments=N)
        out = out @ Wo + bo
        h = out + x
        mu = jnp.mean(h, axis=-1, keepdims=True)
        var = jnp.mean(jnp.square(h - mu), axis=-1, keepdims=True)
        return gamma * (h - mu) / jnp.sqrt(var + 1e-05) + beta

    def _L1_gnn_ref(x, edge_index, edge_attr, ln1_w, lin_l_w, lin_l_b, lin_r_w, lin_r_b, lin_edge_w, att, attn_bias, ln2_w, fc_w, proj_w):
        import jax, jax.numpy as jnp
        import numpy as np
        N, E, D, H = (6250, 100000, 128, 8)
        C = D // H
        NEG_SLOPE = 0.2
        EPS = 1e-05

        def _layer_norm(x, w):
            mu = x.mean(-1, keepdims=True)
            var = ((x - mu) ** 2).mean(-1, keepdims=True)
            return (x - mu) / jnp.sqrt(var + EPS) * w
        n, d = x.shape
        h_heads, c = att.shape
        h = _layer_norm(x, ln1_w)
        xl = (h @ lin_l_w.T + lin_l_b).reshape(n, h_heads, c)
        xr = (h @ lin_r_w.T + lin_r_b).reshape(n, h_heads, c)
        e = (edge_attr @ lin_edge_w.T).reshape(-1, h_heads, c)
        src, dst = (edge_index[0], edge_index[1])
        z = jax.nn.leaky_relu(xl[src] + xr[dst] + e, NEG_SLOPE)
        logits = jnp.einsum('ehc,hc->eh', z, att)
        m = jax.lax.stop_gradient(jax.ops.segment_max(logits, dst, num_segments=n))
        num = jnp.exp(logits - m[dst])
        den = jax.ops.segment_sum(num, dst, num_segments=n)
        alpha = num / den[dst]
        msg = xl[src] * alpha[..., None]
        attn_out = jax.ops.segment_sum(msg, dst, num_segments=n).reshape(n, d) + attn_bias
        x = x + attn_out
        h2 = _layer_norm(x, ln2_w)
        x = x + jax.nn.relu(h2 @ fc_w.T) @ proj_w.T
        return x
    edge_index = jnp.stack([src, dst])
    x = _layernorm(x + _L0_gnn_ref(x, edge_index, L0_gnn_Wqk, L0_gnn_bqk, L0_gnn_Wv, L0_gnn_bv, L0_gnn_Wo, L0_gnn_bo, L0_gnn_gamma, L0_gnn_beta), axis=-1)
    x = _layernorm(x + _L1_gnn_ref(x, edge_index, edge_attr_128, L1_gnn_ln1_w, L1_gnn_lin_l_w, L1_gnn_lin_l_b, L1_gnn_lin_r_w, L1_gnn_lin_r_b, L1_gnn_lin_edge_w, L1_gnn_att, L1_gnn_attn_bias, L1_gnn_ln2_w, L1_gnn_fc_w, L1_gnn_proj_w), axis=-1)
    return x

_drawn_inputs = setup_inputs


def setup_inputs(seed=0):
    import zlib

    import numpy as np

    out = dict(_drawn_inputs(seed))
    spreads = {'L0_gnn_bqk': (0.0, 0.8),
     'L0_gnn_bv': (0.0, 0.8),
     'L0_gnn_bo': (0.0, 0.1),
     'L0_gnn_gamma': (1.0, 0.2),
     'L0_gnn_beta': (0.0, 0.1),
     'L1_gnn_ln1_w': (1.0, 0.6),
     'L1_gnn_lin_l_b': (0.0, 0.1),
     'L1_gnn_lin_r_b': (0.0, 2.0),
     'L1_gnn_attn_bias': (0.0, 0.1),
     'L1_gnn_ln2_w': (1.0, 0.2)}
    factors = {'edge_attr_128': 8.0,
     'L0_gnn_Wqk': 64.0,
     'L0_gnn_Wv': 8.0,
     'L0_gnn_Wo': 8.0,
     'L1_gnn_lin_r_w': 8.0,
     'L1_gnn_lin_edge_w': 8.0,
     'L1_gnn_att': 5.255}
    for name, (base, spread) in spreads.items():
        noise = np.random.default_rng([zlib.crc32(name.encode()), seed]).standard_normal(out[name].shape)
        drawn = base * np.exp(spread * noise) if base else spread * noise
        out[name] = jnp.asarray(drawn.astype(out[name].dtype))
    for name, factor in factors.items():
        out[name] = (out[name] * factor).astype(out[name].dtype)
    return out
```

```python
from contextlib import ExitStack

import concourse.bass as bass
from concourse import mybir

F32 = mybir.dt.float32
BF16 = mybir.dt.bfloat16
I32 = mybir.dt.int32
ALU = mybir.AluOpType
ACT = mybir.ActivationFunctionType
AX = mybir.AxisListType

P = 128
HEADS = 8
HC = P // HEADS
CHUNKS = 16
QT = 4
QUADS = CHUNKS // QT
QW = QT * P
BIG = 3.0e38
TINY = 1.0e-30
EPS = 1e-5
DMA = 16


def sizes(nodes, edges):
    groups = -(-edges // (CHUNKS * P))
    node_groups = -(-(nodes + P) // QW)
    return groups, node_groups


def build(nc, t, N, E):
    groups, node_groups = sizes(N, E)
    tiles = groups * CHUNKS
    NP = node_groups * QW
    CW = groups * P

    qkv_tab = nc.dram_tensor("qkv_tab", (NP, 2 * P), F32).ap()
    xl_tab = nc.dram_tensor("xl_tab", (NP, P), F32).ap()
    xr_tab = nc.dram_tensor("xr_tab", (NP, P), F32).ap()
    rel_rows = nc.dram_tensor("rel_rows", (tiles // QT, QW), BF16).ap()
    rel_rows_out = rel_rows.rearrange("q e -> (q e)").rearrange("(p w) -> p w", w=8 * P)
    xl_edges = nc.dram_tensor("xl_edges", (groups, P, CHUNKS * P), F32).ap()
    turn_dram = [nc.dram_tensor(f"turn{i}", (CHUNKS, HEADS), F32).ap() for i in range(6)]

    persistent = ExitStack()

    def keep(name, shape, dt=F32):
        return persistent.enter_context(nc.sbuf_tensor(name, shape, dt))

    iota_row = keep("iota_row", [P, P])
    iota_col = keep("iota_col", [P, 1])
    ident = keep("ident", [P, P])
    ones = keep("ones", [P, P])
    eps_col = keep("eps_col", [P, 1])
    rel_cols = keep("rel_cols", [P, tiles])
    first_row = keep("first_row", [1, tiles], I32)
    src_cols = keep("src_cols", [P, tiles], I32)
    x1 = keep("x1", [P, node_groups, QT, P])

    def window_bases(eng, j, q):
        return nc.values_load_multi_w_load_instructions(
            first_row[0:1, bass.ds(j * CHUNKS + q * QT, QT)], engines=(eng.engine,), min_val=0, max_val=N,
            skip_runtime_bounds_check_because="destinations are node numbers, or N in the padding")[1]

    def groups_of(eng, total, body):
        body(0, True, False)
        with eng.Fori(1, total - 1) as j:
            body(j, False, False)
        body(total - 1, False, True)

    with ExitStack() as ctx:
        sb = lambda name, shape, dt=F32: ctx.enter_context(nc.sbuf_tensor(name, shape, dt))
        sem = lambda name: ctx.enter_context(nc.semaphore(name))
        iota_i = sb("iota_i", [P, P], I32)
        iota_ci = sb("iota_ci", [P, 1], I32)
        dst_cols = sb("dst_cols", [P, tiles], I32)
        first_all = sb("first_all", [P, tiles], I32)
        dst_rows = sb("dst_rows", [tiles // 8, 8, P], I32)
        rel_out = sb("rel_out", [tiles // 8, 8, P], BF16)
        loaded = sem("indices_loaded")
        iota_made = sem("iota_made")
        const_made = sem("const_made")
        rel_made = sem("rel_made")
        rel_stored = sem("rel_stored")
        with nc.Block() as block:
            @block.sync
            def _(sp):
                sp.dma_start(dst_rows[:], t["dst_rows"].rearrange("(p k) e -> p k e", k=8)).then_inc(loaded, DMA)
                sp.dma_start(dst_cols[:], t["dst_cols"]).then_inc(loaded, DMA)
                sp.dma_start(first_all[:], t["first_dst"].to_broadcast([P, tiles])).then_inc(loaded, DMA)
                sp.dma_start(first_row[:], t["first_dst"]).then_inc(loaded, DMA)
                sp.dma_start(src_cols[:], t["src_cols"]).then_inc(loaded, DMA)
                sp.wait_ge(rel_made, 1)
                sp.dma_start(rel_rows_out, rel_out[:].rearrange("p k e -> p (k e)")).then_inc(rel_stored, DMA)
                sp.wait_ge(rel_stored, DMA)
                sp.wait_ge(loaded, 5 * DMA)

            @block.gpsimd
            def _(pool):
                nc.gpsimd.iota(iota_i[:], [[1, P]], base=0, channel_multiplier=0)
                nc.gpsimd.iota(iota_ci[:], [[1, 1]], base=0, channel_multiplier=1).then_inc(iota_made, 1)

            @block.vector
            def _(dve):
                nc.vector.memset(ones[:], 1.0)
                nc.vector.memset(eps_col[:], EPS)
                dve.wait_ge(iota_made, 1)
                nc.vector.tensor_copy(iota_row[:], iota_i[:])
                nc.vector.tensor_copy(iota_col[:], iota_ci[:]).then_inc(const_made, 1)
                dve.wait_ge(const_made, 1)
                nc.vector.tensor_scalar(ident[:], iota_row[:], iota_col[:, 0:1], None, ALU.is_equal)
                dve.wait_ge(loaded, 5 * DMA)
                nc.vector.tensor_tensor(rel_out[:], dst_rows[:], dst_rows[:, :, 0:1].to_broadcast([tiles // 8, 8, P]),
                                        ALU.subtract).then_inc(rel_made, 1)
                nc.vector.tensor_tensor(rel_cols[:], dst_cols[:], first_all[:], ALU.subtract)

    with ExitStack() as ctx:
        sb = lambda name, shape, dt=F32: ctx.enter_context(nc.sbuf_tensor(name, shape, dt))
        ps = lambda name, shape, dt=F32: ctx.enter_context(nc.psum_tensor(name, shape, dt))
        sem = lambda name: ctx.enter_context(nc.semaphore(name))
        w_qkv = sb("w_qkv", [P, 2 * P])
        b_qkv = sb("b_qkv", [P, 2 * P])
        xT = sb("xT", [P, QT, P])
        qkv = sb("qkv", [P, QT, 2 * P])
        qkv_ps = [ps(f"qkv_ps{i}", [P, 512]) for i in range(QT)]
        weights_in = sem("l0_weights_in")
        x_in = [sem(f"x_in{i}") for i in range(QT)]
        multiplied = sem("qkv_multiplied")
        biased = sem("qkv_biased")
        stored = [sem(f"qkv_stored{i}") for i in range(QT)]
        with nc.Block() as block:
            @block.sync
            def _(sp):
                sp.dma_start(w_qkv[:, 0:P], t["Wqk"]).then_inc(weights_in, DMA)
                sp.dma_start(w_qkv[:, P:], t["Wv"]).then_inc(weights_in, DMA)
                sp.dma_start(b_qkv[:, 0:P], t["bqk"].to_broadcast([P, P])).then_inc(weights_in, DMA)
                sp.dma_start(b_qkv[:, P:], t["bv"].to_broadcast([P, P])).then_inc(weights_in, DMA)

                def body(b, first, last):
                    for i in range(QT):
                        if not first:
                            sp.wait_ge(multiplied, b * QT + i - QT + 1)
                        sp.dma_start(xT[:, i, :], t["xT"][:, bass.ds(b * QW + i * P, P)]).then_inc(x_in[i], DMA)
                groups_of(sp, node_groups, body)

            @block.tensor
            def _(pe):
                pe.wait_ge(weights_in, 4 * DMA)

                def body(b, first, last):
                    for i in range(QT):
                        pe.wait_ge(x_in[i], (b + 1) * DMA)
                        if not first:
                            pe.wait_ge(biased, b * QT + i - QT + 1)
                        nc.tensor.matmul(qkv_ps[i][:, 0:2 * P], xT[:, i, :], w_qkv[:], start=True,
                                         stop=True).then_inc(multiplied, 1)
                groups_of(pe, node_groups, body)

            @block.vector
            def _(dve):
                dve.wait_ge(weights_in, 4 * DMA)

                def body(b, first, last):
                    for i in range(QT):
                        dve.wait_ge(multiplied, b * QT + i + 1)
                        if not first:
                            dve.wait_ge(stored[i], b * DMA)
                        nc.vector.tensor_tensor(qkv[:, i, :], qkv_ps[i][:, 0:2 * P], b_qkv[:],
                                                ALU.add).then_inc(biased, 1)
                groups_of(dve, node_groups, body)

            @block.scalar
            def _(act):
                def body(b, first, last):
                    for i in range(QT):
                        act.wait_ge(biased, b * QT + i + 1)
                        act.dma_start(qkv_tab[bass.ds(b * QW + i * P, P), :], qkv[:, i, :]).then_inc(stored[i], DMA)
                groups_of(act, node_groups, body)
                for i in range(QT):
                    act.wait_ge(stored[i], node_groups * DMA)

    sums = ExitStack()
    node_sums = sums.enter_context(nc.sbuf_tensor("node_sums0", [P, 2, NP], F32))
    with ExitStack() as ctx:
        sb = lambda name, shape, dt=F32: ctx.enter_context(nc.sbuf_tensor(name, shape, dt))
        ps = lambda name, shape, dt=F32: ctx.enter_context(nc.psum_tensor(name, shape, dt))
        sem = lambda name: ctx.enter_context(nc.semaphore(name))
        src_ring = sb("src_ring", [P, CHUNKS], I32)
        rows = sb("rows", [P, CHUNKS, 2 * P])
        window = sb("window", [P, CHUNKS, P])
        rel_bc = sb("rel_bc", [P, QUADS, QW], BF16)
        spread = sb("spread", [P, 2, QW])
        gather1 = sb("gather1", [P, 2, QT, P])
        scores = sb("scores", [P, 2, QT])
        clipped = sb("clipped", [P, 2, QT])
        weight = sb("weight", [P, 2, QT])
        product = sb("product", [P, QT, P])
        q_dst = [ps(f"q_dst{i}", [P, QT, P]) for i in range(2)]
        onehot_ps = [ps(f"onehot_ps{i}", [P, QT, P]) for i in range(2)]
        tile_sums = [ps(f"tile_sums{i}", [P, 2, 2, P]) for i in range(4)]
        quads_asked = sem("quads_asked")
        src_ready = [sem(f"src_ready{i}") for i in range(2)]
        gathered = [sem(f"gathered{q}") for q in range(QUADS)]
        window_in = [sem(f"window_in{q}") for q in range(QUADS)]
        spread_made = sem("spread_made")
        q_spread = sem("q_spread")
        onehot_turned = sem("onehot_turned")
        scored = sem("scored")
        clip_done = sem("clip_done")
        weighted = sem("weighted")
        onehot_made = sem("onehot_made")
        summed = sem("summed")
        added = sem("added")
        cleared = sem("cleared")
        with nc.Block() as block:
            @block.sync
            def _(sp):
                def body(j, first, last):
                    for q in range(QUADS):
                        if not first:
                            sp.wait_ge(q_spread, j * QUADS + q - QUADS + 1)
                        sp.dma_start(rel_bc[:, q, :], rel_rows[bass.ds(j * QUADS + q, 1), :].to_broadcast([P, QW])
                                     ).then_inc(window_in[q], DMA)
                        for i, base in enumerate(window_bases(sp, j, q), q * QT):
                            sp.dma_start(window[:, i, :], qkv_tab[bass.ds(base, P), 0:P]).then_inc(window_in[q], DMA)
                groups_of(sp, groups, body)

            @block.gpsimd
            def _(pool):
                def body(j, first, last):
                    for q in range(QUADS):
                        if q % 2 == 0:
                            pool.wait_ge(src_ready[q // 2], j + 1)
                        if not first:
                            pool.wait_ge(summed, j * QUADS + q - QUADS + 1)
                        pool.sem_inc(quads_asked, 1)
                        for i in range(q * QT, q * QT + QT):
                            nc.gpsimd.indirect_dma_start(
                                out=rows[:, i, :], out_offset=None, in_=qkv_tab,
                                in_offset=bass.IndirectOffsetOnAxis(ap=src_ring[:, i:i + 1], axis=0),
                            ).then_inc(gathered[q], DMA)
                groups_of(pool, groups, body)

            @block.scalar
            def _(act):
                def refill(j, half):
                    a = half * CHUNKS // 2
                    nc.scalar.copy(src_ring[:, a:a + CHUNKS // 2],
                                   src_cols[:, bass.ds(j * CHUNKS + a, CHUNKS // 2)]).then_inc(src_ready[half], 1)

                refill(0, 0)
                refill(0, 1)

                def body(j, first, last):
                    for q in range(QUADS):
                        act.wait_ge(clip_done, j * QUADS + q + 1)
                        nc.scalar.activation(weight[:, q % 2, :], clipped[:, q % 2, :], ACT.Exp).then_inc(weighted, 1)
                        act.wait_ge(weighted, j * QUADS + q + 1)
                        act.wait_ge(onehot_turned, j * QUADS + q + 1)
                        if not (first and q < 2):
                            act.wait_ge(summed, j * QUADS + q - 1)
                        for i in range(QT):
                            o = nc.scalar.mul(gather1[:, q % 2, i, :], onehot_ps[q % 2][:, i, :],
                                              weight[:, q % 2, i:i + 1])
                        o.then_inc(onehot_made, 1)
                        if q == 1 and not last:
                            act.wait_ge(gathered[0], (j + 1) * QT * DMA)
                            act.wait_ge(gathered[1], (j + 1) * QT * DMA)
                            refill(j + 1, 0)
                        if q == 3 and not last:
                            act.wait_ge(gathered[2], (j + 1) * QT * DMA)
                            act.wait_ge(gathered[3], (j + 1) * QT * DMA)
                            refill(j + 1, 1)
                groups_of(act, groups, body)

            @block.tensor
            def _(pe):
                def spread_q(j, q, start=False):
                    pe.wait_ge(spread_made, j * QUADS + q + 1)
                    pe.wait_ge(window_in[q], (j + 1) * (QT + 1) * DMA)
                    if not start:
                        pe.wait_ge(scored, j * QUADS + q - 1)
                    for i in range(QT):
                        mm = nc.tensor.matmul(q_dst[q % 2][:, i, :], spread[:, q % 2, i * P:(i + 1) * P],
                                              window[:, q * QT + i, :], start=True, stop=True)
                    mm.then_inc(q_spread, 1)
                    if not start:
                        pe.wait_ge(onehot_made, j * QUADS + q - 1)
                    for i in range(QT):
                        mm = nc.tensor.transpose(onehot_ps[q % 2][:, i, :], spread[:, q % 2, i * P:(i + 1) * P],
                                                 ident[:])
                    mm.then_inc(onehot_turned, 1)

                def add_up(j, q, start):
                    pe.wait_ge(onehot_made, j * QUADS + q + 1)
                    pe.wait_ge(gathered[q], (j + 1) * QT * DMA)
                    if not start:
                        pe.wait_ge(added, (j * QUADS + q - 1) * QT)
                    for i in range(QT):
                        bank = tile_sums[(q % 2) * 2 + i // 2]
                        nc.tensor.matmul(bank[:, i % 2, 0, :], rows[:, q * QT + i, P:], gather1[:, q % 2, i, :],
                                         start=True, stop=True)
                        mm = nc.tensor.matmul(bank[:, i % 2, 1, :], ones[:], gather1[:, q % 2, i, :],
                                              start=True, stop=True)
                    mm.then_inc(summed, 1)

                spread_q(0, 0, True)

                def body(j, first, last):
                    for q in range(QUADS):
                        if q < QUADS - 1:
                            spread_q(j, q + 1, first and q == 0)
                        elif not last:
                            spread_q(j + 1, 0)
                        add_up(j, q, first and q < 2)
                groups_of(pe, groups, body)

            @block.vector
            def _(dve):
                nc.vector.memset(node_sums[:], 0.0).then_inc(cleared, 1)

                def make_spread(j, q, start=False):
                    dve.wait_ge(window_in[q], (j + 1) * (QT + 1) * DMA)
                    if not start:
                        dve.wait_ge(onehot_turned, j * QUADS + q - 1)
                    nc.vector.tensor_scalar(spread[:, q % 2, :], rel_bc[:, q, :], iota_col[:, 0:1], None,
                                            ALU.is_equal).then_inc(spread_made, 1)

                def score(j, q, i):
                    return nc.vector.tensor_tensor_reduce(product[:, i, :], rows[:, q * QT + i, 0:P],
                                                          q_dst[q % 2][:, i, :], float(P) ** -0.5, 0.0,
                                                          ALU.mult, ALU.add, scores[:, q % 2, i:i + 1])

                def add_tile(j, q, i, base, start=False):
                    if not (start and q == 0 and i == 0):
                        dve.wait_ge(added, (j * QUADS + q) * QT + i)
                    span = node_sums[:, :, bass.ds(base, P)]
                    nc.vector.tensor_tensor(span, span, tile_sums[(q % 2) * 2 + i // 2][:, i % 2, :, :],
                                            ALU.add).then_inc(added, 1)

                dve.wait_ge(cleared, 1)
                make_spread(0, 0, True)

                def body(j, first, last):
                    for q in range(QUADS):
                        if q < QUADS - 1:
                            make_spread(j, q + 1, first and q == 0)
                        elif not last:
                            make_spread(j + 1, 0)
                        before = (j, q - 2) if q >= 2 else (j - 1, q + 2)
                        adds = not (first and q < 2)
                        if adds:
                            bases = window_bases(dve, *before)
                            dve.wait_ge(summed, j * QUADS + q - 1)
                        dve.wait_ge(q_spread, j * QUADS + q + 1)
                        dve.wait_ge(gathered[q], (j + 1) * QT * DMA)
                        for i in range(QT):
                            s = score(j, q, i)
                            if i == QT - 1:
                                s.then_inc(scored, 1)
                            if adds:
                                add_tile(*before, i, bases[i], first)
                        dve.wait_ge(scored, j * QUADS + q + 1)
                        nc.vector.tensor_scalar(clipped[:, q % 2, :], scores[:, q % 2, :], 5.0, -5.0, ALU.min,
                                                ALU.max).then_inc(clip_done, 1)
                groups_of(dve, groups, body)
                for q in (QUADS - 2, QUADS - 1):
                    bases = window_bases(dve, groups - 1, q)
                    dve.wait_ge(summed, (groups - 1) * QUADS + q + 1)
                    for i in range(QT):
                        add_tile(groups - 1, q, i, bases[i])
                dve.wait_ge(added, tiles)

    with ExitStack() as ctx:
        sb = lambda name, shape, dt=F32: ctx.enter_context(nc.sbuf_tensor(name, shape, dt))
        ps = lambda name, shape, dt=F32: ctx.enter_context(nc.psum_tensor(name, shape, dt))
        sem = lambda name: ctx.enter_context(nc.semaphore(name))
        w_o = sb("w_o", [P, P])
        w_lr = sb("w_lr", [P, 2 * P])
        b_o = sb("b_o", [1, P])
        b_lr = sb("b_lr", [1, 2 * P])
        gamma = sb("gamma", [P, P])
        beta = sb("beta", [P, P])
        ln1_w = sb("ln1_w", [P, P])
        x_nm = sb("x_nm", [P, 2, QT, P])
        inv = sb("inv", [P, QW])
        mean_rows = sb("mean_rows", [P, 2, QW])
        h = sb("h", [P, QT, P])
        u = sb("u", [P, QT, P])
        stats = sb("stats", [P, 3, QT, 6])
        mv = sb("mv", [P, 3, QT, 2])
        std = sb("std", [P, 3, QT])
        rstd = sb("rstd", [P, 3, QT])
        hT = sb("hT", [P, QT, P])
        xlr = sb("xlr", [P, QT, 2 * P])
        o_ps = ps("o_ps", [P, QT, P])
        t_ps = ps("t_ps", [P, QT, P])
        lr_ps = [ps(f"lr_ps{i}", [P, 2, 2 * P]) for i in range(2)]
        weights_in = sem("l01_weights_in")
        x_in = sem("x_nm_in")
        step = sem("dve_step")
        averaged = sem("averaged")
        projected = sem("projected")
        var_ready = sem("var_ready")
        std_ready = sem("std_ready")
        h_ready = sem("h_ready")
        turned = sem("turned")
        hT_ready = sem("hT_ready")
        lr_ready = sem("lr_ready")
        lr_copied = sem("lr_copied")
        tables_stored = sem("tables_stored")
        x_nm_dram = t["x"].rearrange("(b i p) d -> b p i d", i=QT, p=P)
        xl_dram = xl_tab.rearrange("(b i p) d -> b p i d", i=QT, p=P)
        xr_dram = xr_tab.rearrange("(b i p) d -> b p i d", i=QT, p=P)
        with nc.Block() as block:
            @block.sync
            def _(sp):
                for dst, src in ((w_o[:], t["Wo"]), (w_lr[:, 0:P], t["lin_l_wT"]), (w_lr[:, P:], t["lin_r_wT"]),
                                 (b_o[:], t["bo"]), (b_lr[:, 0:P], t["lin_l_b"]), (b_lr[:, P:], t["lin_r_b"]),
                                 (gamma[:], t["gamma"].to_broadcast([P, P])), (beta[:], t["beta"].to_broadcast([P, P])),
                                 (ln1_w[:], t["ln1_w"].to_broadcast([P, P]))):
                    sp.dma_start(dst, src).then_inc(weights_in, DMA)
                for b in range(node_groups):
                    if b >= 2:
                        sp.wait_ge(var_ready, 3 * (b - 2) + 2)
                    sp.dma_start(x_nm[:, b % 2], x_nm_dram[b]).then_inc(x_in, DMA)
                    sp.wait_ge(x_in, (b + 1) * DMA)

            @block.tensor
            def _(pe):
                pe.wait_ge(weights_in, 9 * DMA)
                for b in range(node_groups):
                    pe.wait_ge(averaged, b + 1)
                    if b:
                        pe.wait_ge(var_ready, 3 * b - 2)
                    for i in range(QT):
                        nc.tensor.matmul(o_ps[:, i, :], mean_rows[:, b % 2, i * P:(i + 1) * P], w_o[:], start=True,
                                         stop=False)
                        mm = nc.tensor.matmul(o_ps[:, i, :], ones[0:1, :], b_o[:], start=False, stop=True)
                    mm.then_inc(projected, 1)
                    pe.wait_ge(h_ready, b + 1)
                    for i in range(QT):
                        mm = nc.tensor.transpose(t_ps[:, i, :], u[:, i, :], ident[:])
                    mm.then_inc(turned, 1)
                    pe.wait_ge(hT_ready, b + 1)
                    if b:
                        pe.wait_ge(lr_copied, b)
                    for i in range(QT):
                        out = lr_ps[i // 2][:, i % 2, :]
                        nc.tensor.matmul(out, hT[:, i, :], w_lr[:], start=True, stop=False)
                        mm = nc.tensor.matmul(out, ones[0:1, :], b_lr[:], start=False, stop=True)
                    mm.then_inc(lr_ready, 1)

            @block.vector
            def _(dve):
                n = [0]

                def link(ins):
                    n[0] += 1
                    ins.then_inc(step, 1)
                    dve.wait_ge(step, n[0])

                def moments(b, k, src):
                    for i in range(QT):
                        ins = nc.vector.bn_stats(stats[:, k, i, :], src[:, i, :])
                    link(ins)
                    for i in range(QT):
                        ins = nc.vector.bn_aggr(mv[:, k, i, :], stats[:, k, i, :])
                    ins.then_inc(var_ready, 1)
                    dve.wait_ge(std_ready, 3 * b + k + 1)
                    link(nc.vector.reciprocal(rstd[:, k, :], std[:, k, :]))

                def scaled(k, out, src):
                    for i in range(QT):
                        ins = nc.vector.tensor_scalar(out[:, i, :], src[:, i, :], mv[:, k, i, 0:1], rstd[:, k, i:i + 1],
                                                      ALU.subtract, ALU.mult)
                    link(ins)

                def rows_of(v):
                    return v[:].unsqueeze(1).to_broadcast([P, QT, P])

                dve.wait_ge(weights_in, 9 * DMA)
                for b in range(node_groups):
                    sl = slice(b * QW, (b + 1) * QW)
                    link(nc.vector.tensor_scalar(inv[:], node_sums[:, 1, sl], TINY, None, ALU.max))
                    link(nc.vector.reciprocal(inv[:], inv[:]))
                    if b >= 2:
                        dve.wait_ge(projected, b - 1)
                    nc.vector.tensor_tensor(mean_rows[:, b % 2, :], node_sums[:, 0, sl], inv[:],
                                            ALU.mult).then_inc(averaged, 1)
                    x = x_nm[:, b % 2]
                    dve.wait_ge(x_in, (b + 1) * DMA)
                    dve.wait_ge(projected, b + 1)
                    link(nc.vector.tensor_tensor(h[:], o_ps[:], x, ALU.add))
                    moments(b, 0, h)
                    if b:
                        dve.wait_ge(turned, b)
                    scaled(0, u, h)
                    link(nc.vector.tensor_tensor(u[:], u[:], rows_of(gamma), ALU.mult))
                    link(nc.vector.tensor_tensor(u[:], u[:], rows_of(beta), ALU.add))
                    link(nc.vector.tensor_tensor(h[:], u[:], x, ALU.add))
                    moments(b, 1, h)
                    scaled(1, x1[:, b], h)
                    moments(b, 2, x1[:, b])
                    scaled(2, u, x1[:, b])
                    nc.vector.tensor_tensor(u[:], u[:], rows_of(ln1_w), ALU.mult).then_inc(h_ready, 1)

            @block.scalar
            def _(act):
                for b in range(node_groups):
                    for k in range(3):
                        act.wait_ge(var_ready, 3 * b + k + 1)
                        nc.scalar.activation(std[:, k, :], mv[:, k, :, 1], ACT.Sqrt,
                                             bias=eps_col[:, 0:1]).then_inc(std_ready, 1)
                    act.wait_ge(turned, b + 1)
                    nc.scalar.copy(hT[:], t_ps[:]).then_inc(hT_ready, 1)
                    act.wait_ge(lr_ready, b + 1)
                    if b:
                        act.wait_ge(tables_stored, 2 * b * DMA)
                    nc.scalar.copy(xlr[:, 0:2, :], lr_ps[0][:])
                    nc.scalar.copy(xlr[:, 2:4, :], lr_ps[1][:]).then_inc(lr_copied, 1)
                    act.wait_ge(lr_copied, b + 1)
                    act.dma_start(xl_dram[b], xlr[:, :, 0:P]).then_inc(tables_stored, DMA)
                    act.dma_start(xr_dram[b], xlr[:, :, P:]).then_inc(tables_stored, DMA)
                act.wait_ge(tables_stored, 2 * node_groups * DMA)
    sums.close()

    attention = ExitStack()
    logits = attention.enter_context(nc.sbuf_tensor("logits", [P, CW], F32))
    with ExitStack() as ctx:
        sb = lambda name, shape, dt=F32: ctx.enter_context(nc.sbuf_tensor(name, shape, dt))
        ps = lambda name, shape, dt=F32: ctx.enter_context(nc.psum_tensor(name, shape, dt))
        sem = lambda name: ctx.enter_context(nc.semaphore(name))
        w_e = sb("w_e", [P, P])
        att_pad = sb("att_pad", [P, CHUNKS, CHUNKS, HEADS])
        src_ring = sb("src_ring1", [P, CHUNKS], I32)
        rows = sb("rows1", [P, CHUNKS, P])
        window = sb("window1", [P, CHUNKS, P])
        attr = sb("attr", [P, QUADS, QW])
        rel_bc = sb("rel_bc1", [P, QUADS, QW], BF16)
        spread = sb("spread1", [P, 2, QW])
        z_low = sb("z_low", [P, 2, QW])
        z_act = sb("z_act", [P, 2, QW])
        z_ps = [ps(f"z_ps{i}", [P, QW]) for i in range(2)]
        lg_ps = ps("lg_ps", [P, P])
        weights_in = sem("l1_weights_in")
        pad_cleared = sem("pad_cleared")
        att_in = sem("att_in")
        quads_asked = sem("quads_asked1")
        src_ready = [sem(f"src_ready1_{i}") for i in range(2)]
        gathered = [sem(f"gathered1_{q}") for q in range(QUADS)]
        window_in = [sem(f"window_in1_{q}") for q in range(QUADS)]
        attr_in = [sem(f"attr_in{q}") for q in range(QUADS)]
        kept = [sem(f"xl_kept{q}") for q in range(QUADS)]
        spread_made = sem("spread_made1")
        z_ready = sem("z_ready")
        low_ready = sem("low_ready")
        z_act_ready = sem("z_act_ready")
        lg_ready = sem("lg_ready")
        lg_quads = sem("lg_quads")
        lg_copied = sem("lg_copied")
        with nc.Block() as block:
            @block.sync
            def _(sp):
                sp.dma_start(w_e[:], t["lin_edge_wT"]).then_inc(weights_in, DMA)
                sp.wait_ge(pad_cleared, 1)
                for hd in range(HEADS):
                    diag = bass.AP(att_pad[:].tensor, att_pad[hd * HC:(hd + 1) * HC, 0, 0, hd:hd + 1].offset,
                                   [list(att_pad[hd * HC:(hd + 1) * HC].ap[0]), [CHUNKS * HEADS + HEADS, CHUNKS], [1, 1]])
                    sp.dma_start(diag, t["att"][hd].rearrange("(c o) -> c o", o=1).unsqueeze(2).to_broadcast([HC, CHUNKS, 1]),
                                 allow_slow_non_contiguous=True).then_inc(att_in, DMA)

                def body(j, first, last):
                    for q in range(QUADS):
                        if not first:
                            sp.wait_ge(z_ready, j * QUADS + q - QUADS + 1)
                        sp.dma_start(rel_bc[:, q, :], rel_rows[bass.ds(j * QUADS + q, 1), :].to_broadcast([P, QW])
                                     ).then_inc(window_in[q], DMA)
                        for i, base in enumerate(window_bases(sp, j, q), q * QT):
                            sp.dma_start(window[:, i, :], xr_tab[bass.ds(base, P), :]).then_inc(window_in[q], DMA)
                groups_of(sp, groups, body)

            @block.gpsimd
            def _(pool):
                def body(j, first, last):
                    for q in range(QUADS):
                        if q % 2 == 0:
                            pool.wait_ge(src_ready[q // 2], j + 1)
                        if not first:
                            pool.wait_ge(z_ready, j * QUADS + q - QUADS + 1)
                            pool.wait_ge(kept[q], j * DMA)
                        pool.sem_inc(quads_asked, 1)
                        for i in range(q * QT, q * QT + QT):
                            nc.gpsimd.indirect_dma_start(
                                out=rows[:, i, :], out_offset=None, in_=xl_tab,
                                in_offset=bass.IndirectOffsetOnAxis(ap=src_ring[:, i:i + 1], axis=0),
                            ).then_inc(gathered[q], DMA)
                groups_of(pool, groups, body)

            @block.scalar
            def _(act):
                def refill(j, half):
                    a = half * CHUNKS // 2
                    nc.scalar.copy(src_ring[:, a:a + CHUNKS // 2],
                                   src_cols[:, bass.ds(j * CHUNKS + a, CHUNKS // 2)]).then_inc(src_ready[half], 1)

                def load_attr(j, q):
                    act.dma_start(attr[:, q, :], t["attrT"][bass.ds(j, 1), :, q * QW:(q + 1) * QW].rearrange("a p e -> (a p) e")
                                  ).then_inc(attr_in[q], DMA)

                refill(0, 0)
                refill(0, 1)
                for q in range(QUADS):
                    load_attr(0, q)

                def body(j, first, last):
                    for q in range(QUADS):
                        act.wait_ge(z_ready, j * QUADS + q + 1)
                        if not (first and q < 2):
                            act.wait_ge(z_act_ready, j * QUADS + q - 1)
                        nc.scalar.mul(z_low[:, q % 2, :], z_ps[q % 2][:], 0.2).then_inc(low_ready, 1)
                        act.wait_ge(gathered[q], (j + 1) * QT * DMA)
                        act.dma_start(xl_edges[bass.ds(j, 1), :, q * QW:(q + 1) * QW].rearrange("a p e -> (a p) e"),
                                      rows[:, q * QT:(q + 1) * QT, :].rearrange("p i d -> p (i d)")).then_inc(kept[q], DMA)
                        if not last:
                            load_attr(j + 1, q)
                            if q == 1:
                                refill(j + 1, 0)
                            if q == 3:
                                refill(j + 1, 1)
                groups_of(act, groups, body)
                for q in range(QUADS):
                    act.wait_ge(kept[q], groups * DMA)

            @block.tensor
            def _(pe):
                def make_z(j, q, start=False):
                    pe.wait_ge(attr_in[q], (j + 1) * DMA)
                    if not start:
                        pe.wait_ge(z_act_ready, j * QUADS + q - 1)
                        pe.wait_ge(low_ready, j * QUADS + q - 1)
                    z = z_ps[q % 2]
                    nc.tensor.matmul(z[:], w_e[:], attr[:, q, :], start=True, stop=False)
                    pe.wait_ge(spread_made, j * QUADS + q + 1)
                    pe.wait_ge(window_in[q], (j + 1) * (QT + 1) * DMA)
                    for i in range(QT):
                        nc.tensor.matmul(z[:, i * P:(i + 1) * P], window[:, q * QT + i, :],
                                         spread[:, q % 2, i * P:(i + 1) * P], start=False, stop=False)
                    pe.wait_ge(gathered[q], (j + 1) * QT * DMA)
                    for i in range(QT):
                        mm = nc.tensor.matmul(z[:, i * P:(i + 1) * P], rows[:, q * QT + i, :], ident[:],
                                              start=False, stop=(i == QT - 1))
                    mm.then_inc(z_ready, 1)

                def make_logits(j, q, first):
                    pe.wait_ge(z_act_ready, j * QUADS + q + 1)
                    if q == 0 and not first:
                        pe.wait_ge(lg_copied, j)
                    for i in range(QT):
                        c = q * QT + i
                        mm = nc.tensor.matmul(lg_ps[:], att_pad[:, c].rearrange("p a b -> p (a b)"),
                                              z_act[:, q % 2, i * P:(i + 1) * P], start=(c == 0),
                                              stop=(c == CHUNKS - 1))
                    mm.then_inc(lg_quads, 1)

                pe.wait_ge(weights_in, DMA)
                pe.wait_ge(att_in, HEADS * DMA)
                make_z(0, 0, True)

                def body(j, first, last):
                    for q in range(QUADS):
                        if q < QUADS - 1:
                            make_z(j, q + 1, first and q == 0)
                        elif not last:
                            make_z(j + 1, 0)
                        make_logits(j, q, first)
                groups_of(pe, groups, body)

            @block.vector
            def _(dve):
                nc.vector.memset(att_pad[:], 0.0).then_inc(pad_cleared, 1)

                def make_spread(j, q, start=False):
                    dve.wait_ge(window_in[q], (j + 1) * (QT + 1) * DMA)
                    if not start:
                        dve.wait_ge(z_ready, j * QUADS + q - 1)
                    nc.vector.tensor_scalar(spread[:, q % 2, :], rel_bc[:, q, :], iota_col[:, 0:1], None,
                                            ALU.is_equal).then_inc(spread_made, 1)

                make_spread(0, 0, True)

                def body(j, first, last):
                    for q in range(QUADS):
                        if q < QUADS - 1:
                            make_spread(j, q + 1, first and q == 0)
                        elif not last:
                            make_spread(j + 1, 0)
                        dve.wait_ge(low_ready, j * QUADS + q + 1)
                        if not (first and q < 2):
                            dve.wait_ge(lg_quads, j * QUADS + q - 1)
                        nc.vector.tensor_tensor(z_act[:, q % 2, :], z_ps[q % 2][:], z_low[:, q % 2, :],
                                                ALU.max).then_inc(z_act_ready, 1)
                    dve.wait_ge(lg_quads, j * QUADS + QUADS)
                    nc.vector.tensor_copy(logits[:, bass.ds(j * P, P)], lg_ps[:]).then_inc(lg_copied, 1)
                groups_of(dve, groups, body)

    with ExitStack() as ctx:
        sb = lambda name, shape, dt=F32: ctx.enter_context(nc.sbuf_tensor(name, shape, dt))
        sem = lambda name: ctx.enter_context(nc.semaphore(name))
        dst = sb("dst_chunks", [P, CW], I32)
        other = sb("beside", [P, CW])
        fence = sb("fence", [P, CW])
        forward = sb("forward", [P, CW])
        ends = sb("ends", [P, 2, 2])
        turned = sb("turned", [HEADS, 3, CHUNKS])
        enter = sb("enter", [P, 1])
        dst_in = sem("dst_in")
        step = sem("scan_step")
        ends_ready = sem("ends_ready")
        turn_out = sem("turn_out")
        turn_in = sem("turn_in")
        carried = sem("carried")
        enter_out = sem("enter_out")
        enter_in = sem("enter_in")
        nat = t["dst_nat"]

        def chunked(off):
            return bass.AP(nat.tensor, off, [[CW, CHUNKS], [0, HEADS], [1, CW]])

        with nc.Block() as block:
            @block.sync
            def _(sp):
                sp.dma_start(dst[:], chunked(1)).then_inc(dst_in, DMA)
                sp.dma_start(other[:].bitcast(I32), chunked(0)).then_inc(dst_in, DMA)
                for k in range(2):
                    sp.wait_ge(ends_ready, k + 1)
                    for m in range(2):
                        sp.dma_start(turn_dram[3 * k + m].rearrange("c h -> (c h)").rearrange("(p o) -> p o", o=1),
                                     ends[:, k, m:m + 1], allow_slow_non_contiguous=True).then_inc(turn_out, DMA)
                    sp.wait_ge(turn_out, (k + 1) * 2 * DMA)
                    for m in range(2):
                        sp.dma_start(turned[:, m, :], turn_dram[3 * k + m].rearrange("c h -> h c"),
                                     allow_slow_non_contiguous=True).then_inc(turn_in, DMA)
                    sp.wait_ge(carried, k + 1)
                    sp.dma_start(turn_dram[3 * k + 2].rearrange("c h -> h c"), turned[:, 2, :],
                                 allow_slow_non_contiguous=True).then_inc(enter_out, DMA)
                    sp.wait_ge(enter_out, (k + 1) * DMA)
                    sp.dma_start(enter[:], turn_dram[3 * k + 2].rearrange("c h -> (c h)").rearrange("(p o) -> p o", o=1)
                                 , allow_slow_non_contiguous=True).then_inc(enter_in, DMA)
                    if k == 0:
                        sp.dma_start(other[:].bitcast(I32), chunked(2)).then_inc(dst_in, DMA)

            @block.vector
            def _(dve):
                n = [0]

                def link(ins):
                    n[0] += 1
                    ins.then_inc(step, 1)
                    dve.wait_ge(step, n[0])

                for k in range(2):
                    way = slice(None, None, -1 if k else 1)
                    src = forward if k else logits
                    out = other if k else forward
                    exit_at = 0 if k else CW - 1
                    dve.wait_ge(dst_in, (2 + k) * DMA)
                    link(nc.vector.tensor_tensor(fence[:], dst[:], other[:].bitcast(I32), ALU.not_equal))
                    link(nc.vector.tensor_scalar(fence[:], fence[:], -BIG, None, ALU.mult))
                    link(nc.vector.tensor_tensor_scan(out[:, way], fence[:, way], src[:, way], -BIG, ALU.add, ALU.max))
                    nc.vector.tensor_copy(ends[:, k, 0:1], out[:, exit_at:exit_at + 1])
                    nc.vector.tensor_reduce(ends[:, k, 1:2], fence[:], AX.X, ALU.min).then_inc(ends_ready, 1)
                    link(nc.vector.memset(turned[:, 2, :], -BIG))
                    dve.wait_ge(turn_in, (k + 1) * 2 * DMA)
                    to, of = ((slice(CHUNKS - 2, None, -1), slice(CHUNKS - 1, 0, -1)) if k
                              else (slice(1, None), slice(0, CHUNKS - 1)))
                    nc.vector.tensor_tensor_scan(turned[:, 2, to], turned[:, 1, of], turned[:, 0, of], -BIG,
                                                 ALU.add, ALU.max).then_inc(carried, 1)
                    dve.wait_ge(enter_in, (k + 1) * DMA)
                    link(nc.vector.tensor_tensor_scan(out[:, way], fence[:, way], src[:, way], enter[:, 0:1],
                                                      ALU.add, ALU.max))
                link(nc.vector.tensor_tensor(logits[:], logits[:], other[:], ALU.subtract))

    alpha = ExitStack()
    num = alpha.enter_context(nc.sbuf_tensor("num", [P, groups, P], F32))
    with ExitStack() as ctx:
        sb = lambda name, shape, dt=F32: ctx.enter_context(nc.sbuf_tensor(name, shape, dt))
        ps = lambda name, shape, dt=F32: ctx.enter_context(nc.psum_tensor(name, shape, dt))
        sem = lambda name: ctx.enter_context(nc.semaphore(name))
        shifted = sb("shifted", [P, 2, QW])
        n_ps = [ps(f"n_ps{i}", [P, QT, P]) for i in range(2)]
        turned = sem("num_turned")
        powered = sem("powered")
        copied = sem("num_copied")
        quads = groups // QT
        with nc.Block() as block:
            @block.scalar
            def _(act):
                for g in range(quads):
                    if g >= 2:
                        act.wait_ge(turned, g - 1)
                    nc.scalar.activation(shifted[:, g % 2, :], logits[:, g * QW:(g + 1) * QW], ACT.Exp).then_inc(powered, 1)

            @block.tensor
            def _(pe):
                for g in range(quads):
                    pe.wait_ge(powered, g + 1)
                    if g >= 2:
                        pe.wait_ge(copied, g - 1)
                    for i in range(QT):
                        mm = nc.tensor.transpose(n_ps[g % 2][:, i, :], shifted[:, g % 2, i * P:(i + 1) * P], ident[:])
                    mm.then_inc(turned, 1)

            @block.vector
            def _(dve):
                for g in range(quads):
                    dve.wait_ge(turned, g + 1)
                    nc.vector.tensor_copy(num[:, g * QT:(g + 1) * QT, :], n_ps[g % 2][:]).then_inc(copied, 1)

    node_sums = alpha.enter_context(nc.sbuf_tensor("node_sums1", [P, 2, NP], F32))
    with ExitStack() as ctx:
        sb = lambda name, shape, dt=F32: ctx.enter_context(nc.sbuf_tensor(name, shape, dt))
        ps = lambda name, shape, dt=F32: ctx.enter_context(nc.psum_tensor(name, shape, dt))
        sem = lambda name: ctx.enter_context(nc.semaphore(name))
        rows = sb("rows2", [P, QUADS, QW])
        message = sb("message", [P, QUADS, QW])
        numq = sb("numq", [P, QUADS, QW])
        onehot = sb("onehot", [P, 2, QT, P])
        tile_sums = [ps(f"tile_sums1_{i}", [P, 2, 2, P]) for i in range(4)]
        rows_in = [sem(f"rows_in{q}") for q in range(QUADS)]
        numq_made = sem("numq_made")
        message_made = sem("message_made")
        onehot_made = sem("onehot_made1")
        summed = sem("summed1")
        added = sem("added1")
        cleared = sem("cleared1")
        with nc.Block() as block:
            @block.sync
            def _(sp):
                def body(j, first, last):
                    for q in range(QUADS):
                        if not first:
                            sp.wait_ge(message_made, j * QUADS + q - QUADS + 1)
                        sp.dma_start(rows[:, q, :], xl_edges[bass.ds(j, 1), :, q * QW:(q + 1) * QW].rearrange("a p e -> (a p) e")
                                     ).then_inc(rows_in[q], DMA)
                groups_of(sp, groups, body)

            @block.scalar
            def _(act):
                def body(j, first, last):
                    for q in range(QUADS):
                        if not first:
                            act.wait_ge(summed, j * QUADS + q - QUADS + 1)
                        src = num[:, bass.ds(j, 1), q * QT * HEADS:(q + 1) * QT * HEADS].rearrange("p a b -> p (a b)")
                        nc.scalar.copy(numq[:, q, :].rearrange("p (a b) -> p a b", b=HC),
                                       src.unsqueeze(2).to_broadcast([P, QT * HEADS, HC])).then_inc(numq_made, 1)
                groups_of(act, groups, body)

            @block.gpsimd
            def _(pool):
                def body(j, first, last):
                    for q in range(QUADS):
                        pool.wait_ge(rows_in[q], (j + 1) * DMA)
                        pool.wait_ge(numq_made, j * QUADS + q + 1)
                        if not first:
                            pool.wait_ge(summed, j * QUADS + q - QUADS + 1)
                        nc.gpsimd.tensor_tensor(message[:, q, :], rows[:, q, :], numq[:, q, :],
                                                ALU.mult).then_inc(message_made, 1)
                groups_of(pool, groups, body)

            @block.tensor
            def _(pe):
                def body(j, first, last):
                    for q in range(QUADS):
                        pe.wait_ge(onehot_made, j * QUADS + q + 1)
                        pe.wait_ge(message_made, j * QUADS + q + 1)
                        if not (first and q < 2):
                            pe.wait_ge(added, (j * QUADS + q - 1) * QT)
                        for i in range(QT):
                            bank = tile_sums[(q % 2) * 2 + i // 2]
                            nc.tensor.matmul(bank[:, i % 2, 0, :], message[:, q, i * P:(i + 1) * P],
                                             onehot[:, q % 2, i, :], start=True, stop=True)
                            mm = nc.tensor.matmul(bank[:, i % 2, 1, :], numq[:, q, i * P:(i + 1) * P],
                                                  onehot[:, q % 2, i, :], start=True, stop=True)
                        mm.then_inc(summed, 1)
                groups_of(pe, groups, body)

            @block.vector
            def _(dve):
                nc.vector.memset(node_sums[:], 0.0).then_inc(cleared, 1)
                dve.wait_ge(cleared, 1)

                def add_tile(j, q, i, base, start=False):
                    if not (start and q == 0 and i == 0):
                        dve.wait_ge(added, (j * QUADS + q) * QT + i)
                    span = node_sums[:, :, bass.ds(base, P)]
                    nc.vector.tensor_tensor(span, span, tile_sums[(q % 2) * 2 + i // 2][:, i % 2, :, :],
                                            ALU.add).then_inc(added, 1)

                def body(j, first, last):
                    for q in range(QUADS):
                        before = (j, q - 2) if q >= 2 else (j - 1, q + 2)
                        adds = not (first and q < 2)
                        if adds:
                            bases = window_bases(dve, *before)
                            dve.wait_ge(summed, j * QUADS + q - 1)
                        for i in range(QT):
                            o = nc.vector.tensor_scalar(onehot[:, q % 2, i, :], iota_row[:],
                                                        rel_cols[:, bass.ds(j * CHUNKS + q * QT + i, 1)], None,
                                                        ALU.is_equal)
                            if i == QT - 1:
                                o.then_inc(onehot_made, 1)
                            if adds:
                                add_tile(*before, i, bases[i], first)
                groups_of(dve, groups, body)
                for q in (QUADS - 2, QUADS - 1):
                    bases = window_bases(dve, groups - 1, q)
                    dve.wait_ge(summed, (groups - 1) * QUADS + q + 1)
                    for i in range(QT):
                        add_tile(groups - 1, q, i, bases[i])
                dve.wait_ge(added, tiles)

    FC = 4
    with ExitStack() as ctx:
        sb = lambda name, shape, dt=F32: ctx.enter_context(nc.sbuf_tensor(name, shape, dt))
        ps = lambda name, shape, dt=F32: ctx.enter_context(nc.psum_tensor(name, shape, dt))
        sem = lambda name: ctx.enter_context(nc.semaphore(name))
        fc = sb("fc", [P, FC * P])
        proj = sb("proj", [P, FC, P])
        a_bias = sb("a_bias", [P, P])
        ln2_w = sb("ln2_w", [P, P])
        inv = sb("inv1", [P, QW])
        mean_rows = sb("mean_rows1", [P, QW])
        x2 = sb("x2", [P, QT, P])
        u = sb("u1", [P, QT, P])
        result = sb("result", [P, 2, QT, P])
        stats = sb("stats1", [P, 2, QT, 6])
        mv = sb("mv1", [P, 2, QT, 2])
        std = sb("std1", [P, 2, QT])
        rstd = sb("rstd1", [P, 2, QT])
        hT = sb("hT1", [P, QW])
        hidden = sb("hidden", [P, FC, QW])
        a_ps = ps("a_ps", [P, QT, P])
        t_ps = ps("t_ps1", [P, QW])
        f_ps = [ps(f"f_ps{i}", [P, QW]) for i in range(FC)]
        y_ps = ps("y_ps", [P, QT, P])
        weights_in = sem("mlp_weights_in")
        step = sem("dve_step1")
        averaged = sem("averaged1")
        row_major = sem("row_major")
        var_ready = sem("var_ready1")
        std_ready = sem("std_ready1")
        h_ready = sem("h_ready1")
        turned = sem("turned1")
        hT_ready = sem("hT_ready1")
        fc_ready = sem("fc_ready")
        relu_ready = sem("relu_ready")
        y_ready = sem("y_ready")
        result_ready = sem("result_ready")
        out_stored = [sem(f"out_stored{i}") for i in range(2)]
        out_dram = t["out"].rearrange("(b i p) d -> b p i d", i=QT, p=P)
        with nc.Block() as block:
            @block.sync
            def _(sp):
                sp.dma_start(fc[:], t["fc_wT"]).then_inc(weights_in, DMA)
                sp.dma_start(proj[:], t["proj_wT"].rearrange("(k p) d -> p k d", p=P)).then_inc(weights_in, DMA)
                sp.dma_start(a_bias[:], t["attn_bias"].to_broadcast([P, P])).then_inc(weights_in, DMA)
                sp.dma_start(ln2_w[:], t["ln2_w"].to_broadcast([P, P])).then_inc(weights_in, DMA)
                for b in range(node_groups):
                    sp.wait_ge(result_ready, b + 1)
                    sp.dma_start(out_dram[b], result[:, b % 2]).then_inc(out_stored[b % 2], DMA)
                for i in range(2):
                    sp.wait_ge(out_stored[i], (node_groups + 1 - i) // 2 * DMA)

            @block.tensor
            def _(pe):
                pe.wait_ge(weights_in, 4 * DMA)
                for b in range(node_groups):
                    pe.wait_ge(averaged, b + 1)
                    for i in range(QT):
                        mm = nc.tensor.transpose(a_ps[:, i, :], mean_rows[:, i * P:(i + 1) * P], ident[:])
                    mm.then_inc(row_major, 1)
                    pe.wait_ge(h_ready, b + 1)
                    for i in range(QT):
                        mm = nc.tensor.transpose(t_ps[:, i * P:(i + 1) * P], u[:, i, :], ident[:])
                    mm.then_inc(turned, 1)
                    pe.wait_ge(hT_ready, b + 1)
                    for k in range(FC):
                        nc.tensor.matmul(f_ps[k][:], fc[:, k * P:(k + 1) * P], hT[:], start=True,
                                         stop=True).then_inc(fc_ready, 1)
                    pe.wait_ge(relu_ready, FC * (b + 1))
                    for i in range(QT):
                        for k in range(FC):
                            mm = nc.tensor.matmul(y_ps[:, i, :], hidden[:, k, i * P:(i + 1) * P], proj[:, k, :],
                                                  start=(k == 0), stop=(k == FC - 1))
                    mm.then_inc(y_ready, 1)

            @block.scalar
            def _(act):
                for b in range(node_groups):
                    act.wait_ge(var_ready, 2 * b + 1)
                    nc.scalar.activation(std[:, 0, :], mv[:, 0, :, 1], ACT.Sqrt, bias=eps_col[:, 0:1]).then_inc(std_ready, 1)
                    act.wait_ge(turned, b + 1)
                    nc.scalar.copy(hT[:], t_ps[:]).then_inc(hT_ready, 1)
                    for k in range(FC):
                        act.wait_ge(fc_ready, FC * b + k + 1)
                        nc.scalar.activation(hidden[:, k, :], f_ps[k][:], ACT.Relu).then_inc(relu_ready, 1)
                    act.wait_ge(var_ready, 2 * b + 2)
                    nc.scalar.activation(std[:, 1, :], mv[:, 1, :, 1], ACT.Sqrt, bias=eps_col[:, 0:1]).then_inc(std_ready, 1)

            @block.vector
            def _(dve):
                n = [0]

                def link(ins):
                    n[0] += 1
                    ins.then_inc(step, 1)
                    dve.wait_ge(step, n[0])

                def moments(b, k, src):
                    for i in range(QT):
                        ins = nc.vector.bn_stats(stats[:, k, i, :], src[:, i, :])
                    link(ins)
                    for i in range(QT):
                        ins = nc.vector.bn_aggr(mv[:, k, i, :], stats[:, k, i, :])
                    ins.then_inc(var_ready, 1)
                    dve.wait_ge(std_ready, 2 * b + k + 1)
                    link(nc.vector.reciprocal(rstd[:, k, :], std[:, k, :]))

                def scaled(k, out, src):
                    for i in range(QT):
                        ins = nc.vector.tensor_scalar(out[:, i, :], src[:, i, :], mv[:, k, i, 0:1], rstd[:, k, i:i + 1],
                                                      ALU.subtract, ALU.mult)
                    return ins

                def rows_of(v):
                    return v[:].unsqueeze(1).to_broadcast([P, QT, P])

                dve.wait_ge(weights_in, 4 * DMA)
                for b in range(node_groups):
                    sl = slice(b * QW, (b + 1) * QW)
                    link(nc.vector.tensor_scalar(inv[:], node_sums[:, 1, sl], TINY, None, ALU.max))
                    link(nc.vector.reciprocal(inv[:], inv[:]))
                    nc.vector.tensor_tensor(mean_rows[:], node_sums[:, 0, sl], inv[:], ALU.mult).then_inc(averaged, 1)
                    dve.wait_ge(row_major, b + 1)
                    link(nc.vector.tensor_tensor(u[:], a_ps[:], rows_of(a_bias), ALU.add))
                    link(nc.vector.tensor_tensor(x2[:], u[:], x1[:, b], ALU.add))
                    moments(b, 0, x2)
                    link(scaled(0, u, x2))
                    nc.vector.tensor_tensor(u[:], u[:], rows_of(ln2_w), ALU.mult).then_inc(h_ready, 1)
                    dve.wait_ge(y_ready, b + 1)
                    link(nc.vector.tensor_tensor(x2[:], y_ps[:], x2[:], ALU.add))
                    link(nc.vector.tensor_tensor(x2[:], x2[:], x1[:, b], ALU.add))
                    moments(b, 1, x2)
                    if b >= 2:
                        dve.wait_ge(out_stored[b % 2], b // 2 * DMA)
                    scaled(1, result[:, b % 2], x2).then_inc(result_ready, 1)
    alpha.close()
    attention.close()
    persistent.close()


def kernel(x, src, dst, edge_attr_128, **w):
    import numpy as np
    import concourse.bacc as bacc
    from concourse.bass_utils import run_bass_kernel_spmd

    x, src, dst, attr = (np.asarray(a) for a in (x, src, dst, edge_attr_128))
    w = {k: np.asarray(v) for k, v in w.items()}
    N, D = x.shape
    E = src.shape[0]
    groups, node_groups = sizes(N, E)
    EP, NP, tiles = groups * CHUNKS * P, node_groups * QW, groups * CHUNKS

    def edges(a, fill):
        full = np.full((EP,) + a.shape[1:], fill, a.dtype)
        full[:E] = a
        return full.reshape((CHUNKS, groups, P) + a.shape[1:])

    def row(a):
        return np.ascontiguousarray(a.reshape(1, -1))

    def turned(a):
        return np.ascontiguousarray(a.T)

    srcs, dsts = edges(src, 0), edges(dst, N)
    xp = np.zeros((NP, D), x.dtype)
    xp[:N] = x
    beside = np.full((EP + 2,), -1, dst.dtype)
    beside[1:-1] = dsts.reshape(-1)
    arrays = {
        "x": xp,
        "xT": turned(xp),
        "src_cols": np.ascontiguousarray(srcs.transpose(2, 1, 0)).reshape(P, tiles),
        "dst_cols": np.ascontiguousarray(dsts.transpose(2, 1, 0)).reshape(P, tiles),
        "dst_rows": np.ascontiguousarray(dsts.transpose(1, 0, 2)).reshape(tiles, P),
        "first_dst": np.ascontiguousarray(dsts[:, :, 0].T).reshape(1, tiles),
        "dst_nat": beside,
        "attrT": np.ascontiguousarray(edges(attr, 0).transpose(1, 3, 0, 2)).reshape(groups, D, CHUNKS * P),
        "Wqk": w["L0_gnn_Wqk"], "Wv": w["L0_gnn_Wv"], "Wo": w["L0_gnn_Wo"],
        "bqk": row(w["L0_gnn_bqk"]), "bv": row(w["L0_gnn_bv"]), "bo": row(w["L0_gnn_bo"]),
        "gamma": row(w["L0_gnn_gamma"]), "beta": row(w["L0_gnn_beta"]),
        "ln1_w": row(w["L1_gnn_ln1_w"]), "ln2_w": row(w["L1_gnn_ln2_w"]),
        "lin_l_wT": turned(w["L1_gnn_lin_l_w"]), "lin_r_wT": turned(w["L1_gnn_lin_r_w"]),
        "lin_l_b": row(w["L1_gnn_lin_l_b"]), "lin_r_b": row(w["L1_gnn_lin_r_b"]),
        "lin_edge_wT": turned(w["L1_gnn_lin_edge_w"]), "att": w["L1_gnn_att"],
        "attn_bias": row(w["L1_gnn_attn_bias"]),
        "fc_wT": turned(w["L1_gnn_fc_w"]), "proj_wT": turned(w["L1_gnn_proj_w"]),
    }
    nc = bacc.Bacc("TRN2", target_bir_lowering=False, num_devices=1)
    t = {k: nc.dram_tensor("in_" + k, a.shape, mybir.dt.from_np(a.dtype), kind="ExternalInput").ap()
         for k, a in arrays.items()}
    t["out"] = nc.dram_tensor("out_nodes", (NP, D), F32, kind="ExternalOutput").ap()
    build(nc, t, N, E)
    r = run_bass_kernel_spmd(nc, [{"in_" + k: a for k, a in arrays.items()}], core_ids=[0])
    return r.results[0]["out_nodes"][:N]
```

```python
from contextlib import ExitStack

import concourse.bass as bass
from concourse import mybir

F32 = mybir.dt.float32
BF16 = mybir.dt.bfloat16
I32 = mybir.dt.int32
ALU = mybir.AluOpType
ACT = mybir.ActivationFunctionType
AX = mybir.AxisListType

P = 128
HEADS = 8
HC = P // HEADS
CHUNKS = 16
QT = 4
QUADS = CHUNKS // QT
QW = QT * P
BIG = 1.0e38
TINY = 1.0e-30
EPS = 1e-5
DMA = 16


def sizes(nodes, edges):
    groups = -(-edges // (CHUNKS * P))
    node_groups = -(-(nodes + P) // QW)
    return groups, node_groups


def build(nc, t, N, E):
    groups, node_groups = sizes(N, E)
    tiles = groups * CHUNKS
    NP = node_groups * QW
    CW = groups * P

    qkv_tab = nc.dram_tensor("qkv_tab", (NP, 2 * P), F32).ap()
    xl_tab = nc.dram_tensor("xl_tab", (NP, P), F32).ap()
    xr_tab = nc.dram_tensor("xr_tab", (NP, P), F32).ap()
    rel_rows = nc.dram_tensor("rel_rows", (tiles // QT, QW), BF16).ap()
    rel_rows_out = rel_rows.rearrange("q e -> (q e)").rearrange("(p w) -> p w", w=8 * P)
    xl_edges = nc.dram_tensor("xl_edges", (groups, P, CHUNKS * P), F32).ap()
    onehot_edges = nc.dram_tensor("onehot_edges", (groups, P, CHUNKS * P), BF16).ap()
    ends_dram = nc.dram_tensor("ends_dram", (CHUNKS * HEADS, 2), F32).ap()
    enter_dram = nc.dram_tensor("enter_dram", (CHUNKS * HEADS, 2), F32).ap()

    persistent = ExitStack()

    def keep(name, shape, dt=F32):
        return persistent.enter_context(nc.sbuf_tensor(name, shape, dt))

    iota_row = keep("iota_row", [P, P])
    iota_col = keep("iota_col", [P, 1])
    ident = keep("ident", [P, P])
    ones = keep("ones", [P, P])
    eps_col = keep("eps_col", [P, 1])
    rel_cols = keep("rel_cols", [P, tiles])
    first_row = keep("first_row", [1, tiles], I32)
    src_cols = keep("src_cols", [P, tiles], I32)
    x1 = keep("x1", [P, node_groups, QT, P])

    def window_bases(eng, j, q):
        return nc.values_load_multi_w_load_instructions(
            first_row[0:1, bass.ds(j * CHUNKS + q * QT, QT)], engines=(eng.engine,), min_val=0, max_val=N,
            skip_runtime_bounds_check_because="destinations are node numbers, or N in the padding")[1]

    def groups_of(eng, total, body):
        body(0, True, False)
        with eng.Fori(1, total - 1) as j:
            body(j, False, False)
        body(total - 1, False, True)

    with ExitStack() as ctx:
        sb = lambda name, shape, dt=F32: ctx.enter_context(nc.sbuf_tensor(name, shape, dt))
        sem = lambda name: ctx.enter_context(nc.semaphore(name))
        iota_i = sb("iota_i", [P, P], I32)
        iota_ci = sb("iota_ci", [P, 1], I32)
        dst_cols = sb("dst_cols", [P, tiles], I32)
        first_all = sb("first_all", [P, tiles], I32)
        dst_rows = sb("dst_rows", [tiles // 8, 8, P], I32)
        rel_out = sb("rel_out", [tiles // 8, 8, P], BF16)
        loaded = sem("indices_loaded")
        iota_made = sem("iota_made")
        const_made = sem("const_made")
        rel_made = sem("rel_made")
        rel_stored = sem("rel_stored")
        with nc.Block() as block:
            @block.sync
            def _(sp):
                sp.dma_start(dst_rows[:], t["dst_rows"].rearrange("(p k) e -> p k e", k=8)).then_inc(loaded, DMA)
                sp.dma_start(dst_cols[:], t["dst_cols"]).then_inc(loaded, DMA)
                sp.dma_start(first_all[:], t["first_dst"].to_broadcast([P, tiles])).then_inc(loaded, DMA)
                sp.dma_start(first_row[:], t["first_dst"]).then_inc(loaded, DMA)
                sp.dma_start(src_cols[:], t["src_cols"]).then_inc(loaded, DMA)
                sp.wait_ge(rel_made, 1)
                sp.dma_start(rel_rows_out, rel_out[:].rearrange("p k e -> p (k e)")).then_inc(rel_stored, DMA)
                sp.wait_ge(rel_stored, DMA)
                sp.wait_ge(loaded, 5 * DMA)

            @block.gpsimd
            def _(pool):
                nc.gpsimd.iota(iota_i[:], [[1, P]], base=0, channel_multiplier=0)
                nc.gpsimd.iota(iota_ci[:], [[1, 1]], base=0, channel_multiplier=1).then_inc(iota_made, 1)

            @block.vector
            def _(dve):
                nc.vector.memset(ones[:], 1.0)
                nc.vector.memset(eps_col[:], EPS)
                dve.wait_ge(iota_made, 1)
                nc.vector.tensor_copy(iota_row[:], iota_i[:])
                nc.vector.tensor_copy(iota_col[:], iota_ci[:]).then_inc(const_made, 1)
                dve.wait_ge(const_made, 1)
                nc.vector.tensor_scalar(ident[:], iota_row[:], iota_col[:, 0:1], None, ALU.is_equal)
                dve.wait_ge(loaded, 5 * DMA)
                nc.vector.tensor_tensor(rel_out[:], dst_rows[:], dst_rows[:, :, 0:1].to_broadcast([tiles // 8, 8, P]),
                                        ALU.subtract).then_inc(rel_made, 1)
                nc.vector.tensor_tensor(rel_cols[:], dst_cols[:], first_all[:], ALU.subtract)

    with ExitStack() as ctx:
        sb = lambda name, shape, dt=F32: ctx.enter_context(nc.sbuf_tensor(name, shape, dt))
        ps = lambda name, shape, dt=F32: ctx.enter_context(nc.psum_tensor(name, shape, dt))
        sem = lambda name: ctx.enter_context(nc.semaphore(name))
        w_qkv = sb("w_qkv", [P, 2 * P])
        b_qkv = sb("b_qkv", [P, 2 * P])
        xT = sb("xT", [P, QT, P])
        qkv = sb("qkv", [P, QT, 2 * P])
        qkv_ps = [ps(f"qkv_ps{i}", [P, 512]) for i in range(QT)]
        weights_in = sem("l0_weights_in")
        x_in = [sem(f"x_in{i}") for i in range(QT)]
        multiplied = sem("qkv_multiplied")
        biased = sem("qkv_biased")
        stored = [sem(f"qkv_stored{i}") for i in range(QT)]
        with nc.Block() as block:
            @block.sync
            def _(sp):
                sp.dma_start(w_qkv[:, 0:P], t["Wqk"]).then_inc(weights_in, DMA)
                sp.dma_start(w_qkv[:, P:], t["Wv"]).then_inc(weights_in, DMA)
                sp.dma_start(b_qkv[:, 0:P], t["bqk"].to_broadcast([P, P])).then_inc(weights_in, DMA)
                sp.dma_start(b_qkv[:, P:], t["bv"].to_broadcast([P, P])).then_inc(weights_in, DMA)

                def body(b, first, last):
                    for i in range(QT):
                        if not first:
                            sp.wait_ge(multiplied, b * QT + i - QT + 1)
                        sp.dma_start(xT[:, i, :], t["xT"][:, bass.ds(b * QW + i * P, P)]).then_inc(x_in[i], DMA)
                groups_of(sp, node_groups, body)

            @block.tensor
            def _(pe):
                pe.wait_ge(weights_in, 4 * DMA)

                def body(b, first, last):
                    for i in range(QT):
                        pe.wait_ge(x_in[i], (b + 1) * DMA)
                        if not first:
                            pe.wait_ge(biased, b * QT + i - QT + 1)
                        nc.tensor.matmul(qkv_ps[i][:, 0:2 * P], xT[:, i, :], w_qkv[:], start=True,
                                         stop=True).then_inc(multiplied, 1)
                groups_of(pe, node_groups, body)

            @block.vector
            def _(dve):
                dve.wait_ge(weights_in, 4 * DMA)

                def body(b, first, last):
                    for i in range(QT):
                        dve.wait_ge(multiplied, b * QT + i + 1)
                        if not first:
                            dve.wait_ge(stored[i], b * DMA)
                        nc.vector.tensor_tensor(qkv[:, i, :], qkv_ps[i][:, 0:2 * P], b_qkv[:],
                                                ALU.add).then_inc(biased, 1)
                groups_of(dve, node_groups, body)

            @block.scalar
            def _(act):
                def body(b, first, last):
                    for i in range(QT):
                        act.wait_ge(biased, b * QT + i + 1)
                        act.dma_start(qkv_tab[bass.ds(b * QW + i * P, P), :], qkv[:, i, :]).then_inc(stored[i], DMA)
                groups_of(act, node_groups, body)
                for i in range(QT):
                    act.wait_ge(stored[i], node_groups * DMA)

    sums = ExitStack()
    node_sums = sums.enter_context(nc.sbuf_tensor("node_sums0", [P, 2, NP], F32))
    with ExitStack() as ctx:
        sb = lambda name, shape, dt=F32: ctx.enter_context(nc.sbuf_tensor(name, shape, dt))
        ps = lambda name, shape, dt=F32: ctx.enter_context(nc.psum_tensor(name, shape, dt))
        sem = lambda name: ctx.enter_context(nc.semaphore(name))
        src_ring = sb("src_ring", [P, CHUNKS], I32)
        rows = sb("rows", [P, CHUNKS, 2 * P])
        window = sb("window", [P, CHUNKS, P])
        rel_bc = sb("rel_bc", [P, QUADS, QW], BF16)
        spread = sb("spread", [P, 2, QW])
        gather1 = sb("gather1", [P, 2, QT, P])
        scores = sb("scores", [P, 2, QT])
        clipped = sb("clipped", [P, 2, QT])
        weight = sb("weight", [P, 2, QT])
        product = sb("product", [P, QT, P])
        q_dst = [ps(f"q_dst{i}", [P, QT, P]) for i in range(2)]
        onehot_ps = [ps(f"onehot_ps{i}", [P, QT, P]) for i in range(2)]
        tile_sums = [ps(f"tile_sums{i}", [P, 2, 2, P]) for i in range(4)]
        quads_asked = sem("quads_asked")
        src_ready = [sem(f"src_ready{i}") for i in range(2)]
        gathered = [sem(f"gathered{q}") for q in range(QUADS)]
        window_in = [sem(f"window_in{q}") for q in range(QUADS)]
        spread_made = sem("spread_made")
        q_spread = sem("q_spread")
        onehot_turned = sem("onehot_turned")
        scored = sem("scored")
        clip_done = sem("clip_done")
        weighted = sem("weighted")
        onehot_made = sem("onehot_made")
        summed = sem("summed")
        added = sem("added")
        cleared = sem("cleared")
        with nc.Block() as block:
            @block.sync
            def _(sp):
                def body(j, first, last):
                    for q in range(QUADS):
                        if not first:
                            sp.wait_ge(q_spread, j * QUADS + q - QUADS + 1)
                        sp.dma_start(rel_bc[:, q, :], rel_rows[bass.ds(j * QUADS + q, 1), :].to_broadcast([P, QW])
                                     ).then_inc(window_in[q], DMA)
                        for i, base in enumerate(window_bases(sp, j, q), q * QT):
                            sp.dma_start(window[:, i, :], qkv_tab[bass.ds(base, P), 0:P]).then_inc(window_in[q], DMA)
                groups_of(sp, groups, body)

            @block.gpsimd
            def _(pool):
                def body(j, first, last):
                    for q in range(QUADS):
                        if q % 2 == 0:
                            pool.wait_ge(src_ready[q // 2], j + 1)
                        if not first:
                            pool.wait_ge(summed, j * QUADS + q - QUADS + 1)
                        pool.sem_inc(quads_asked, 1)
                        for i in range(q * QT, q * QT + QT):
                            nc.gpsimd.indirect_dma_start(
                                out=rows[:, i, :], out_offset=None, in_=qkv_tab,
                                in_offset=bass.IndirectOffsetOnAxis(ap=src_ring[:, i:i + 1], axis=0),
                            ).then_inc(gathered[q], DMA)
                groups_of(pool, groups, body)

            @block.scalar
            def _(act):
                def refill(j, half):
                    a = half * CHUNKS // 2
                    nc.scalar.copy(src_ring[:, a:a + CHUNKS // 2],
                                   src_cols[:, bass.ds(j * CHUNKS + a, CHUNKS // 2)]).then_inc(src_ready[half], 1)

                refill(0, 0)
                refill(0, 1)

                def body(j, first, last):
                    for q in range(QUADS):
                        act.wait_ge(clip_done, j * QUADS + q + 1)
                        nc.scalar.activation(weight[:, q % 2, :], clipped[:, q % 2, :], ACT.Exp).then_inc(weighted, 1)
                        act.wait_ge(weighted, j * QUADS + q + 1)
                        act.wait_ge(onehot_turned, j * QUADS + q + 1)
                        if not (first and q < 2):
                            act.wait_ge(summed, j * QUADS + q - 1)
                        for i in range(QT):
                            o = nc.scalar.mul(gather1[:, q % 2, i, :], onehot_ps[q % 2][:, i, :],
                                              weight[:, q % 2, i:i + 1])
                        o.then_inc(onehot_made, 1)
                        if q == 1 and not last:
                            act.wait_ge(gathered[0], (j + 1) * QT * DMA)
                            act.wait_ge(gathered[1], (j + 1) * QT * DMA)
                            refill(j + 1, 0)
                        if q == 3 and not last:
                            act.wait_ge(gathered[2], (j + 1) * QT * DMA)
                            act.wait_ge(gathered[3], (j + 1) * QT * DMA)
                            refill(j + 1, 1)
                groups_of(act, groups, body)

            @block.tensor
            def _(pe):
                def spread_q(j, q, start=False):
                    pe.wait_ge(spread_made, j * QUADS + q + 1)
                    pe.wait_ge(window_in[q], (j + 1) * (QT + 1) * DMA)
                    if not start:
                        pe.wait_ge(scored, j * QUADS + q - 1)
                    for i in range(QT):
                        mm = nc.tensor.matmul(q_dst[q % 2][:, i, :], spread[:, q % 2, i * P:(i + 1) * P],
                                              window[:, q * QT + i, :], start=True, stop=True)
                    mm.then_inc(q_spread, 1)
                    if not start:
                        pe.wait_ge(onehot_made, j * QUADS + q - 1)
                    for i in range(QT):
                        mm = nc.tensor.transpose(onehot_ps[q % 2][:, i, :], spread[:, q % 2, i * P:(i + 1) * P],
                                                 ident[:])
                    mm.then_inc(onehot_turned, 1)

                def add_up(j, q, start):
                    pe.wait_ge(onehot_made, j * QUADS + q + 1)
                    pe.wait_ge(gathered[q], (j + 1) * QT * DMA)
                    if not start:
                        pe.wait_ge(added, (j * QUADS + q - 1) * QT)
                    for i in range(QT):
                        bank = tile_sums[(q % 2) * 2 + i // 2]
                        nc.tensor.matmul(bank[:, i % 2, 0, :], rows[:, q * QT + i, P:], gather1[:, q % 2, i, :],
                                         start=True, stop=True)
                        mm = nc.tensor.matmul(bank[:, i % 2, 1, :], ones[:], gather1[:, q % 2, i, :],
                                              start=True, stop=True)
                    mm.then_inc(summed, 1)

                spread_q(0, 0, True)

                def body(j, first, last):
                    for q in range(QUADS):
                        if q < QUADS - 1:
                            spread_q(j, q + 1, first and q == 0)
                        elif not last:
                            spread_q(j + 1, 0)
                        add_up(j, q, first and q < 2)
                groups_of(pe, groups, body)

            @block.vector
            def _(dve):
                nc.vector.memset(node_sums[:, 0, :], 0.0)
                nc.vector.memset(node_sums[:, 1, :], TINY).then_inc(cleared, 1)

                def make_spread(j, q, start=False):
                    dve.wait_ge(window_in[q], (j + 1) * (QT + 1) * DMA)
                    if not start:
                        dve.wait_ge(onehot_turned, j * QUADS + q - 1)
                    nc.vector.tensor_scalar(spread[:, q % 2, :], rel_bc[:, q, :], iota_col[:, 0:1], None,
                                            ALU.is_equal).then_inc(spread_made, 1)

                def score(j, q, i):
                    return nc.vector.tensor_tensor_reduce(product[:, i, :], rows[:, q * QT + i, 0:P],
                                                          q_dst[q % 2][:, i, :], float(P) ** -0.5, 0.0,
                                                          ALU.mult, ALU.add, scores[:, q % 2, i:i + 1])

                def add_tile(j, q, i, base, start=False):
                    if not (start and q == 0 and i == 0):
                        dve.wait_ge(added, (j * QUADS + q) * QT + i)
                    span = node_sums[:, :, bass.ds(base, P)]
                    nc.vector.tensor_tensor(span, span, tile_sums[(q % 2) * 2 + i // 2][:, i % 2, :, :],
                                            ALU.add).then_inc(added, 1)

                dve.wait_ge(cleared, 1)
                make_spread(0, 0, True)

                def body(j, first, last):
                    for q in range(QUADS):
                        if q < QUADS - 1:
                            make_spread(j, q + 1, first and q == 0)
                        elif not last:
                            make_spread(j + 1, 0)
                        before = (j, q - 2) if q >= 2 else (j - 1, q + 2)
                        adds = not (first and q < 2)
                        if adds:
                            bases = window_bases(dve, *before)
                            dve.wait_ge(summed, j * QUADS + q - 1)
                        dve.wait_ge(q_spread, j * QUADS + q + 1)
                        dve.wait_ge(gathered[q], (j + 1) * QT * DMA)
                        for i in range(QT):
                            s = score(j, q, i)
                            if i == QT - 1:
                                s.then_inc(scored, 1)
                            if adds:
                                add_tile(*before, i, bases[i], first)
                        dve.wait_ge(scored, j * QUADS + q + 1)
                        nc.vector.tensor_scalar(clipped[:, q % 2, :], scores[:, q % 2, :], 5.0, -5.0, ALU.min,
                                                ALU.max).then_inc(clip_done, 1)
                groups_of(dve, groups, body)
                for q in (QUADS - 2, QUADS - 1):
                    bases = window_bases(dve, groups - 1, q)
                    dve.wait_ge(summed, (groups - 1) * QUADS + q + 1)
                    for i in range(QT):
                        add_tile(groups - 1, q, i, bases[i])
                dve.wait_ge(added, tiles)

    with ExitStack() as ctx:
        sb = lambda name, shape, dt=F32: ctx.enter_context(nc.sbuf_tensor(name, shape, dt))
        ps = lambda name, shape, dt=F32: ctx.enter_context(nc.psum_tensor(name, shape, dt))
        sem = lambda name: ctx.enter_context(nc.semaphore(name))
        w_o = sb("w_o", [P, P])
        w_lr = sb("w_lr", [P, 2 * P])
        b_o = sb("b_o", [P, P])
        b_lr = sb("b_lr", [P, 2 * P])
        gamma = sb("gamma", [P, P])
        beta = sb("beta", [P, P])
        inv_cols = sb("inv_cols", [P, QT, HEADS, HC])
        ln1_col = sb("ln1_col", [P, 1])
        x_nm = sb("x_nm", [P, 2, QT, P])
        inv8 = sb("inv8", [P, 2, QT, HEADS])
        mean_rows = sb("mean_rows", [P, QW])
        x_o = sb("x_o", [P, 2, QT, P])
        h = sb("h", [P, 2, QT, P])
        u = sb("u", [P, 2, QT, P])
        v = sb("v", [P, 2, QT, P])
        stats = sb("stats", [P, 3, QT, 6])
        mv = sb("mv", [P, 3, QT, 2])
        std = sb("std", [P, 3, QT])
        rstd = sb("rstd", [P, 3, QT])
        shift = sb("shift", [P, 3, QT])
        hT = sb("hT", [P, QT, P])
        xlr = sb("xlr", [P, 2, QT, 2 * P])
        w_ps = [ps(f"w_ps{i}", [P, QT, P]) for i in range(2)]
        inv_ps = ps("inv_ps", [P, QW])
        o_ps = ps("o_ps", [P, QT, P])
        t_ps = ps("t_ps", [P, QT, P])
        lr_ps = [ps(f"lr_ps{i}", [P, 2, 2 * P]) for i in range(2)]
        weights_in = sem("l01_weights_in")
        w_scaled = sem("w_lr_scaled")
        x_in = [sem(f"x_nm_in{i}") for i in range(2)]
        step = sem("dve_step")
        weights_turned = sem("weights_turned")
        inverted = sem("inverted")
        inverse_copied = sem("inverse_copied")
        inverse_spread = sem("inverse_spread")
        averaged = sem("averaged")
        projected = sem("projected")
        x_biased = sem("x_biased")
        h_made = sem("h_made")
        var_ready = [sem(f"var_ready{k}") for k in range(3)]
        std_ready = [sem(f"std_ready{k}") for k in range(3)]
        shift_ready = [sem(f"shift_ready{k}") for k in range(3)]
        u_ready = sem("u_ready")
        pool_step = sem("pool_step")
        summed_up = sem("summed_up")
        x1_made = sem("x1_made")
        v_ready = sem("v_ready")
        turned = sem("turned")
        hT_ready = sem("hT_ready")
        lr_ready = sem("lr_ready")
        lr_copied = sem("lr_copied")
        tables_stored = [sem(f"tables_stored{i}") for i in range(2)]
        x_nm_dram = t["x"].rearrange("(b i p) d -> b p i d", i=QT, p=P)
        xl_dram = xl_tab.rearrange("(b i p) d -> b p i d", i=QT, p=P)
        xr_dram = xr_tab.rearrange("(b i p) d -> b p i d", i=QT, p=P)

        def rows_of(w):
            return w[:].unsqueeze(1).to_broadcast([P, QT, P])

        def all_steps(stages):
            for s in range(-2, node_groups + 4):
                for lag, stage in stages:
                    if 0 <= s - lag < node_groups:
                        stage(s - lag)

        with nc.Block() as block:
            @block.sync
            def _(sp):
                for dst, src in ((w_o[:], t["Wo"]), (w_lr[:, 0:P], t["lin_l_wT"]), (w_lr[:, P:], t["lin_r_wT"]),
                                 (b_o[:], t["bo"].to_broadcast([P, P])),
                                 (b_lr[:, 0:P], t["lin_l_b"].to_broadcast([P, P])),
                                 (b_lr[:, P:], t["lin_r_b"].to_broadcast([P, P])),
                                 (gamma[:], t["gamma"].to_broadcast([P, P])), (beta[:], t["beta"].to_broadcast([P, P]))):
                    sp.dma_start(dst, src).then_inc(weights_in, DMA)
                sp.dma_start(ln1_col[:], t["ln1_w"].rearrange("o d -> d o"), allow_slow_non_contiguous=True
                             ).then_inc(weights_in, DMA)
                for b in range(node_groups):
                    if b >= 2:
                        sp.wait_ge(summed_up, b - 1)
                    sp.dma_start(x_nm[:, b % 2], x_nm_dram[b]).then_inc(x_in[b % 2], DMA)

            @block.tensor
            def _(pe):
                def turn_weights(b):
                    if b >= 2:
                        pe.wait_ge(inverted, b - 1)
                    for i in range(QT):
                        at = b * QW + i * P
                        mm = nc.tensor.transpose(w_ps[b % 2][:, i, :], node_sums[:, 1, at:at + P], ident[:])
                    mm.then_inc(weights_turned, 1)

                def spread_inverse(b):
                    pe.wait_ge(inverse_copied, b + 1)
                    if b:
                        pe.wait_ge(averaged, b)
                    for i in range(QT):
                        mm = nc.tensor.transpose(inv_ps[:, i * P:(i + 1) * P],
                                                 inv_cols[:, i].rearrange("p a b -> p (a b)"), ident[:])
                    mm.then_inc(inverse_spread, 1)

                def project(b):
                    pe.wait_ge(averaged, b + 1)
                    if b:
                        pe.wait_ge(h_made, b)
                    for i in range(QT):
                        mm = nc.tensor.matmul(o_ps[:, i, :], mean_rows[:, i * P:(i + 1) * P], w_o[:], start=True,
                                              stop=True)
                    mm.then_inc(projected, 1)

                def turn_v(b):
                    pe.wait_ge(v_ready, b + 1)
                    for i in range(QT):
                        mm = nc.tensor.transpose(t_ps[:, i, :], v[:, b % 2, i, :], ident[:])
                    mm.then_inc(turned, 1)

                def tables(b):
                    pe.wait_ge(hT_ready, b + 1)
                    if b:
                        pe.wait_ge(lr_copied, b)
                    for i in range(QT):
                        mm = nc.tensor.matmul(lr_ps[i // 2][:, i % 2, :], hT[:, i, :], w_lr[:], start=True, stop=True)
                    mm.then_inc(lr_ready, 1)

                pe.wait_ge(weights_in, 9 * DMA)
                pe.wait_ge(w_scaled, 1)
                all_steps([(0, project), (3, turn_v), (-1, spread_inverse), (-2, turn_weights), (3, tables)])

            @block.vector
            def _(dve):
                n = [0]

                def link(ins):
                    n[0] += 1
                    ins.then_inc(step, 1)
                    dve.wait_ge(step, n[0])

                def moments(k, src):
                    for i in range(QT):
                        ins = nc.vector.bn_stats(stats[:, k, i, :], src[:, i, :])
                    link(ins)
                    for i in range(QT):
                        ins = nc.vector.bn_aggr(mv[:, k, i, :], stats[:, k, i, :])
                    ins.then_inc(var_ready[k], 1)

                def shift_of(b, k, used):
                    dve.wait_ge(std_ready[k], b + 1)
                    if b:
                        dve.wait_ge(used, b)
                    link(nc.vector.reciprocal(rstd[:, k, :], std[:, k, :]))
                    nc.vector.scalar_tensor_tensor(shift[:, k, :], mv[:, k, :, 0], -1.0, rstd[:, k, :], ALU.mult,
                                                   ALU.mult).then_inc(shift_ready[k], 1)

                def invert(b):
                    dve.wait_ge(weights_turned, b + 1)
                    if b >= 2:
                        dve.wait_ge(inverse_copied, b - 1)
                    nc.vector.reciprocal(inv8[:, b % 2], w_ps[b % 2][:, :, ::HC]).then_inc(inverted, 1)

                def average(b):
                    dve.wait_ge(inverse_spread, b + 1)
                    if b:
                        dve.wait_ge(projected, b)
                    nc.vector.tensor_tensor(mean_rows[:], node_sums[:, 0, b * QW:(b + 1) * QW], inv_ps[:],
                                            ALU.mult).then_inc(averaged, 1)

                def residual(b):
                    dve.wait_ge(x_biased, b + 1)
                    dve.wait_ge(projected, b + 1)
                    if b >= 2:
                        dve.wait_ge(x1_made, b - 1)
                    nc.vector.tensor_tensor(h[:, b % 2], o_ps[:], x_o[:, b % 2], ALU.add).then_inc(h_made, 1)
                    dve.wait_ge(h_made, b + 1)
                    moments(0, h[:, b % 2])

                def moments1(b):
                    dve.wait_ge(summed_up, b + 1)
                    moments(1, h[:, b % 2])

                def add_bias(b):
                    dve.wait_ge(lr_ready, b + 1)
                    if b >= 2:
                        dve.wait_ge(tables_stored[b % 2], 2 * (b // 2) * DMA)
                    bias = b_lr[:].unsqueeze(1).to_broadcast([P, 2, 2 * P])
                    nc.vector.tensor_tensor(xlr[:, b % 2, 0:2, :], lr_ps[0][:], bias, ALU.add)
                    nc.vector.tensor_tensor(xlr[:, b % 2, 2:4, :], lr_ps[1][:], bias, ALU.add).then_inc(lr_copied, 1)

                def moments2(b):
                    dve.wait_ge(x1_made, b + 1)
                    moments(2, x1[:, b])

                dve.wait_ge(weights_in, 9 * DMA)
                nc.vector.tensor_scalar(w_lr[:], w_lr[:], ln1_col[:, 0:1], None, ALU.mult).then_inc(w_scaled, 1)
                all_steps([(0, average), (1, residual), (3, lambda b: shift_of(b, 2, v_ready)), (-1, invert),
                           (2, moments1), (1, lambda b: shift_of(b, 0, u_ready)), (2, lambda b: shift_of(b, 1, x1_made)), (4, add_bias), (2, moments2)])

            @block.gpsimd
            def _(pool):
                n = [0]

                def link(ins):
                    n[0] += 1
                    ins.then_inc(pool_step, 1)
                    pool.wait_ge(pool_step, n[0])

                def bias(b):
                    x = x_nm[:, b % 2]
                    pool.wait_ge(x_in[b % 2], (b // 2 + 1) * DMA)
                    if b >= 2:
                        pool.wait_ge(h_made, b - 1)
                    nc.gpsimd.tensor_tensor(x_o[:, b % 2], x, rows_of(b_o), ALU.add).then_inc(x_biased, 1)
                    link(nc.gpsimd.tensor_tensor(x, x, rows_of(beta), ALU.add))

                def affine(b):
                    y, x = u[:, b % 2], x_nm[:, b % 2]
                    pool.wait_ge(u_ready, b + 1)
                    link(nc.gpsimd.tensor_tensor(y, y, rows_of(gamma), ALU.mult))
                    nc.gpsimd.tensor_tensor(h[:, b % 2], y, x, ALU.add).then_inc(summed_up, 1)

                pool.wait_ge(weights_in, 9 * DMA)
                all_steps([(0, bias), (1, affine)])

            @block.scalar
            def _(act):
                def root(b, k):
                    act.wait_ge(var_ready[k], b + 1)
                    nc.scalar.activation(std[:, k, :], mv[:, k, :, 1], ACT.Sqrt,
                                         bias=eps_col[:, 0:1]).then_inc(std_ready[k], 1)

                def norm(b, k, out, rows, done):
                    act.wait_ge(shift_ready[k], b + 1)
                    for i in range(QT):
                        ins = nc.scalar.activation(out[:, i, :], rows[:, i, :], ACT.Identity,
                                                   bias=shift[:, k, i:i + 1], scale=rstd[:, k, i:i + 1])
                    ins.then_inc(done, 1)

                def copy_inverse(b):
                    act.wait_ge(inverted, b + 1)
                    if b:
                        act.wait_ge(inverse_spread, b)
                    nc.scalar.copy(inv_cols[:], inv8[:, b % 2].unsqueeze(3).to_broadcast([P, QT, HEADS, HC])
                                   ).then_inc(inverse_copied, 1)

                def norm0(b):
                    if b >= 2:
                        act.wait_ge(summed_up, b - 1)
                    norm(b, 0, u[:, b % 2], h[:, b % 2], u_ready)

                def norm2(b):
                    if b >= 2:
                        act.wait_ge(turned, b - 1)
                    norm(b, 2, v[:, b % 2], x1[:, b], v_ready)

                def copy_hT(b):
                    act.wait_ge(turned, b + 1)
                    if b:
                        act.wait_ge(lr_ready, b)
                    nc.scalar.copy(hT[:], t_ps[:]).then_inc(hT_ready, 1)

                def store_tables(b):
                    act.wait_ge(lr_copied, b + 1)
                    act.dma_start(xl_dram[b], xlr[:, b % 2, :, 0:P]).then_inc(tables_stored[b % 2], DMA)
                    act.dma_start(xr_dram[b], xlr[:, b % 2, :, P:]).then_inc(tables_stored[b % 2], DMA)

                def norm1(b):
                    norm(b, 1, x1[:, b], h[:, b % 2], x1_made)

                all_steps([(1, lambda b: root(b, 0)), (3, norm2), (-1, copy_inverse), (2, lambda b: root(b, 1)), (1, norm0),
                           (2, norm1), (3, copy_hT), (4, store_tables), (2, lambda b: root(b, 2))])
                for i in range(2):
                    act.wait_ge(tables_stored[i], 2 * ((node_groups + 1 - i) // 2) * DMA)
    sums.close()

    attention = ExitStack()
    logits = attention.enter_context(nc.sbuf_tensor("logits", [P, CW], F32))
    maxima = ExitStack()
    largest = maxima.enter_context(nc.sbuf_tensor("largest", [P, CW], F32))
    last_fence = maxima.enter_context(nc.sbuf_tensor("last_fence", [P, CW], BF16))
    head_fence = maxima.enter_context(nc.sbuf_tensor("head_fence", [P, CW], BF16))
    head_max = maxima.enter_context(nc.sbuf_tensor("head_max", [P, groups], F32))
    with ExitStack() as ctx:
        sb = lambda name, shape, dt=F32: ctx.enter_context(nc.sbuf_tensor(name, shape, dt))
        ps = lambda name, shape, dt=F32: ctx.enter_context(nc.psum_tensor(name, shape, dt))
        sem = lambda name: ctx.enter_context(nc.semaphore(name))
        w_e = sb("w_e", [P, P])
        att_pad = sb("att_pad", [P, CHUNKS, CHUNKS, HEADS])
        src_ring = sb("src_ring1", [P, CHUNKS], I32)
        rows = sb("rows1", [P, CHUNKS, P])
        window = sb("window1", [P, CHUNKS, P])
        attr = sb("attr", [P, QUADS, QW])
        rel_bc = sb("rel_bc1", [P, QUADS, QW], BF16)
        spread = sb("spread1", [P, 2, QW])
        z_low = sb("z_low", [P, 2, QW])
        z_act = sb("z_act", [P, 2, QW])
        z_ps = [ps(f"z_ps{i}", [P, QW]) for i in range(2)]
        lg_ps = ps("lg_ps", [P, P])
        weights_in = sem("l1_weights_in")
        pad_cleared = sem("pad_cleared")
        att_in = sem("att_in")
        quads_asked = sem("quads_asked1")
        src_ready = [sem(f"src_ready1_{i}") for i in range(2)]
        gathered = [sem(f"gathered1_{q}") for q in range(QUADS)]
        window_in = [sem(f"window_in1_{q}") for q in range(QUADS)]
        attr_in = [sem(f"attr_in{q}") for q in range(QUADS)]
        kept = [sem(f"xl_kept{q}") for q in range(QUADS)]
        spread_made = sem("spread_made1")
        z_ready = sem("z_ready")
        low_ready = sem("low_ready")
        z_act_ready = sem("z_act_ready")
        lg_ready = sem("lg_ready")
        lg_quads = sem("lg_quads")
        lg_copied = sem("lg_copied")
        halo = sb("halo", [P, P + 2], I32)
        chunk_first = sb("chunk_first", [P, 1], I32)
        chunk_first_f = sb("chunk_first_f", [P, 1])
        flags = sb("flags", [P, 2, P])
        first_fence = sb("first_fence", [P, P])
        head_now = sb("head_now", [P, P])
        onehot = sb("onehot_bf", [P, 2, QT, P], BF16)
        halo_in = sem("halo_in")
        chunk_first_in = sem("chunk_first_in")
        chunk_first_made = sem("chunk_first_made")
        flags_made = sem("flags_made")
        fences_made = sem("fences_made")
        scanned = sem("scanned")
        onehot_made = sem("onehot_bf_made")
        onehot_kept = [sem(f"onehot_kept{i}") for i in range(2)]
        with nc.Block() as block:
            @block.sync
            def _(sp):
                sp.dma_start(w_e[:], t["lin_edge_wT"]).then_inc(weights_in, DMA)
                sp.dma_start(chunk_first[:], bass.AP(t["dst_nat"].tensor, 1, [[CW, CHUNKS], [0, HEADS], [1, 1]]),
                             allow_slow_non_contiguous=True).then_inc(chunk_first_in, DMA)
                sp.wait_ge(pad_cleared, 1)
                for hd in range(HEADS):
                    diag = bass.AP(att_pad[:].tensor, att_pad[hd * HC:(hd + 1) * HC, 0, 0, hd:hd + 1].offset,
                                   [list(att_pad[hd * HC:(hd + 1) * HC].ap[0]), [CHUNKS * HEADS + HEADS, CHUNKS], [1, 1]])
                    sp.dma_start(diag, t["att"][hd].rearrange("(c o) -> c o", o=1).unsqueeze(2).to_broadcast([HC, CHUNKS, 1]),
                                 allow_slow_non_contiguous=True).then_inc(att_in, DMA)

                def body(j, first, last):
                    for q in range(QUADS):
                        if not first:
                            sp.wait_ge(z_ready, j * QUADS + q - QUADS + 1)
                        sp.dma_start(rel_bc[:, q, :], rel_rows[bass.ds(j * QUADS + q, 1), :].to_broadcast([P, QW])
                                     ).then_inc(window_in[q], DMA)
                        for i, base in enumerate(window_bases(sp, j, q), q * QT):
                            sp.dma_start(window[:, i, :], xr_tab[bass.ds(base, P), :]).then_inc(window_in[q], DMA)
                        if q == 1:
                            if not first:
                                sp.wait_ge(fences_made, 3 * j)
                            sp.dma_start(halo[:], t["dst_halo"][bass.ds(j, 1)].rearrange("a c e -> (a c) e").unsqueeze(1)
                                         .to_broadcast([CHUNKS, HEADS, P + 2])).then_inc(halo_in, DMA)
                groups_of(sp, groups, body)

            @block.gpsimd
            def _(pool):
                def body(j, first, last):
                    for q in range(QUADS):
                        if q % 2 == 0:
                            pool.wait_ge(src_ready[q // 2], j + 1)
                        if not first:
                            pool.wait_ge(z_ready, j * QUADS + q - QUADS + 1)
                            pool.wait_ge(kept[q], j * DMA)
                        pool.sem_inc(quads_asked, 1)
                        for i in range(q * QT, q * QT + QT):
                            nc.gpsimd.indirect_dma_start(
                                out=rows[:, i, :], out_offset=None, in_=xl_tab,
                                in_offset=bass.IndirectOffsetOnAxis(ap=src_ring[:, i:i + 1], axis=0),
                            ).then_inc(gathered[q], DMA)
                groups_of(pool, groups, body)

            @block.scalar
            def _(act):
                def refill(j, half):
                    a = half * CHUNKS // 2
                    nc.scalar.copy(src_ring[:, a:a + CHUNKS // 2],
                                   src_cols[:, bass.ds(j * CHUNKS + a, CHUNKS // 2)]).then_inc(src_ready[half], 1)

                def load_attr(j, q):
                    act.dma_start(attr[:, q, :], t["attrT"][bass.ds(j, 1), :, q * QW:(q + 1) * QW].rearrange("a p e -> (a p) e")
                                  ).then_inc(attr_in[q], DMA)

                refill(0, 0)
                refill(0, 1)
                for q in range(QUADS):
                    load_attr(0, q)

                def body(j, first, last):
                    for q in range(QUADS):
                        act.wait_ge(z_ready, j * QUADS + q + 1)
                        if not (first and q < 2):
                            act.wait_ge(z_act_ready, j * QUADS + q - 1)
                        nc.scalar.mul(z_low[:, q % 2, :], z_ps[q % 2][:], 0.2).then_inc(low_ready, 1)
                        act.wait_ge(gathered[q], (j + 1) * QT * DMA)
                        act.dma_start(xl_edges[bass.ds(j, 1), :, q * QW:(q + 1) * QW].rearrange("a p e -> (a p) e"),
                                      rows[:, q * QT:(q + 1) * QT, :].rearrange("p i d -> p (i d)")).then_inc(kept[q], DMA)
                        act.wait_ge(onehot_made, j * QUADS + q + 1)
                        act.dma_start(onehot_edges[bass.ds(j, 1), :, q * QW:(q + 1) * QW].rearrange("a p e -> (a p) e"),
                                      onehot[:, q % 2].rearrange("p i d -> p (i d)")).then_inc(onehot_kept[q % 2], DMA)
                        if not last:
                            load_attr(j + 1, q)
                            if q == 1:
                                refill(j + 1, 0)
                            if q == 3:
                                refill(j + 1, 1)
                groups_of(act, groups, body)
                for q in range(QUADS):
                    act.wait_ge(kept[q], groups * DMA)
                for i in range(2):
                    act.wait_ge(onehot_kept[i], 2 * groups * DMA)

            @block.tensor
            def _(pe):
                def make_z(j, q, start=False):
                    pe.wait_ge(attr_in[q], (j + 1) * DMA)
                    if not start:
                        pe.wait_ge(z_act_ready, j * QUADS + q - 1)
                        pe.wait_ge(low_ready, j * QUADS + q - 1)
                    z = z_ps[q % 2]
                    nc.tensor.matmul(z[:], w_e[:], attr[:, q, :], start=True, stop=False)
                    pe.wait_ge(spread_made, j * QUADS + q + 1)
                    pe.wait_ge(window_in[q], (j + 1) * (QT + 1) * DMA)
                    for i in range(QT):
                        nc.tensor.matmul(z[:, i * P:(i + 1) * P], window[:, q * QT + i, :],
                                         spread[:, q % 2, i * P:(i + 1) * P], start=False, stop=False)
                    pe.wait_ge(gathered[q], (j + 1) * QT * DMA)
                    for i in range(QT):
                        mm = nc.tensor.matmul(z[:, i * P:(i + 1) * P], rows[:, q * QT + i, :], ident[:],
                                              start=False, stop=(i == QT - 1))
                    mm.then_inc(z_ready, 1)

                def make_logits(j, q, first):
                    pe.wait_ge(z_act_ready, j * QUADS + q + 1)
                    if q == 0 and not first:
                        pe.wait_ge(lg_copied, j)
                    for i in range(QT):
                        c = q * QT + i
                        mm = nc.tensor.matmul(lg_ps[:], att_pad[:, c].rearrange("p a b -> p (a b)"),
                                              z_act[:, q % 2, i * P:(i + 1) * P], start=(c == 0),
                                              stop=(c == CHUNKS - 1))
                    mm.then_inc(lg_quads, 1)

                pe.wait_ge(weights_in, DMA)
                pe.wait_ge(att_in, HEADS * DMA)
                make_z(0, 0, True)

                def body(j, first, last):
                    for q in range(QUADS):
                        if q < QUADS - 1:
                            make_z(j, q + 1, first and q == 0)
                        elif not last:
                            make_z(j + 1, 0)
                        make_logits(j, q, first)
                groups_of(pe, groups, body)

            @block.vector
            def _(dve):
                nc.vector.memset(att_pad[:], 0.0).then_inc(pad_cleared, 1)

                def make_spread(j, q, start=False):
                    dve.wait_ge(window_in[q], (j + 1) * (QT + 1) * DMA)
                    if not start:
                        dve.wait_ge(z_ready, j * QUADS + q - 1)
                    nc.vector.tensor_scalar(spread[:, q % 2, :], rel_bc[:, q, :], iota_col[:, 0:1], None,
                                            ALU.is_equal).then_inc(spread_made, 1)

                def make_onehots(j, q, start):
                    if not start:
                        dve.wait_ge(onehot_kept[q % 2], (j * 2 + q // 2) * DMA)
                    for i in range(QT):
                        o = nc.vector.tensor_scalar(onehot[:, q % 2, i, :], iota_row[:],
                                                    rel_cols[:, bass.ds(j * CHUNKS + q * QT + i, 1)], None,
                                                    ALU.is_equal)
                    o.then_inc(onehot_made, 1)

                def fence_off(j, first):
                    at = bass.ds(j * P, P)
                    dve.wait_ge(halo_in, (j + 1) * DMA)
                    if not first:
                        dve.wait_ge(scanned, 3 * j)
                    nc.vector.tensor_tensor(flags[:, 0, :], halo[:, 1:P + 1], halo[:, 0:P], ALU.not_equal)
                    nc.vector.tensor_tensor(flags[:, 1, :], halo[:, 1:P + 1], halo[:, 2:P + 2],
                                            ALU.not_equal).then_inc(flags_made, 1)
                    nc.vector.tensor_scalar(head_fence[:, at], halo[:, 1:P + 1], chunk_first_f[:, 0:1], -BIG,
                                            ALU.not_equal, ALU.mult).then_inc(fences_made, 1)
                    dve.wait_ge(flags_made, j + 1)
                    nc.vector.tensor_scalar(first_fence[:], flags[:, 0, :], -BIG, None, ALU.mult).then_inc(fences_made, 1)
                    nc.vector.tensor_scalar(last_fence[:, at], flags[:, 1, :], -BIG, None,
                                            ALU.mult).then_inc(fences_made, 1)

                def scan_group(j, first):
                    at = bass.ds(j * P, P)
                    dve.wait_ge(lg_quads, j * QUADS + QUADS)
                    nc.vector.tensor_copy(logits[:, at], lg_ps[:]).then_inc(lg_copied, 1)
                    dve.wait_ge(lg_copied, j + 1)
                    dve.wait_ge(fences_made, 3 * j + 3)
                    before = -BIG if first else largest[:, bass.ds(j * P - 1, 1)]
                    nc.vector.tensor_tensor_scan(largest[:, at], first_fence[:], logits[:, at], before, ALU.add,
                                                 ALU.max).then_inc(scanned, 1)
                    dve.wait_ge(scanned, 3 * j + 1)
                    nc.vector.tensor_tensor(head_now[:], largest[:, at], head_fence[:, at], ALU.add).then_inc(scanned, 1)
                    dve.wait_ge(scanned, 3 * j + 2)
                    nc.vector.tensor_reduce(head_max[:, bass.ds(j, 1)], head_now[:], AX.X, ALU.max).then_inc(scanned, 1)

                dve.wait_ge(chunk_first_in, DMA)
                nc.vector.tensor_copy(chunk_first_f[:], chunk_first[:]).then_inc(chunk_first_made, 1)
                dve.wait_ge(chunk_first_made, 1)
                make_spread(0, 0, True)

                def body(j, first, last):
                    for q in range(QUADS):
                        if q < QUADS - 1:
                            make_spread(j, q + 1, first and q == 0)
                        elif not last:
                            make_spread(j + 1, 0)
                        make_onehots(j, q, first and q < 2)
                        if q == 2:
                            fence_off(j, first)
                        dve.wait_ge(low_ready, j * QUADS + q + 1)
                        if not (first and q < 2):
                            dve.wait_ge(lg_quads, j * QUADS + q - 1)
                        nc.vector.tensor_tensor(z_act[:, q % 2, :], z_ps[q % 2][:], z_low[:, q % 2, :],
                                                ALU.max).then_inc(z_act_ready, 1)
                    scan_group(j, first)
                groups_of(dve, groups, body)
                dve.wait_ge(scanned, 3 * groups)

    with ExitStack() as ctx:
        sb = lambda name, shape, dt=F32: ctx.enter_context(nc.sbuf_tensor(name, shape, dt))
        sem = lambda name: ctx.enter_context(nc.semaphore(name))
        ends = sb("ends", [P, 2])
        turned = sb("turned", [HEADS, 2, CHUNKS])
        enter = sb("enter", [P, 2])
        entering = sb("entering", [HEADS, 2, CHUNKS])
        scanned_ends = sb("scanned_ends", [HEADS, 2, CHUNKS])
        edge_dst = sb("edge_dst", [HEADS, 4, CHUNKS], I32)
        bars = sb("bars", [HEADS, 4, CHUNKS])
        right = sb("right", [HEADS, 2, CHUNKS])
        dst_in = sem("edge_dst_in")
        step = sem("ends_step")
        ends_ready = sem("ends_ready")
        ends_out = sem("ends_out")
        ends_turned = sem("ends_turned")
        entering_ready = sem("entering_ready")
        enter_out = sem("enter_out")
        enter_in = sem("enter_in")
        nat = t["dst_nat"].tensor
        BEFORE, FIRST, LAST, AFTER = range(4)
        START, INSIDE, WHOLE, END = range(4)
        with nc.Block() as block:
            @block.sync
            def _(sp):
                for k, off in ((BEFORE, 0), (FIRST, 1), (LAST, CW), (AFTER, CW + 1)):
                    sp.dma_start(edge_dst[:, k, :], bass.AP(nat, off, [[0, HEADS], [CW, CHUNKS], [1, 1]]),
                                 allow_slow_non_contiguous=True).then_inc(dst_in, DMA)
                sp.wait_ge(ends_ready, 1)
                sp.dma_start(ends_dram, ends[:]).then_inc(ends_out, DMA)
                sp.wait_ge(ends_out, DMA)
                sp.dma_start(turned[:], ends_dram.rearrange("(c h) m -> h m c", h=HEADS),
                             allow_slow_non_contiguous=True).then_inc(ends_turned, DMA)
                sp.wait_ge(entering_ready, 2)
                sp.dma_start(enter_dram.rearrange("(c h) m -> h m c", h=HEADS), entering[:],
                             allow_slow_non_contiguous=True).then_inc(enter_out, DMA)
                sp.wait_ge(enter_out, DMA)
                sp.dma_start(enter[:], enter_dram).then_inc(enter_in, DMA)

            @block.vector
            def _(dve):
                n = [0]

                def link(ins):
                    n[0] += 1
                    ins.then_inc(step, 1)
                    dve.wait_ge(step, n[0])

                nc.vector.tensor_copy(ends[:, 0:1], largest[:, CW - 1:CW])
                nc.vector.tensor_reduce(ends[:, 1:2], head_max[:], AX.X, ALU.max).then_inc(ends_ready, 1)
                dve.wait_ge(dst_in, 4 * DMA)
                for k, a, b in ((START, BEFORE, FIRST), (INSIDE, BEFORE, LAST), (WHOLE, FIRST, LAST), (END, LAST, AFTER)):
                    ins = nc.vector.tensor_tensor(bars[:, k, :], edge_dst[:, a, :], edge_dst[:, b, :], ALU.not_equal)
                link(ins)
                link(nc.vector.tensor_scalar(bars[:], bars[:], -BIG, None, ALU.mult))
                nc.vector.memset(entering[:], -BIG)
                C1 = CHUNKS - 1
                nc.vector.tensor_tensor(right[:, 0, 0:C1], bars[:, END, 0:C1], bars[:, WHOLE, 1:], ALU.add)
                dve.wait_ge(ends_turned, DMA)
                link(nc.vector.tensor_tensor(right[:, 1, 0:C1], bars[:, END, 0:C1], turned[:, 1, 1:], ALU.add))
                nc.vector.tensor_tensor_scan(scanned_ends[:, 0, :], bars[:, INSIDE, :], turned[:, 0, :], -BIG,
                                             ALU.add, ALU.max)
                nc.vector.tensor_tensor_scan(entering[:, 1, C1 - 1::-1], right[:, 0, C1 - 1::-1],
                                             right[:, 1, C1 - 1::-1], -BIG, ALU.add,
                                             ALU.max).then_inc(entering_ready, 1)
                dve.wait_ge(entering_ready, 1)
                nc.vector.tensor_tensor(entering[:, 0, 1:], scanned_ends[:, 0, 0:C1], bars[:, START, 1:],
                                        ALU.add).then_inc(entering_ready, 1)
                dve.wait_ge(enter_in, DMA)
                link(nc.vector.scalar_tensor_tensor(largest[:], head_fence[:], enter[:, 0:1], largest[:], ALU.add,
                                                    ALU.max))
                link(nc.vector.tensor_tensor_scan(largest[:, ::-1], last_fence[:, ::-1], largest[:, ::-1],
                                                  enter[:, 1:2], ALU.add, ALU.max))
                nc.vector.tensor_tensor(logits[:], logits[:], largest[:], ALU.subtract)
    maxima.close()

    sums = ExitStack()
    node_sums = [sums.enter_context(nc.sbuf_tensor(f"node_sums1_{k}", [P, 2, NP], F32)) for k in range(2)]
    with ExitStack() as ctx:
        sb = lambda name, shape, dt=F32: ctx.enter_context(nc.sbuf_tensor(name, shape, dt))
        ps = lambda name, shape, dt=F32: ctx.enter_context(nc.psum_tensor(name, shape, dt))
        sem = lambda name: ctx.enter_context(nc.semaphore(name))
        rows = sb("rows2", [P, QUADS, QW])
        message = sb("message", [P, QUADS, QW])
        power = sb("power", [P, P])
        numerator = sb("numerator", [P, QUADS, QW])
        onehot_in = sb("onehot_in", [P, QUADS, QW], BF16)
        onehot = sb("onehot", [P, 2, QT, P])
        tile_sums = [ps(f"tile_sums1_{i}", [P, 2, 2, P]) for i in range(4)]
        num_ps = ps("num_ps", [P, QUADS, QT * HEADS])
        rows_in = [sem(f"rows_in{q}") for q in range(QUADS)]
        powered = sem("powered")
        num_turned = sem("num_turned")
        numerator_made = sem("numerator_made")
        message_made = sem("message_made")
        onehot_made = sem("onehot_made1")
        summed = sem("summed1")
        added = sem("added1")
        cleared = sem("cleared1")
        with nc.Block() as block:
            @block.sync
            def _(sp):
                def body(j, first, last):
                    for q in range(QUADS):
                        if not first:
                            sp.wait_ge(message_made, j * QUADS + q - QUADS + 1)
                            sp.wait_ge(onehot_made, j * QUADS + q - QUADS + 1)
                        sp.dma_start(rows[:, q, :], xl_edges[bass.ds(j, 1), :, q * QW:(q + 1) * QW].rearrange("a p e -> (a p) e")
                                     ).then_inc(rows_in[q], DMA)
                        sp.dma_start(onehot_in[:, q, :],
                                     onehot_edges[bass.ds(j, 1), :, q * QW:(q + 1) * QW].rearrange("a p e -> (a p) e")
                                     ).then_inc(rows_in[q], DMA)
                groups_of(sp, groups, body)

            @block.scalar
            def _(act):
                def exponentiate(j, start):
                    if not start:
                        act.wait_ge(num_turned, j)
                    nc.scalar.activation(power[:], logits[:, bass.ds(j * P, P)], ACT.Exp).then_inc(powered, 1)

                exponentiate(0, True)

                def body(j, first, last):
                    for q in range(QUADS):
                        act.wait_ge(num_turned, j + 1)
                        if not first:
                            act.wait_ge(summed, j * QUADS + q - QUADS + 1)
                        nc.scalar.copy(numerator[:, q, :].rearrange("p (a b) -> p a b", b=HC),
                                       num_ps[:, q, :].unsqueeze(2).to_broadcast([P, QT * HEADS, HC])
                                       ).then_inc(numerator_made, 1)
                        act.wait_ge(rows_in[q], (j + 1) * 2 * DMA)
                        if not (first and q < 2):
                            act.wait_ge(summed, j * QUADS + q - 1)
                        nc.scalar.copy(onehot[:, q % 2].rearrange("p i n -> p (i n)"),
                                       onehot_in[:, q, :]).then_inc(onehot_made, 1)
                        if q == 0 and not last:
                            exponentiate(j + 1, False)
                groups_of(act, groups, body)

            @block.gpsimd
            def _(pool):
                nc.gpsimd.memset(node_sums[1][:], 0.0).then_inc(cleared, 1)

                def body(j, first, last):
                    for q in range(QUADS):
                        pool.wait_ge(rows_in[q], (j + 1) * 2 * DMA)
                        pool.wait_ge(numerator_made, j * QUADS + q + 1)
                        if not first:
                            pool.wait_ge(summed, j * QUADS + q - QUADS + 1)
                        nc.gpsimd.tensor_tensor(message[:, q, :], rows[:, q, :], numerator[:, q, :],
                                                ALU.mult).then_inc(message_made, 1)
                groups_of(pool, groups, body)

            @block.tensor
            def _(pe):
                def turn(j, start):
                    pe.wait_ge(powered, j + 1)
                    if not start:
                        pe.wait_ge(numerator_made, j * QUADS)
                    nc.tensor.transpose(num_ps[:].rearrange("p q n -> p (q n)"), power[:], ident[:]
                                        ).then_inc(num_turned, 1)

                turn(0, True)

                def body(j, first, last):
                    for q in range(QUADS):
                        pe.wait_ge(onehot_made, j * QUADS + q + 1)
                        pe.wait_ge(message_made, j * QUADS + q + 1)
                        if not (first and q < 2):
                            pe.wait_ge(added, (j * QUADS + q - 1) * QT)
                        for i in range(QT):
                            bank = tile_sums[(q % 2) * 2 + i // 2]
                            nc.tensor.matmul(bank[:, i % 2, 0, :], message[:, q, i * P:(i + 1) * P],
                                             onehot[:, q % 2, i, :], start=True, stop=True)
                            mm = nc.tensor.matmul(bank[:, i % 2, 1, :], numerator[:, q, i * P:(i + 1) * P],
                                                  onehot[:, q % 2, i, :], start=True, stop=True)
                        mm.then_inc(summed, 1)
                        if q == 1 and not last:
                            turn(j + 1, False)
                groups_of(pe, groups, body)

            @block.vector
            def _(dve):
                def add_tile(j, q, i, base, start=False):
                    if not (start and q == 0 and i < 2):
                        dve.wait_ge(added, (j * QUADS + q) * QT + i - 1)
                    span = node_sums[i % 2][:, :, bass.ds(base, P)]
                    nc.vector.tensor_tensor(span, span, tile_sums[(q % 2) * 2 + i // 2][:, i % 2, :, :],
                                            ALU.add).then_inc(added, 1)

                nc.vector.memset(node_sums[0][:, 0, :], 0.0)
                nc.vector.memset(node_sums[0][:, 1, :], TINY).then_inc(cleared, 1)
                dve.wait_ge(cleared, 2)

                def body(j, first, last):
                    for q in range(QUADS):
                        bases = window_bases(dve, j, q)
                        dve.wait_ge(summed, j * QUADS + q + 1)
                        for i in range(QT):
                            add_tile(j, q, i, bases[i], first)
                groups_of(dve, groups, body)
                dve.wait_ge(added, tiles)


    FC = 4
    with ExitStack() as ctx:
        sb = lambda name, shape, dt=F32: ctx.enter_context(nc.sbuf_tensor(name, shape, dt))
        ps = lambda name, shape, dt=F32: ctx.enter_context(nc.psum_tensor(name, shape, dt))
        sem = lambda name: ctx.enter_context(nc.semaphore(name))
        fc = sb("fc", [P, FC * P])
        proj = sb("proj", [P, FC, P])
        a_bias = sb("a_bias", [P, P])
        ln2_col = sb("ln2_col", [P, 1])
        inv8 = sb("inv8_1", [P, 2, QT, HEADS])
        mean = sb("mean1", [P, QT, P])
        x1_bias = sb("x1_bias", [P, 2, QT, P])
        x2 = sb("x2", [P, 2, QT, P])
        x12 = sb("x12", [P, 2, QT, P])
        total = sb("total", [P, 2, QT, P])
        u = sb("u1", [P, 2, QT, P])
        result = sb("result", [P, 2, QT, P])
        stats = sb("stats1", [P, 2, QT, 6])
        mv = sb("mv1", [P, 2, QT, 2])
        std = sb("std1", [P, 2, QT])
        rstd = sb("rstd1", [P, 2, QT])
        hT = sb("hT1", [P, QW])
        hidden = logits[:, 0:2 * FC * QW].rearrange("p (a k e) -> p a k e", a=2, k=FC)
        w_ps = ps("weights_ps", [P, QT, P])
        a_ps = ps("a_ps", [P, QT, P])
        t_ps = ps("t_ps1", [P, QW])
        f_ps = [ps(f"f_ps{i}", [P, QW]) for i in range(FC)]
        y_ps = ps("y_ps", [P, QT, P])
        weights_in = sem("mlp_weights_in")
        fc_scaled = sem("fc_scaled")
        step = sem("dve_step1")
        merged = sem("sums_merged")
        biased = sem("x1_biased")
        weights_turned = sem("weights_turned1")
        inverted = sem("inverted1")
        row_major = sem("row_major")
        mean_made = sem("mean_made")
        x2_made = sem("x2_made")
        var_ready = [sem(f"var_ready1_{k}") for k in range(2)]
        std_ready = [sem(f"std_ready1_{k}") for k in range(2)]
        u_ready = sem("u_ready1")
        x12_ready = sem("x12_ready")
        turned = sem("turned1")
        hT_ready = sem("hT_ready1")
        fc_ready = sem("fc_ready")
        relu_ready = sem("relu_ready")
        y_ready = sem("y_ready")
        total_ready = sem("total_ready")
        result_ready = sem("result_ready")
        out_stored = [sem(f"out_stored{i}") for i in range(2)]
        out_dram = t["out"].rearrange("(b i p) d -> b p i d", i=QT, p=P)

        def all_steps(stages):
            for s in range(-4, node_groups + 3):
                for lag, stage in stages:
                    if 0 <= s - lag < node_groups:
                        stage(s - lag)

        with nc.Block() as block:
            @block.sync
            def _(sp):
                sp.dma_start(a_bias[:], t["attn_bias"].to_broadcast([P, P])).then_inc(weights_in, DMA)
                sp.dma_start(ln2_col[:], t["ln2_w"].rearrange("o d -> d o"), allow_slow_non_contiguous=True
                             ).then_inc(weights_in, DMA)
                sp.dma_start(fc[:], t["fc_wT"]).then_inc(weights_in, DMA)
                sp.dma_start(proj[:], t["proj_wT"].rearrange("(k p) d -> p k d", p=P)).then_inc(weights_in, DMA)
                for b in range(node_groups):
                    sp.wait_ge(result_ready, b + 1)
                    sp.dma_start(out_dram[b], result[:, b % 2]).then_inc(out_stored[b % 2], DMA)
                for i in range(2):
                    sp.wait_ge(out_stored[i], (node_groups + 1 - i) // 2 * DMA)

            @block.tensor
            def _(pe):
                def turn_sums(b):
                    pe.wait_ge(merged, b + 1)
                    if b:
                        pe.wait_ge(inverted, b)
                    for i in range(QT):
                        at = b * QW + i * P
                        mm = nc.tensor.transpose(w_ps[:, i, :], node_sums[0][:, 1, at:at + P], ident[:])
                    mm.then_inc(weights_turned, 1)
                    if b:
                        pe.wait_ge(mean_made, b)
                    for i in range(QT):
                        at = b * QW + i * P
                        mm = nc.tensor.transpose(a_ps[:, i, :], node_sums[0][:, 0, at:at + P], ident[:])
                    mm.then_inc(row_major, 1)

                def turn_u(b):
                    pe.wait_ge(u_ready, b + 1)
                    for i in range(QT):
                        mm = nc.tensor.transpose(t_ps[:, i * P:(i + 1) * P], u[:, b % 2, i, :], ident[:])
                    mm.then_inc(turned, 1)

                def expand(b):
                    pe.wait_ge(hT_ready, b + 1)
                    for k in range(FC):
                        if b:
                            pe.wait_ge(relu_ready, FC * (b - 1) + k + 1)
                        nc.tensor.matmul(f_ps[k][:], fc[:, k * P:(k + 1) * P], hT[:], start=True,
                                         stop=True).then_inc(fc_ready, 1)

                def contract(b):
                    pe.wait_ge(relu_ready, FC * (b + 1))
                    if b:
                        pe.wait_ge(total_ready, b)
                    for i in range(QT):
                        for k in range(FC):
                            mm = nc.tensor.matmul(y_ps[:, i, :], hidden[:, b % 2, k, i * P:(i + 1) * P], proj[:, k, :],
                                                  start=(k == 0), stop=(k == FC - 1))
                    mm.then_inc(y_ready, 1)

                pe.wait_ge(weights_in, 4 * DMA)
                pe.wait_ge(fc_scaled, 1)
                all_steps([(0, turn_u), (1, contract), (0, expand), (-2, turn_sums)])

            @block.scalar
            def _(act):
                def root(b, k):
                    act.wait_ge(var_ready[k], b + 1)
                    nc.scalar.activation(std[:, k, :], mv[:, k, :, 1], ACT.Sqrt,
                                         bias=eps_col[:, 0:1]).then_inc(std_ready[k], 1)

                def copy_hT(b):
                    act.wait_ge(turned, b + 1)
                    if b:
                        act.wait_ge(fc_ready, FC * b)
                    nc.scalar.copy(hT[:], t_ps[:]).then_inc(hT_ready, 1)

                def relu(b):
                    if b >= 2:
                        act.wait_ge(y_ready, b - 1)
                    for k in range(FC):
                        act.wait_ge(fc_ready, FC * b + k + 1)
                        nc.scalar.activation(hidden[:, b % 2, k, :], f_ps[k][:], ACT.Relu).then_inc(relu_ready, 1)

                all_steps([(0, copy_hT), (-1, lambda b: root(b, 0)), (0, relu), (1, lambda b: root(b, 1))])

            @block.gpsimd
            def _(pool):
                def merge(b):
                    both = [part[:, :, b * QW:(b + 1) * QW] for part in node_sums]
                    nc.gpsimd.tensor_tensor(both[0], both[0], both[1], ALU.add).then_inc(merged, 1)

                def bias(b):
                    if b >= 2:
                        pool.wait_ge(x2_made, b - 1)
                    nc.gpsimd.tensor_tensor(x1_bias[:, b % 2], x1[:, b], a_bias[:].unsqueeze(1).to_broadcast([P, QT, P]),
                                            ALU.add).then_inc(biased, 1)

                def residual(b):
                    pool.wait_ge(x2_made, b + 1)
                    if b >= 2:
                        pool.wait_ge(total_ready, b - 1)
                    nc.gpsimd.tensor_tensor(x12[:, b % 2], x2[:, b % 2], x1[:, b], ALU.add).then_inc(x12_ready, 1)

                pool.wait_ge(weights_in, 4 * DMA)
                all_steps([(-3, merge), (-2, bias), (-1, residual)])

            @block.vector
            def _(dve):
                n = [0]

                def link(ins):
                    n[0] += 1
                    ins.then_inc(step, 1)
                    dve.wait_ge(step, n[0])

                def moments(k, src):
                    for i in range(QT):
                        ins = nc.vector.bn_stats(stats[:, k, i, :], src[:, i, :])
                    link(ins)
                    for i in range(QT):
                        ins = nc.vector.bn_aggr(mv[:, k, i, :], stats[:, k, i, :])
                    ins.then_inc(var_ready[k], 1)

                def scaled(b, k, out, src):
                    dve.wait_ge(std_ready[k], b + 1)
                    link(nc.vector.reciprocal(rstd[:, k, :], std[:, k, :]))
                    for i in range(QT):
                        ins = nc.vector.tensor_scalar(out[:, i, :], src[:, i, :], mv[:, k, i, 0:1], rstd[:, k, i:i + 1],
                                                      ALU.subtract, ALU.mult)
                    return ins

                def invert(b):
                    dve.wait_ge(weights_turned, b + 1)
                    nc.vector.reciprocal(inv8[:, b % 2], w_ps[:, :, ::HC]).then_inc(inverted, 1)

                def residual(b):
                    dve.wait_ge(row_major, b + 1)
                    dve.wait_ge(inverted, b + 1)
                    nc.vector.tensor_tensor(mean[:].rearrange("p i (a b) -> p i a b", b=HC),
                                            a_ps[:].rearrange("p i (a b) -> p i a b", b=HC),
                                            inv8[:, b % 2].unsqueeze(3).to_broadcast([P, QT, HEADS, HC]),
                                            ALU.mult).then_inc(mean_made, 1)
                    dve.wait_ge(biased, b + 1)
                    if b >= 2:
                        dve.wait_ge(x12_ready, b - 1)
                    dve.wait_ge(mean_made, b + 1)
                    nc.vector.tensor_tensor(x2[:, b % 2], mean[:], x1_bias[:, b % 2], ALU.add).then_inc(x2_made, 1)
                    dve.wait_ge(x2_made, b + 1)
                    moments(0, x2[:, b % 2])

                def norm0(b):
                    if b >= 2:
                        dve.wait_ge(turned, b - 1)
                    scaled(b, 0, u[:, b % 2], x2[:, b % 2]).then_inc(u_ready, 1)

                def add_mlp(b):
                    dve.wait_ge(y_ready, b + 1)
                    dve.wait_ge(x12_ready, b + 1)
                    nc.vector.tensor_tensor(total[:, b % 2], y_ps[:], x12[:, b % 2], ALU.add).then_inc(total_ready, 1)
                    dve.wait_ge(total_ready, b + 1)
                    moments(1, total[:, b % 2])

                def norm1(b):
                    if b >= 2:
                        dve.wait_ge(out_stored[b % 2], b // 2 * DMA)
                    scaled(b, 1, result[:, b % 2], total[:, b % 2]).then_inc(result_ready, 1)

                dve.wait_ge(weights_in, 4 * DMA)
                nc.vector.tensor_scalar(fc[:], fc[:], ln2_col[:, 0:1], None, ALU.mult).then_inc(fc_scaled, 1)
                all_steps([(-1, residual), (2, norm1), (-1, norm0), (-2, invert), (1, add_mlp)])
    sums.close()
    attention.close()
    persistent.close()


def kernel(x, src, dst, edge_attr_128, **w):
    import numpy as np
    import concourse.bacc as bacc
    from concourse.bass_utils import run_bass_kernel_spmd

    x, src, dst, attr = (np.asarray(a) for a in (x, src, dst, edge_attr_128))
    w = {k: np.asarray(v) for k, v in w.items()}
    N, D = x.shape
    E = src.shape[0]
    groups, node_groups = sizes(N, E)
    EP, NP, tiles = groups * CHUNKS * P, node_groups * QW, groups * CHUNKS

    def edges(a, fill):
        full = np.full((EP,) + a.shape[1:], fill, a.dtype)
        full[:E] = a
        return full.reshape((CHUNKS, groups, P) + a.shape[1:])

    def row(a):
        return np.ascontiguousarray(a.reshape(1, -1))

    def turned(a):
        return np.ascontiguousarray(a.T)

    srcs, dsts = edges(src, 0), edges(dst, N)
    xp = np.zeros((NP, D), x.dtype)
    xp[:N] = x
    beside = np.full((EP + 2,), -1, dst.dtype)
    beside[1:-1] = dsts.reshape(-1)
    halo = np.lib.stride_tricks.as_strided(beside, (groups, CHUNKS, P + 2), [n * beside.itemsize
                                                                             for n in (P, groups * P, 1)])
    arrays = {
        "x": xp,
        "dst_halo": np.ascontiguousarray(halo),
        "xT": turned(xp),
        "src_cols": np.ascontiguousarray(srcs.transpose(2, 1, 0)).reshape(P, tiles),
        "dst_cols": np.ascontiguousarray(dsts.transpose(2, 1, 0)).reshape(P, tiles),
        "dst_rows": np.ascontiguousarray(dsts.transpose(1, 0, 2)).reshape(tiles, P),
        "first_dst": np.ascontiguousarray(dsts[:, :, 0].T).reshape(1, tiles),
        "dst_nat": beside,
        "attrT": np.ascontiguousarray(edges(attr, 0).transpose(1, 3, 0, 2)).reshape(groups, D, CHUNKS * P),
        "Wqk": w["L0_gnn_Wqk"], "Wv": w["L0_gnn_Wv"], "Wo": w["L0_gnn_Wo"],
        "bqk": row(w["L0_gnn_bqk"]), "bv": row(w["L0_gnn_bv"]), "bo": row(w["L0_gnn_bo"]),
        "gamma": row(w["L0_gnn_gamma"]), "beta": row(w["L0_gnn_beta"]),
        "ln1_w": row(w["L1_gnn_ln1_w"]), "ln2_w": row(w["L1_gnn_ln2_w"]),
        "lin_l_wT": turned(w["L1_gnn_lin_l_w"]), "lin_r_wT": turned(w["L1_gnn_lin_r_w"]),
        "lin_l_b": row(w["L1_gnn_lin_l_b"]), "lin_r_b": row(w["L1_gnn_lin_r_b"]),
        "lin_edge_wT": turned(w["L1_gnn_lin_edge_w"]), "att": w["L1_gnn_att"],
        "attn_bias": row(w["L1_gnn_attn_bias"]),
        "fc_wT": turned(w["L1_gnn_fc_w"]), "proj_wT": turned(w["L1_gnn_proj_w"]),
    }
    nc = bacc.Bacc("TRN2", target_bir_lowering=False, num_devices=1)
    t = {k: nc.dram_tensor("in_" + k, a.shape, mybir.dt.from_np(a.dtype), kind="ExternalInput").ap()
         for k, a in arrays.items()}
    t["out"] = nc.dram_tensor("out_nodes", (NP, D), F32, kind="ExternalOutput").ap()
    build(nc, t, N, E)
    r = run_bass_kernel_spmd(nc, [{"in_" + k: a for k, a in arrays.items()}], core_ids=[0])
    return r.results[0]["out_nodes"][:N]
```

```python
from contextlib import ExitStack

import concourse.bass as bass
from concourse import mybir

F32 = mybir.dt.float32
BF16 = mybir.dt.bfloat16
I32 = mybir.dt.int32
ALU = mybir.AluOpType
ACT = mybir.ActivationFunctionType
AX = mybir.AxisListType

P = 128
HEADS = 8
HC = P // HEADS
CHUNKS = 16
QT = 4
QUADS = CHUNKS // QT
QW = QT * P
BIG = 1.0e38
TINY = 1.0e-30
EPS = 1e-5
DMA = 16


def sizes(nodes, edges):
    groups = -(-edges // (CHUNKS * P))
    node_groups = -(-(nodes + P) // QW)
    return groups, node_groups


def build(nc, t, N, E):
    groups, node_groups = sizes(N, E)
    tiles = groups * CHUNKS
    NP = node_groups * QW
    CW = groups * P

    qkv_tab = nc.dram_tensor("qkv_tab", (NP, 2 * P), F32).ap()
    xl_tab = nc.dram_tensor("xl_tab", (NP, P), F32).ap()
    xr_tab = nc.dram_tensor("xr_tab", (NP, P), F32).ap()
    rel_rows = nc.dram_tensor("rel_rows", (tiles // QT, QW), BF16).ap()
    rel_rows_out = rel_rows.rearrange("q e -> (q e)").rearrange("(p w) -> p w", w=8 * P)
    xl_edges = nc.dram_tensor("xl_edges", (groups, P, CHUNKS * P), F32).ap()
    onehot_edges = nc.dram_tensor("onehot_edges", (groups, P, CHUNKS * P), BF16).ap()
    ends_dram = nc.dram_tensor("ends_dram", (CHUNKS * HEADS, 2), F32).ap()
    enter_dram = nc.dram_tensor("enter_dram", (CHUNKS * HEADS, 2), F32).ap()
    end_sums_dram = nc.dram_tensor("end_sums_dram", (CHUNKS * HEADS, 2), F32).ap()
    end_totals_dram = nc.dram_tensor("end_totals_dram", (CHUNKS * HEADS, 2), F32).ap()

    persistent = ExitStack()

    def keep(name, shape, dt=F32):
        return persistent.enter_context(nc.sbuf_tensor(name, shape, dt))

    iota_row = keep("iota_row", [P, P])
    iota_col = keep("iota_col", [P, 1])
    ident = keep("ident", [P, P])
    ones = keep("ones", [P, P])
    eps_col = keep("eps_col", [P, 1])
    rel_cols = keep("rel_cols", [P, tiles])
    first_row = keep("first_row", [1, tiles], I32)
    src_cols = keep("src_cols", [P, tiles], I32)
    x1 = keep("x1", [P, node_groups, QT, P])

    def window_bases(eng, j, q, count=QT):
        return nc.values_load_multi_w_load_instructions(
            first_row[0:1, bass.ds(j * CHUNKS + q * QT, count)], engines=(eng.engine,), min_val=0, max_val=N,
            skip_runtime_bounds_check_because="destinations are node numbers, or N in the padding")[1]

    def groups_of(eng, total, body):
        body(0, True, False)
        with eng.Fori(1, total - 1) as j:
            body(j, False, False)
        body(total - 1, False, True)

    with ExitStack() as ctx:
        sb = lambda name, shape, dt=F32: ctx.enter_context(nc.sbuf_tensor(name, shape, dt))
        sem = lambda name: ctx.enter_context(nc.semaphore(name))
        iota_i = sb("iota_i", [P, P], I32)
        iota_ci = sb("iota_ci", [P, 1], I32)
        dst_cols = sb("dst_cols", [P, tiles], I32)
        first_all = sb("first_all", [P, tiles], I32)
        dst_rows = sb("dst_rows", [tiles // 8, 8, P], I32)
        rel_out = sb("rel_out", [tiles // 8, 8, P], BF16)
        loaded = sem("indices_loaded")
        iota_made = sem("iota_made")
        const_made = sem("const_made")
        rel_made = sem("rel_made")
        rel_stored = sem("rel_stored")
        with nc.Block() as block:
            @block.sync
            def _(sp):
                sp.dma_start(dst_rows[:], t["dst_rows"].rearrange("(p k) e -> p k e", k=8)).then_inc(loaded, DMA)
                sp.dma_start(dst_cols[:], t["dst_cols"]).then_inc(loaded, DMA)
                sp.dma_start(first_all[:], t["first_dst"].to_broadcast([P, tiles])).then_inc(loaded, DMA)
                sp.dma_start(first_row[:], t["first_dst"]).then_inc(loaded, DMA)
                sp.dma_start(src_cols[:], t["src_cols"]).then_inc(loaded, DMA)
                sp.wait_ge(rel_made, 1)
                sp.dma_start(rel_rows_out, rel_out[:].rearrange("p k e -> p (k e)")).then_inc(rel_stored, DMA)
                sp.wait_ge(rel_stored, DMA)
                sp.wait_ge(loaded, 5 * DMA)

            @block.gpsimd
            def _(pool):
                nc.gpsimd.iota(iota_i[:], [[1, P]], base=0, channel_multiplier=0)
                nc.gpsimd.iota(iota_ci[:], [[1, 1]], base=0, channel_multiplier=1).then_inc(iota_made, 1)

            @block.vector
            def _(dve):
                nc.vector.memset(ones[:], 1.0)
                nc.vector.memset(eps_col[:], EPS)
                dve.wait_ge(iota_made, 1)
                nc.vector.tensor_copy(iota_row[:], iota_i[:])
                nc.vector.tensor_copy(iota_col[:], iota_ci[:]).then_inc(const_made, 1)
                dve.wait_ge(const_made, 1)
                nc.vector.tensor_scalar(ident[:], iota_row[:], iota_col[:, 0:1], None, ALU.is_equal)
                dve.wait_ge(loaded, 5 * DMA)
                nc.vector.tensor_tensor(rel_out[:], dst_rows[:], dst_rows[:, :, 0:1].to_broadcast([tiles // 8, 8, P]),
                                        ALU.subtract).then_inc(rel_made, 1)
                nc.vector.tensor_tensor(rel_cols[:], dst_cols[:], first_all[:], ALU.subtract)

    with ExitStack() as ctx:
        sb = lambda name, shape, dt=F32: ctx.enter_context(nc.sbuf_tensor(name, shape, dt))
        ps = lambda name, shape, dt=F32: ctx.enter_context(nc.psum_tensor(name, shape, dt))
        sem = lambda name: ctx.enter_context(nc.semaphore(name))
        w_qkv = sb("w_qkv", [P, 2 * P])
        b_qkv = sb("b_qkv", [P, 2 * P])
        RING = 4
        xT = sb("xT", [P, RING, QW])
        qkv = sb("qkv", [P, RING, QT, 2 * P])
        qkv_ps = [ps(f"qkv_ps{i}", [P, 2, 2 * P]) for i in range(4)]
        weights_in = sem("l0_weights_in")
        x_in = [sem(f"x_in{i}") for i in range(RING)]
        multiplied = sem("qkv_multiplied")
        biased = sem("qkv_biased")
        stored = [sem(f"qkv_stored{i}") for i in range(RING)]
        qkv_dram = qkv_tab.rearrange("(b i p) d -> b p i d", i=QT, p=P)
        with nc.Block() as block:
            @block.sync
            def _(sp):
                sp.dma_start(w_qkv[:, 0:P], t["Wqk"]).then_inc(weights_in, DMA)
                sp.dma_start(w_qkv[:, P:], t["Wv"]).then_inc(weights_in, DMA)
                sp.dma_start(b_qkv[:, 0:P], t["bqk"].to_broadcast([P, P])).then_inc(weights_in, DMA)
                sp.dma_start(b_qkv[:, P:], t["bv"].to_broadcast([P, P])).then_inc(weights_in, DMA)
                for b in range(node_groups):
                    if b >= RING:
                        sp.wait_ge(multiplied, 2 * (b - RING + 1))
                    sp.dma_start(xT[:, b % RING, :], t["xT"][:, b * QW:(b + 1) * QW]).then_inc(x_in[b % RING], DMA)

            @block.tensor
            def _(pe):
                pe.wait_ge(weights_in, 4 * DMA)
                for b in range(node_groups):
                    pe.wait_ge(x_in[b % RING], (b // RING + 1) * DMA)
                    for k in range(2):
                        if b >= 2:
                            pe.wait_ge(biased, 2 * (b - 2) + k + 1)
                        bank = qkv_ps[b % 2 * 2 + k]
                        for i in range(2):
                            mm = nc.tensor.matmul(bank[:, i, :], xT[:, b % RING, (k * 2 + i) * P:(k * 2 + i + 1) * P],
                                                  w_qkv[:], start=True, stop=True)
                        mm.then_inc(multiplied, 1)

            @block.vector
            def _(dve):
                dve.wait_ge(weights_in, 4 * DMA)
                for b in range(node_groups):
                    if b >= RING:
                        dve.wait_ge(stored[b % RING], b // RING * DMA)
                    for k in range(2):
                        dve.wait_ge(multiplied, 2 * b + k + 1)
                        nc.vector.tensor_tensor(qkv[:, b % RING, 2 * k:2 * k + 2, :], qkv_ps[b % 2 * 2 + k][:],
                                                b_qkv[:].unsqueeze(1).to_broadcast([P, 2, 2 * P]),
                                                ALU.add).then_inc(biased, 1)

            @block.scalar
            def _(act):
                for b in range(node_groups):
                    act.wait_ge(biased, 2 * b + 2)
                    act.dma_start(qkv_dram[b], qkv[:, b % RING]).then_inc(stored[b % RING], DMA)
                for i in range(RING):
                    act.wait_ge(stored[i], (node_groups + RING - 1 - i) // RING * DMA)

    sums = ExitStack()
    node_sums = sums.enter_context(nc.sbuf_tensor("node_sums0", [P, 2, NP], F32))
    with ExitStack() as ctx:
        sb = lambda name, shape, dt=F32: ctx.enter_context(nc.sbuf_tensor(name, shape, dt))
        ps = lambda name, shape, dt=F32: ctx.enter_context(nc.psum_tensor(name, shape, dt))
        sem = lambda name: ctx.enter_context(nc.semaphore(name))
        src_ring = sb("src_ring", [P, CHUNKS], I32)
        rows = sb("rows", [P, CHUNKS, 2 * P])
        window = sb("window", [P, CHUNKS, P])
        rel_bc = sb("rel_bc", [P, QUADS, QW], BF16)
        spread = sb("spread", [P, 2, QW])
        gather1 = sb("gather1", [P, 2, QT, P])
        scores = sb("scores", [P, 2, QT])
        clipped = sb("clipped", [P, 2, QT])
        weight = sb("weight", [P, 2, QT])
        product = sb("product", [P, QT, P])
        q_dst = [ps(f"q_dst{i}", [P, QT, P]) for i in range(2)]
        onehot_ps = [ps(f"onehot_ps{i}", [P, QT, P]) for i in range(2)]
        tile_sums = [ps(f"tile_sums{i}", [P, 2, 2, P]) for i in range(4)]
        quads_asked = sem("quads_asked")
        src_ready = [sem(f"src_ready{i}") for i in range(2)]
        gathered = [sem(f"gathered{q}") for q in range(QUADS)]
        window_in = [sem(f"window_in{q}") for q in range(QUADS)]
        spread_made = sem("spread_made")
        q_spread = sem("q_spread")
        onehot_turned = sem("onehot_turned")
        scored = sem("scored")
        clip_done = sem("clip_done")
        weighted = sem("weighted")
        onehot_made = sem("onehot_made")
        summed = sem("summed")
        added = sem("added")
        cleared = sem("cleared")
        with nc.Block() as block:
            @block.sync
            def _(sp):
                def body(j, first, last):
                    for q in range(QUADS):
                        if not first:
                            sp.wait_ge(q_spread, j * QUADS + q - QUADS + 1)
                        sp.dma_start(rel_bc[:, q, :], rel_rows[bass.ds(j * QUADS + q, 1), :].to_broadcast([P, QW])
                                     ).then_inc(window_in[q], DMA)
                        for i, base in enumerate(window_bases(sp, j, q), q * QT):
                            sp.dma_start(window[:, i, :], qkv_tab[bass.ds(base, P), 0:P]).then_inc(window_in[q], DMA)
                groups_of(sp, groups, body)

            @block.gpsimd
            def _(pool):
                def body(j, first, last):
                    for q in range(QUADS):
                        if q % 2 == 0:
                            pool.wait_ge(src_ready[q // 2], j + 1)
                        if not first:
                            pool.wait_ge(summed, j * QUADS + q - QUADS + 1)
                        pool.sem_inc(quads_asked, 1)
                        for i in range(q * QT, q * QT + QT):
                            nc.gpsimd.indirect_dma_start(
                                out=rows[:, i, :], out_offset=None, in_=qkv_tab,
                                in_offset=bass.IndirectOffsetOnAxis(ap=src_ring[:, i:i + 1], axis=0),
                            ).then_inc(gathered[q], DMA)
                groups_of(pool, groups, body)

            @block.scalar
            def _(act):
                def refill(j, half):
                    a = half * CHUNKS // 2
                    nc.scalar.copy(src_ring[:, a:a + CHUNKS // 2],
                                   src_cols[:, bass.ds(j * CHUNKS + a, CHUNKS // 2)]).then_inc(src_ready[half], 1)

                refill(0, 0)
                refill(0, 1)

                def body(j, first, last):
                    for q in range(QUADS):
                        act.wait_ge(clip_done, j * QUADS + q + 1)
                        nc.scalar.activation(weight[:, q % 2, :], clipped[:, q % 2, :], ACT.Exp).then_inc(weighted, 1)
                        act.wait_ge(weighted, j * QUADS + q + 1)
                        act.wait_ge(onehot_turned, j * QUADS + q + 1)
                        if not (first and q < 2):
                            act.wait_ge(summed, j * QUADS + q - 1)
                        for i in range(QT):
                            o = nc.scalar.mul(gather1[:, q % 2, i, :], onehot_ps[q % 2][:, i, :],
                                              weight[:, q % 2, i:i + 1])
                        o.then_inc(onehot_made, 1)
                        if q == 1 and not last:
                            act.wait_ge(gathered[0], (j + 1) * QT * DMA)
                            act.wait_ge(gathered[1], (j + 1) * QT * DMA)
                            refill(j + 1, 0)
                        if q == 3 and not last:
                            act.wait_ge(gathered[2], (j + 1) * QT * DMA)
                            act.wait_ge(gathered[3], (j + 1) * QT * DMA)
                            refill(j + 1, 1)
                groups_of(act, groups, body)

            @block.tensor
            def _(pe):
                def spread_q(j, q, start=False):
                    pe.wait_ge(spread_made, j * QUADS + q + 1)
                    pe.wait_ge(window_in[q], (j + 1) * (QT + 1) * DMA)
                    if not start:
                        pe.wait_ge(scored, j * QUADS + q - 1)
                    for i in range(QT):
                        mm = nc.tensor.matmul(q_dst[q % 2][:, i, :], spread[:, q % 2, i * P:(i + 1) * P],
                                              window[:, q * QT + i, :], start=True, stop=True)
                    mm.then_inc(q_spread, 1)
                    if not start:
                        pe.wait_ge(onehot_made, j * QUADS + q - 1)
                    for i in range(QT):
                        mm = nc.tensor.transpose(onehot_ps[q % 2][:, i, :], spread[:, q % 2, i * P:(i + 1) * P],
                                                 ident[:])
                    mm.then_inc(onehot_turned, 1)

                def add_up(j, q, start):
                    pe.wait_ge(onehot_made, j * QUADS + q + 1)
                    pe.wait_ge(gathered[q], (j + 1) * QT * DMA)
                    if not start:
                        pe.wait_ge(added, (j * QUADS + q - 1) * QT)
                    for i in range(QT):
                        bank = tile_sums[(q % 2) * 2 + i // 2]
                        nc.tensor.matmul(bank[:, i % 2, 0, :], rows[:, q * QT + i, P:], gather1[:, q % 2, i, :],
                                         start=True, stop=True)
                        mm = nc.tensor.matmul(bank[:, i % 2, 1, :], ones[:], gather1[:, q % 2, i, :],
                                              start=True, stop=True)
                    mm.then_inc(summed, 1)

                spread_q(0, 0, True)

                def body(j, first, last):
                    for q in range(QUADS):
                        if q < QUADS - 1:
                            spread_q(j, q + 1, first and q == 0)
                        elif not last:
                            spread_q(j + 1, 0)
                        add_up(j, q, first and q < 2)
                groups_of(pe, groups, body)

            @block.vector
            def _(dve):
                nc.vector.memset(node_sums[:, 0, :], 0.0)
                nc.vector.memset(node_sums[:, 1, :], TINY).then_inc(cleared, 1)

                def make_spread(j, q, start=False):
                    dve.wait_ge(window_in[q], (j + 1) * (QT + 1) * DMA)
                    if not start:
                        dve.wait_ge(onehot_turned, j * QUADS + q - 1)
                    nc.vector.tensor_scalar(spread[:, q % 2, :], rel_bc[:, q, :], iota_col[:, 0:1], None,
                                            ALU.is_equal).then_inc(spread_made, 1)

                def score(j, q, i):
                    return nc.vector.tensor_tensor_reduce(product[:, i, :], rows[:, q * QT + i, 0:P],
                                                          q_dst[q % 2][:, i, :], float(P) ** -0.5, 0.0,
                                                          ALU.mult, ALU.add, scores[:, q % 2, i:i + 1])

                def add_tile(j, q, i, base, start=False):
                    if not (start and q == 0 and i == 0):
                        dve.wait_ge(added, (j * QUADS + q) * QT + i)
                    span = node_sums[:, :, bass.ds(base, P)]
                    nc.vector.tensor_tensor(span, span, tile_sums[(q % 2) * 2 + i // 2][:, i % 2, :, :],
                                            ALU.add).then_inc(added, 1)

                dve.wait_ge(cleared, 1)
                make_spread(0, 0, True)

                def body(j, first, last):
                    for q in range(QUADS):
                        if q < QUADS - 1:
                            make_spread(j, q + 1, first and q == 0)
                        elif not last:
                            make_spread(j + 1, 0)
                        before = (j, q - 2) if q >= 2 else (j - 1, q + 2)
                        adds = not (first and q < 2)
                        if adds:
                            bases = window_bases(dve, *before)
                            dve.wait_ge(summed, j * QUADS + q - 1)
                        dve.wait_ge(q_spread, j * QUADS + q + 1)
                        dve.wait_ge(gathered[q], (j + 1) * QT * DMA)
                        for i in range(QT):
                            s = score(j, q, i)
                            if i == QT - 1:
                                s.then_inc(scored, 1)
                            if adds:
                                add_tile(*before, i, bases[i], first)
                        dve.wait_ge(scored, j * QUADS + q + 1)
                        nc.vector.tensor_scalar(clipped[:, q % 2, :], scores[:, q % 2, :], 5.0, -5.0, ALU.min,
                                                ALU.max).then_inc(clip_done, 1)
                groups_of(dve, groups, body)
                for q in (QUADS - 2, QUADS - 1):
                    bases = window_bases(dve, groups - 1, q)
                    dve.wait_ge(summed, (groups - 1) * QUADS + q + 1)
                    for i in range(QT):
                        add_tile(groups - 1, q, i, bases[i])
                dve.wait_ge(added, tiles)

    with ExitStack() as ctx:
        sb = lambda name, shape, dt=F32: ctx.enter_context(nc.sbuf_tensor(name, shape, dt))
        ps = lambda name, shape, dt=F32: ctx.enter_context(nc.psum_tensor(name, shape, dt))
        sem = lambda name: ctx.enter_context(nc.semaphore(name))
        w_o = sb("w_o", [P, P])
        w_lr = sb("w_lr", [P, 2 * P])
        b_o = sb("b_o", [P, P])
        b_lr = sb("b_lr", [P, 2 * P])
        gamma = sb("gamma", [P, P])
        beta = sb("beta", [P, P])
        inv_cols = sb("inv_cols", [P, QT, HEADS, HC])
        ln1_col = sb("ln1_col", [P, 1])
        x_nm = sb("x_nm", [P, 2, QT, P])
        inv8 = sb("inv8", [P, 2, QT, HEADS])
        mean_rows = sb("mean_rows", [P, QW])
        x_o = sb("x_o", [P, 2, QT, P])
        h = sb("h", [P, 2, QT, P])
        u = sb("u", [P, 2, QT, P])
        v = sb("v", [P, 2, QT, P])
        stats = sb("stats", [P, 3, QT, 6])
        mv = sb("mv", [P, 3, QT, 2])
        std = sb("std", [P, 3, QT])
        rstd = sb("rstd", [P, 3, QT])
        shift = sb("shift", [P, 3, QT])
        hT = sb("hT", [P, QT, P])
        xlr = sb("xlr", [P, 2, QT, 2 * P])
        w_ps = [ps(f"w_ps{i}", [P, QT, P]) for i in range(2)]
        inv_ps = ps("inv_ps", [P, QW])
        o_ps = ps("o_ps", [P, QT, P])
        t_ps = ps("t_ps", [P, QT, P])
        lr_ps = [ps(f"lr_ps{i}", [P, 2, 2 * P]) for i in range(2)]
        weights_in = sem("l01_weights_in")
        w_scaled = sem("w_lr_scaled")
        x_in = [sem(f"x_nm_in{i}") for i in range(2)]
        step = sem("dve_step")
        weights_turned = sem("weights_turned")
        inverted = sem("inverted")
        inverse_copied = sem("inverse_copied")
        inverse_spread = sem("inverse_spread")
        averaged = sem("averaged")
        projected = sem("projected")
        x_biased = sem("x_biased")
        h_made = sem("h_made")
        var_ready = [sem(f"var_ready{k}") for k in range(3)]
        std_ready = [sem(f"std_ready{k}") for k in range(3)]
        shift_ready = [sem(f"shift_ready{k}") for k in range(3)]
        u_ready = sem("u_ready")
        pool_step = sem("pool_step")
        summed_up = sem("summed_up")
        x1_made = sem("x1_made")
        v_ready = sem("v_ready")
        turned = sem("turned")
        hT_ready = sem("hT_ready")
        lr_ready = sem("lr_ready")
        lr_copied = sem("lr_copied")
        tables_stored = [sem(f"tables_stored{i}") for i in range(2)]
        x_nm_dram = t["x"].rearrange("(b i p) d -> b p i d", i=QT, p=P)
        xl_dram = xl_tab.rearrange("(b i p) d -> b p i d", i=QT, p=P)
        xr_dram = xr_tab.rearrange("(b i p) d -> b p i d", i=QT, p=P)

        def rows_of(w):
            return w[:].unsqueeze(1).to_broadcast([P, QT, P])

        def all_steps(stages):
            for s in range(-2, node_groups + 4):
                for lag, stage in stages:
                    if 0 <= s - lag < node_groups:
                        stage(s - lag)

        with nc.Block() as block:
            @block.sync
            def _(sp):
                for dst, src in ((w_o[:], t["Wo"]), (w_lr[:, 0:P], t["lin_l_wT"]), (w_lr[:, P:], t["lin_r_wT"]),
                                 (b_o[:], t["bo"].to_broadcast([P, P])),
                                 (b_lr[:, 0:P], t["lin_l_b"].to_broadcast([P, P])),
                                 (b_lr[:, P:], t["lin_r_b"].to_broadcast([P, P])),
                                 (gamma[:], t["gamma"].to_broadcast([P, P])), (beta[:], t["beta"].to_broadcast([P, P]))):
                    sp.dma_start(dst, src).then_inc(weights_in, DMA)
                sp.dma_start(ln1_col[:], t["ln1_w"].rearrange("o d -> d o"), allow_slow_non_contiguous=True
                             ).then_inc(weights_in, DMA)
                for b in range(node_groups):
                    if b >= 2:
                        sp.wait_ge(summed_up, b - 1)
                    sp.dma_start(x_nm[:, b % 2], x_nm_dram[b]).then_inc(x_in[b % 2], DMA)

            @block.tensor
            def _(pe):
                def turn_weights(b):
                    if b >= 2:
                        pe.wait_ge(inverted, b - 1)
                    for i in range(QT):
                        at = b * QW + i * P
                        mm = nc.tensor.transpose(w_ps[b % 2][:, i, :], node_sums[:, 1, at:at + P], ident[:])
                    mm.then_inc(weights_turned, 1)

                def spread_inverse(b):
                    pe.wait_ge(inverse_copied, b + 1)
                    if b:
                        pe.wait_ge(averaged, b)
                    for i in range(QT):
                        mm = nc.tensor.transpose(inv_ps[:, i * P:(i + 1) * P],
                                                 inv_cols[:, i].rearrange("p a b -> p (a b)"), ident[:])
                    mm.then_inc(inverse_spread, 1)

                def project(b):
                    pe.wait_ge(averaged, b + 1)
                    if b:
                        pe.wait_ge(h_made, b)
                    for i in range(QT):
                        mm = nc.tensor.matmul(o_ps[:, i, :], mean_rows[:, i * P:(i + 1) * P], w_o[:], start=True,
                                              stop=True)
                    mm.then_inc(projected, 1)

                def turn_v(b):
                    pe.wait_ge(v_ready, b + 1)
                    for i in range(QT):
                        mm = nc.tensor.transpose(t_ps[:, i, :], v[:, b % 2, i, :], ident[:])
                    mm.then_inc(turned, 1)

                def tables(b):
                    pe.wait_ge(hT_ready, b + 1)
                    if b:
                        pe.wait_ge(lr_copied, b)
                    for i in range(QT):
                        mm = nc.tensor.matmul(lr_ps[i // 2][:, i % 2, :], hT[:, i, :], w_lr[:], start=True, stop=True)
                    mm.then_inc(lr_ready, 1)

                pe.wait_ge(weights_in, 9 * DMA)
                pe.wait_ge(w_scaled, 1)
                all_steps([(0, project), (3, turn_v), (-1, spread_inverse), (-2, turn_weights), (3, tables)])

            @block.vector
            def _(dve):
                n = [0]

                def link(ins):
                    n[0] += 1
                    ins.then_inc(step, 1)
                    dve.wait_ge(step, n[0])

                def moments(k, src):
                    for i in range(QT):
                        ins = nc.vector.bn_stats(stats[:, k, i, :], src[:, i, :])
                    link(ins)
                    for i in range(QT):
                        ins = nc.vector.bn_aggr(mv[:, k, i, :], stats[:, k, i, :])
                    ins.then_inc(var_ready[k], 1)

                def shift_of(b, k, used):
                    dve.wait_ge(std_ready[k], b + 1)
                    if b:
                        dve.wait_ge(used, b)
                    link(nc.vector.reciprocal(rstd[:, k, :], std[:, k, :]))
                    nc.vector.scalar_tensor_tensor(shift[:, k, :], mv[:, k, :, 0], -1.0, rstd[:, k, :], ALU.mult,
                                                   ALU.mult).then_inc(shift_ready[k], 1)

                def invert(b):
                    dve.wait_ge(weights_turned, b + 1)
                    if b >= 2:
                        dve.wait_ge(inverse_copied, b - 1)
                    nc.vector.reciprocal(inv8[:, b % 2], w_ps[b % 2][:, :, ::HC]).then_inc(inverted, 1)

                def average(b):
                    dve.wait_ge(inverse_spread, b + 1)
                    if b:
                        dve.wait_ge(projected, b)
                    nc.vector.tensor_tensor(mean_rows[:], node_sums[:, 0, b * QW:(b + 1) * QW], inv_ps[:],
                                            ALU.mult).then_inc(averaged, 1)

                def residual(b):
                    dve.wait_ge(x_biased, b + 1)
                    dve.wait_ge(projected, b + 1)
                    if b >= 2:
                        dve.wait_ge(x1_made, b - 1)
                    nc.vector.tensor_tensor(h[:, b % 2], o_ps[:], x_o[:, b % 2], ALU.add).then_inc(h_made, 1)
                    dve.wait_ge(h_made, b + 1)
                    moments(0, h[:, b % 2])

                def moments1(b):
                    dve.wait_ge(summed_up, b + 1)
                    moments(1, h[:, b % 2])

                def add_bias(b):
                    dve.wait_ge(lr_ready, b + 1)
                    if b >= 2:
                        dve.wait_ge(tables_stored[b % 2], 2 * (b // 2) * DMA)
                    bias = b_lr[:].unsqueeze(1).to_broadcast([P, 2, 2 * P])
                    nc.vector.tensor_tensor(xlr[:, b % 2, 0:2, :], lr_ps[0][:], bias, ALU.add)
                    nc.vector.tensor_tensor(xlr[:, b % 2, 2:4, :], lr_ps[1][:], bias, ALU.add).then_inc(lr_copied, 1)

                def norm1(b):
                    dve.wait_ge(std_ready[1], b + 1)
                    link(nc.vector.reciprocal(rstd[:, 1, :], std[:, 1, :]))
                    for i in range(QT):
                        ins = nc.vector.tensor_scalar(x1[:, b, i, :], h[:, b % 2, i, :], mv[:, 1, i, 0:1],
                                                      rstd[:, 1, i:i + 1], ALU.subtract, ALU.mult)
                    ins.then_inc(x1_made, 1)

                def moments2(b):
                    dve.wait_ge(x1_made, b + 1)
                    moments(2, x1[:, b])

                dve.wait_ge(weights_in, 9 * DMA)
                nc.vector.tensor_scalar(w_lr[:], w_lr[:], ln1_col[:, 0:1], None, ALU.mult).then_inc(w_scaled, 1)
                all_steps([(0, average), (1, residual), (3, lambda b: shift_of(b, 2, v_ready)), (-1, invert),
                           (2, moments1), (1, lambda b: shift_of(b, 0, u_ready)), (2, norm1), (4, add_bias), (2, moments2)])

            @block.gpsimd
            def _(pool):
                n = [0]

                def link(ins):
                    n[0] += 1
                    ins.then_inc(pool_step, 1)
                    pool.wait_ge(pool_step, n[0])

                def bias(b):
                    x = x_nm[:, b % 2]
                    pool.wait_ge(x_in[b % 2], (b // 2 + 1) * DMA)
                    if b >= 2:
                        pool.wait_ge(h_made, b - 1)
                    nc.gpsimd.tensor_tensor(x_o[:, b % 2], x, rows_of(b_o), ALU.add).then_inc(x_biased, 1)
                    link(nc.gpsimd.tensor_tensor(x, x, rows_of(beta), ALU.add))

                def affine(b):
                    y, x = u[:, b % 2], x_nm[:, b % 2]
                    pool.wait_ge(u_ready, b + 1)
                    link(nc.gpsimd.tensor_tensor(y, y, rows_of(gamma), ALU.mult))
                    nc.gpsimd.tensor_tensor(h[:, b % 2], y, x, ALU.add).then_inc(summed_up, 1)

                pool.wait_ge(weights_in, 9 * DMA)
                all_steps([(0, bias), (1, affine)])

            @block.scalar
            def _(act):
                def root(b, k):
                    act.wait_ge(var_ready[k], b + 1)
                    nc.scalar.activation(std[:, k, :], mv[:, k, :, 1], ACT.Sqrt,
                                         bias=eps_col[:, 0:1]).then_inc(std_ready[k], 1)

                def norm(b, k, out, rows, done):
                    act.wait_ge(shift_ready[k], b + 1)
                    for i in range(QT):
                        ins = nc.scalar.activation(out[:, i, :], rows[:, i, :], ACT.Identity,
                                                   bias=shift[:, k, i:i + 1], scale=rstd[:, k, i:i + 1])
                    ins.then_inc(done, 1)

                def copy_inverse(b):
                    act.wait_ge(inverted, b + 1)
                    if b:
                        act.wait_ge(inverse_spread, b)
                    nc.scalar.copy(inv_cols[:], inv8[:, b % 2].unsqueeze(3).to_broadcast([P, QT, HEADS, HC])
                                   ).then_inc(inverse_copied, 1)

                def norm0(b):
                    if b >= 2:
                        act.wait_ge(summed_up, b - 1)
                    norm(b, 0, u[:, b % 2], h[:, b % 2], u_ready)

                def norm2(b):
                    if b >= 2:
                        act.wait_ge(turned, b - 1)
                    norm(b, 2, v[:, b % 2], x1[:, b], v_ready)

                def copy_hT(b):
                    act.wait_ge(turned, b + 1)
                    if b:
                        act.wait_ge(lr_ready, b)
                    nc.scalar.copy(hT[:], t_ps[:]).then_inc(hT_ready, 1)

                def store_tables(b):
                    act.wait_ge(lr_copied, b + 1)
                    act.dma_start(xl_dram[b], xlr[:, b % 2, :, 0:P]).then_inc(tables_stored[b % 2], DMA)
                    act.dma_start(xr_dram[b], xlr[:, b % 2, :, P:]).then_inc(tables_stored[b % 2], DMA)

                all_steps([(1, lambda b: root(b, 0)), (3, norm2), (-1, copy_inverse), (2, lambda b: root(b, 1)), (1, norm0),
                           (3, copy_hT), (4, store_tables), (2, lambda b: root(b, 2))])
                for i in range(2):
                    act.wait_ge(tables_stored[i], 2 * ((node_groups + 1 - i) // 2) * DMA)
    sums.close()

    attention = ExitStack()
    logits = attention.enter_context(nc.sbuf_tensor("logits", [P, CW], F32))
    largest = attention.enter_context(nc.sbuf_tensor("largest", [P, CW], F32))
    fences = ExitStack()

    def fence(name):
        return fences.enter_context(nc.sbuf_tensor(name, [P, CW], BF16))

    first_fence = fence("first_fence")
    last_fence = fence("last_fence")
    inner = fence("inner")
    head_fence = fence("head_fence")
    tail_fence = fence("tail_fence")
    head_max = fences.enter_context(nc.sbuf_tensor("head_max", [P, groups], F32))
    with ExitStack() as ctx:
        sb = lambda name, shape, dt=F32: ctx.enter_context(nc.sbuf_tensor(name, shape, dt))
        ps = lambda name, shape, dt=F32: ctx.enter_context(nc.psum_tensor(name, shape, dt))
        sem = lambda name: ctx.enter_context(nc.semaphore(name))
        w_e = sb("w_e", [P, P])
        att_pad = sb("att_pad", [P, CHUNKS, CHUNKS, HEADS])
        src_ring = sb("src_ring1", [P, CHUNKS], I32)
        rows = sb("rows1", [P, CHUNKS, P])
        window = sb("window1", [P, CHUNKS, P])
        attr = sb("attr", [P, QUADS, QW])
        rel_bc = sb("rel_bc1", [P, QUADS, QW], BF16)
        spread = sb("spread1", [P, 2, QW])
        z_low = sb("z_low", [P, 2, QW])
        z_act = sb("z_act", [P, 2, QW])
        z_ps = [ps(f"z_ps{i}", [P, QW]) for i in range(2)]
        lg_ps = ps("lg_ps", [P, P])
        weights_in = sem("l1_weights_in")
        pad_cleared = sem("pad_cleared")
        att_in = sem("att_in")
        quads_asked = sem("quads_asked1")
        src_ready = [sem(f"src_ready1_{i}") for i in range(2)]
        gathered = [sem(f"gathered1_{q}") for q in range(QUADS)]
        window_in = [sem(f"window_in1_{q}") for q in range(QUADS)]
        attr_in = [sem(f"attr_in{q}") for q in range(QUADS)]
        kept = [sem(f"xl_kept{q}") for q in range(QUADS)]
        spread_made = sem("spread_made1")
        z_ready = sem("z_ready")
        low_ready = sem("low_ready")
        z_act_ready = sem("z_act_ready")
        lg_ready = sem("lg_ready")
        lg_quads = sem("lg_quads")
        lg_copied = sem("lg_copied")
        halo = sb("halo", [P, P + 2], I32)
        chunk_ends = sb("chunk_ends", [P, 2], I32)
        chunk_ends_f = sb("chunk_ends_f", [P, 2])
        flags = sb("flags", [P, 2, P])
        head_now = sb("head_now", [P, P])
        onehot = sb("onehot_bf", [P, 2, QT, P], BF16)
        halo_in = sem("halo_in")
        chunk_ends_in = sem("chunk_ends_in")
        chunk_ends_made = sem("chunk_ends_made")
        flags_made = sem("flags_made")
        fences_made = sem("fences_made")
        scanned = sem("scanned")
        onehot_made = sem("onehot_bf_made")
        onehot_kept = [sem(f"onehot_kept{i}") for i in range(2)]
        with nc.Block() as block:
            @block.sync
            def _(sp):
                sp.dma_start(w_e[:], t["lin_edge_wT"]).then_inc(weights_in, DMA)
                for k, off in enumerate((1, CW)):
                    sp.dma_start(chunk_ends[:, k:k + 1], bass.AP(t["dst_nat"].tensor, off, [[CW, CHUNKS], [0, HEADS], [1, 1]]),
                                 allow_slow_non_contiguous=True).then_inc(chunk_ends_in, DMA)
                sp.wait_ge(pad_cleared, 1)
                for hd in range(HEADS):
                    diag = bass.AP(att_pad[:].tensor, att_pad[hd * HC:(hd + 1) * HC, 0, 0, hd:hd + 1].offset,
                                   [list(att_pad[hd * HC:(hd + 1) * HC].ap[0]), [CHUNKS * HEADS + HEADS, CHUNKS], [1, 1]])
                    sp.dma_start(diag, t["att"][hd].rearrange("(c o) -> c o", o=1).unsqueeze(2).to_broadcast([HC, CHUNKS, 1]),
                                 allow_slow_non_contiguous=True).then_inc(att_in, DMA)

                def body(j, first, last):
                    for q in range(QUADS):
                        if not first:
                            sp.wait_ge(z_ready, j * QUADS + q - QUADS + 1)
                        sp.dma_start(rel_bc[:, q, :], rel_rows[bass.ds(j * QUADS + q, 1), :].to_broadcast([P, QW])
                                     ).then_inc(window_in[q], DMA)
                        for i, base in enumerate(window_bases(sp, j, q), q * QT):
                            sp.dma_start(window[:, i, :], xr_tab[bass.ds(base, P), :]).then_inc(window_in[q], DMA)
                        if q == 1:
                            if not first:
                                sp.wait_ge(fences_made, 5 * j)
                            sp.dma_start(halo[:], t["dst_halo"][bass.ds(j, 1)].rearrange("a c e -> (a c) e").unsqueeze(1)
                                         .to_broadcast([CHUNKS, HEADS, P + 2])).then_inc(halo_in, DMA)
                groups_of(sp, groups, body)

            @block.gpsimd
            def _(pool):
                def body(j, first, last):
                    for q in range(QUADS):
                        if q % 2 == 0:
                            pool.wait_ge(src_ready[q // 2], j + 1)
                        if not first:
                            pool.wait_ge(z_ready, j * QUADS + q - QUADS + 1)
                            pool.wait_ge(kept[q], j * DMA)
                        pool.sem_inc(quads_asked, 1)
                        for i in range(q * QT, q * QT + QT):
                            nc.gpsimd.indirect_dma_start(
                                out=rows[:, i, :], out_offset=None, in_=xl_tab,
                                in_offset=bass.IndirectOffsetOnAxis(ap=src_ring[:, i:i + 1], axis=0),
                            ).then_inc(gathered[q], DMA)
                groups_of(pool, groups, body)

            @block.scalar
            def _(act):
                def refill(j, half):
                    a = half * CHUNKS // 2
                    nc.scalar.copy(src_ring[:, a:a + CHUNKS // 2],
                                   src_cols[:, bass.ds(j * CHUNKS + a, CHUNKS // 2)]).then_inc(src_ready[half], 1)

                def load_attr(j, q):
                    act.dma_start(attr[:, q, :], t["attrT"][bass.ds(j, 1), :, q * QW:(q + 1) * QW].rearrange("a p e -> (a p) e")
                                  ).then_inc(attr_in[q], DMA)

                refill(0, 0)
                refill(0, 1)
                for q in range(QUADS):
                    load_attr(0, q)

                def body(j, first, last):
                    for q in range(QUADS):
                        act.wait_ge(z_ready, j * QUADS + q + 1)
                        if not (first and q < 2):
                            act.wait_ge(z_act_ready, j * QUADS + q - 1)
                        nc.scalar.mul(z_low[:, q % 2, :], z_ps[q % 2][:], 0.2).then_inc(low_ready, 1)
                        act.wait_ge(gathered[q], (j + 1) * QT * DMA)
                        act.dma_start(xl_edges[bass.ds(j, 1), :, q * QW:(q + 1) * QW].rearrange("a p e -> (a p) e"),
                                      rows[:, q * QT:(q + 1) * QT, :].rearrange("p i d -> p (i d)")).then_inc(kept[q], DMA)
                        act.wait_ge(onehot_made, j * QUADS + q + 1)
                        act.dma_start(onehot_edges[bass.ds(j, 1), :, q * QW:(q + 1) * QW].rearrange("a p e -> (a p) e"),
                                      onehot[:, q % 2].rearrange("p i d -> p (i d)")).then_inc(onehot_kept[q % 2], DMA)
                        if not last:
                            load_attr(j + 1, q)
                            if q == 1:
                                refill(j + 1, 0)
                            if q == 3:
                                refill(j + 1, 1)
                groups_of(act, groups, body)
                for q in range(QUADS):
                    act.wait_ge(kept[q], groups * DMA)
                for i in range(2):
                    act.wait_ge(onehot_kept[i], 2 * groups * DMA)

            @block.tensor
            def _(pe):
                def make_z(j, q, start=False):
                    pe.wait_ge(attr_in[q], (j + 1) * DMA)
                    if not start:
                        pe.wait_ge(z_act_ready, j * QUADS + q - 1)
                        pe.wait_ge(low_ready, j * QUADS + q - 1)
                    z = z_ps[q % 2]
                    nc.tensor.matmul(z[:], w_e[:], attr[:, q, :], start=True, stop=False)
                    pe.wait_ge(spread_made, j * QUADS + q + 1)
                    pe.wait_ge(window_in[q], (j + 1) * (QT + 1) * DMA)
                    for i in range(QT):
                        nc.tensor.matmul(z[:, i * P:(i + 1) * P], window[:, q * QT + i, :],
                                         spread[:, q % 2, i * P:(i + 1) * P], start=False, stop=False)
                    pe.wait_ge(gathered[q], (j + 1) * QT * DMA)
                    for i in range(QT):
                        mm = nc.tensor.matmul(z[:, i * P:(i + 1) * P], rows[:, q * QT + i, :], ident[:],
                                              start=False, stop=(i == QT - 1))
                    mm.then_inc(z_ready, 1)

                def make_logits(j, q, first):
                    pe.wait_ge(z_act_ready, j * QUADS + q + 1)
                    if q == 0 and not first:
                        pe.wait_ge(lg_copied, j)
                    for i in range(QT):
                        c = q * QT + i
                        mm = nc.tensor.matmul(lg_ps[:], att_pad[:, c].rearrange("p a b -> p (a b)"),
                                              z_act[:, q % 2, i * P:(i + 1) * P], start=(c == 0),
                                              stop=(c == CHUNKS - 1))
                    mm.then_inc(lg_quads, 1)

                pe.wait_ge(weights_in, DMA)
                pe.wait_ge(att_in, HEADS * DMA)
                make_z(0, 0, True)

                def body(j, first, last):
                    for q in range(QUADS):
                        if q < QUADS - 1:
                            make_z(j, q + 1, first and q == 0)
                        elif not last:
                            make_z(j + 1, 0)
                        make_logits(j, q, first)
                groups_of(pe, groups, body)

            @block.vector
            def _(dve):
                nc.vector.memset(att_pad[:], 0.0).then_inc(pad_cleared, 1)

                def make_spread(j, q, start=False):
                    dve.wait_ge(window_in[q], (j + 1) * (QT + 1) * DMA)
                    if not start:
                        dve.wait_ge(z_ready, j * QUADS + q - 1)
                    nc.vector.tensor_scalar(spread[:, q % 2, :], rel_bc[:, q, :], iota_col[:, 0:1], None,
                                            ALU.is_equal).then_inc(spread_made, 1)

                def make_onehots(j, q, start):
                    if not start:
                        dve.wait_ge(onehot_kept[q % 2], (j * 2 + q // 2) * DMA)
                    for i in range(QT):
                        o = nc.vector.tensor_scalar(onehot[:, q % 2, i, :], iota_row[:],
                                                    rel_cols[:, bass.ds(j * CHUNKS + q * QT + i, 1)], None,
                                                    ALU.is_equal)
                    o.then_inc(onehot_made, 1)

                def fence_off(j, first):
                    at = bass.ds(j * P, P)
                    here = halo[:, 1:P + 1]
                    dve.wait_ge(halo_in, (j + 1) * DMA)
                    if not first:
                        dve.wait_ge(fences_made, 5 * j)
                    nc.vector.tensor_tensor(flags[:, 0, :], here, halo[:, 0:P], ALU.not_equal)
                    nc.vector.tensor_tensor(flags[:, 1, :], here, halo[:, 2:P + 2], ALU.not_equal).then_inc(flags_made, 1)
                    nc.vector.tensor_tensor(inner[:, at], here, halo[:, 2:P + 2], ALU.is_equal).then_inc(fences_made, 1)
                    for k, out in enumerate((head_fence, tail_fence)):
                        nc.vector.tensor_scalar(out[:, at], here, chunk_ends_f[:, k:k + 1], -BIG, ALU.not_equal,
                                                ALU.mult).then_inc(fences_made, 1)
                    dve.wait_ge(flags_made, j + 1)
                    for k, out in enumerate((first_fence, last_fence)):
                        nc.vector.tensor_scalar(out[:, at], flags[:, k, :], -BIG, None, ALU.mult).then_inc(fences_made, 1)

                def scan_group(j, first):
                    at = bass.ds(j * P, P)
                    dve.wait_ge(lg_quads, j * QUADS + QUADS)
                    nc.vector.tensor_copy(logits[:, at], lg_ps[:]).then_inc(lg_copied, 1)
                    dve.wait_ge(lg_copied, j + 1)
                    dve.wait_ge(fences_made, 5 * j + 5)
                    before = -BIG if first else largest[:, bass.ds(j * P - 1, 1)]
                    nc.vector.tensor_tensor_scan(largest[:, at], first_fence[:, at], logits[:, at], before, ALU.add,
                                                 ALU.max).then_inc(scanned, 1)
                    dve.wait_ge(scanned, 3 * j + 1)
                    nc.vector.tensor_tensor(head_now[:], largest[:, at], head_fence[:, at], ALU.add).then_inc(scanned, 1)
                    dve.wait_ge(scanned, 3 * j + 2)
                    nc.vector.tensor_reduce(head_max[:, bass.ds(j, 1)], head_now[:], AX.X, ALU.max).then_inc(scanned, 1)

                dve.wait_ge(chunk_ends_in, 2 * DMA)
                nc.vector.tensor_copy(chunk_ends_f[:], chunk_ends[:]).then_inc(chunk_ends_made, 1)
                dve.wait_ge(chunk_ends_made, 1)
                make_spread(0, 0, True)

                def body(j, first, last):
                    for q in range(QUADS):
                        if q < QUADS - 1:
                            make_spread(j, q + 1, first and q == 0)
                        elif not last:
                            make_spread(j + 1, 0)
                        make_onehots(j, q, first and q < 2)
                        if q == 2:
                            fence_off(j, first)
                        dve.wait_ge(low_ready, j * QUADS + q + 1)
                        if not (first and q < 2):
                            dve.wait_ge(lg_quads, j * QUADS + q - 1)
                        nc.vector.tensor_tensor(z_act[:, q % 2, :], z_ps[q % 2][:], z_low[:, q % 2, :],
                                                ALU.max).then_inc(z_act_ready, 1)
                    scan_group(j, first)
                groups_of(dve, groups, body)
                dve.wait_ge(scanned, 3 * groups)

    with ExitStack() as ctx:
        sb = lambda name, shape, dt=F32: ctx.enter_context(nc.sbuf_tensor(name, shape, dt))
        sem = lambda name: ctx.enter_context(nc.semaphore(name))
        ends = sb("ends", [P, 2])
        turned = sb("turned", [HEADS, 2, CHUNKS])
        enter = sb("enter", [P, 2])
        entering = sb("entering", [HEADS, 2, CHUNKS])
        scanned_ends = sb("scanned_ends", [HEADS, 2, CHUNKS])
        edge_dst = sb("edge_dst", [HEADS, 4, CHUNKS], I32)
        bars = sb("bars", [HEADS, 4, CHUNKS])
        right = sb("right", [HEADS, 2, CHUNKS])
        end_sums = sb("end_sums", [P, 2])
        turned_sums = sb("turned_sums", [HEADS, 2, CHUNKS])
        unbroken = sb("unbroken", [HEADS, 4, CHUNKS])
        right_sums = sb("right_sums", [HEADS, 2, CHUNKS])
        scanned_sums = sb("scanned_sums", [HEADS, CHUNKS])
        more = sb("more", [HEADS, 2, CHUNKS])
        through = sb("through", [HEADS, 2, CHUNKS])
        totals = sb("totals", [HEADS, 2, CHUNKS])
        end_totals = sb("end_totals", [P, 2])
        dst_in = sem("edge_dst_in")
        shifted = sem("shifted")
        powered = sem("powered")
        summed = sem("powers_summed")
        totals_ready = sem("end_totals_ready")
        step = sem("ends_step")
        ends_ready = sem("ends_ready")
        ends_out = sem("ends_out")
        ends_turned = sem("ends_turned")
        entering_ready = sem("entering_ready")
        enter_out = sem("enter_out")
        enter_in = sem("enter_in")
        nat = t["dst_nat"].tensor
        BEFORE, FIRST, LAST, AFTER = range(4)
        START, INSIDE, WHOLE, END = range(4)
        PIECES = 4
        piece = CW // PIECES
        with nc.Block() as block:
            @block.sync
            def _(sp):
                for k, off in ((BEFORE, 0), (FIRST, 1), (LAST, CW), (AFTER, CW + 1)):
                    sp.dma_start(edge_dst[:, k, :], bass.AP(nat, off, [[0, HEADS], [CW, CHUNKS], [1, 1]]),
                                 allow_slow_non_contiguous=True).then_inc(dst_in, DMA)
                sp.wait_ge(ends_ready, 1)
                sp.dma_start(ends_dram, ends[:]).then_inc(ends_out, DMA)
                sp.wait_ge(ends_out, DMA)
                sp.dma_start(turned[:], ends_dram.rearrange("(c h) m -> h m c", h=HEADS),
                             allow_slow_non_contiguous=True).then_inc(ends_turned, DMA)
                sp.wait_ge(entering_ready, 2)
                sp.dma_start(enter_dram.rearrange("(c h) m -> h m c", h=HEADS), entering[:],
                             allow_slow_non_contiguous=True).then_inc(enter_out, DMA)
                sp.wait_ge(enter_out, DMA)
                sp.dma_start(enter[:], enter_dram).then_inc(enter_in, DMA)
                sp.wait_ge(summed, 1)
                sp.dma_start(end_sums_dram, end_sums[:]).then_inc(ends_out, DMA)
                sp.wait_ge(ends_out, 2 * DMA)
                sp.dma_start(turned_sums[:], end_sums_dram.rearrange("(c h) m -> h m c", h=HEADS),
                             allow_slow_non_contiguous=True).then_inc(ends_turned, DMA)
                sp.wait_ge(totals_ready, 1)
                sp.dma_start(end_totals_dram.rearrange("(c h) m -> h m c", h=HEADS), totals[:],
                             allow_slow_non_contiguous=True).then_inc(enter_out, DMA)
                sp.wait_ge(enter_out, 2 * DMA)
                sp.dma_start(end_totals[:], end_totals_dram).then_inc(enter_in, DMA)

            @block.scalar
            def _(act):
                for n, k in enumerate(reversed(range(PIECES))):
                    act.wait_ge(shifted, n + 1)
                    part = logits[:, k * piece:(k + 1) * piece]
                    nc.scalar.activation(part, part, ACT.Exp).then_inc(powered, 1)

            @block.vector
            def _(dve):
                n = [0]

                def link(ins):
                    n[0] += 1
                    ins.then_inc(step, 1)
                    dve.wait_ge(step, n[0])

                nc.vector.tensor_copy(ends[:, 0:1], largest[:, CW - 1:CW])
                nc.vector.tensor_reduce(ends[:, 1:2], head_max[:], AX.X, ALU.max).then_inc(ends_ready, 1)
                dve.wait_ge(dst_in, 4 * DMA)
                for k, a, b in ((START, BEFORE, FIRST), (INSIDE, BEFORE, LAST), (WHOLE, FIRST, LAST), (END, LAST, AFTER)):
                    ins = nc.vector.tensor_tensor(bars[:, k, :], edge_dst[:, a, :], edge_dst[:, b, :], ALU.not_equal)
                link(ins)
                link(nc.vector.tensor_scalar(bars[:], bars[:], -BIG, None, ALU.mult))
                nc.vector.memset(entering[:], -BIG)
                C1 = CHUNKS - 1
                nc.vector.tensor_tensor(right[:, 0, 0:C1], bars[:, END, 0:C1], bars[:, WHOLE, 1:], ALU.add)
                dve.wait_ge(ends_turned, DMA)
                link(nc.vector.tensor_tensor(right[:, 1, 0:C1], bars[:, END, 0:C1], turned[:, 1, 1:], ALU.add))
                nc.vector.tensor_tensor_scan(scanned_ends[:, 0, :], bars[:, INSIDE, :], turned[:, 0, :], -BIG,
                                             ALU.add, ALU.max)
                nc.vector.tensor_tensor_scan(entering[:, 1, C1 - 1::-1], right[:, 0, C1 - 1::-1],
                                             right[:, 1, C1 - 1::-1], -BIG, ALU.add,
                                             ALU.max).then_inc(entering_ready, 1)
                dve.wait_ge(entering_ready, 1)
                nc.vector.tensor_tensor(entering[:, 0, 1:], scanned_ends[:, 0, 0:C1], bars[:, START, 1:],
                                        ALU.add).then_inc(entering_ready, 1)
                dve.wait_ge(enter_in, DMA)
                link(nc.vector.scalar_tensor_tensor(largest[:], head_fence[:], enter[:, 0:1], largest[:], ALU.add,
                                                    ALU.max))
                link(nc.vector.tensor_tensor_scan(largest[:, ::-1], last_fence[:, ::-1], largest[:, ::-1],
                                                  enter[:, 1:2], ALU.add, ALU.max))

                def shift(k):
                    part = slice(k * piece, (k + 1) * piece)
                    nc.vector.tensor_tensor(logits[:, part], logits[:, part], largest[:, part],
                                            ALU.subtract).then_inc(shifted, 1)

                def sum_up(k):
                    dve.wait_ge(powered, PIECES - k)
                    a, z = k * piece, (k + 1) * piece
                    back = slice(z - 1, a - 1 if a else None, -1)
                    after = largest[:, z:z + 1] if z < CW else 0.0
                    link(nc.vector.tensor_tensor_scan(largest[:, back], inner[:, back], logits[:, back], after,
                                                      ALU.mult, ALU.add))

                shift(PIECES - 1)
                for k in reversed(range(PIECES)):
                    if k:
                        shift(k - 1)
                    if k == 0:
                        dve.wait_ge(shifted, PIECES)
                    sum_up(k)
                link(nc.vector.tensor_tensor_scan(largest[:], first_fence[:], largest[:], -BIG, ALU.add, ALU.max))
                nc.vector.tensor_copy(end_sums[:, 0:1], largest[:, CW - 1:CW])
                nc.vector.tensor_copy(end_sums[:, 1:2], largest[:, 0:1]).then_inc(summed, 1)
                nc.vector.memset(more[:], 0.0)
                link(nc.vector.tensor_scalar(unbroken[:], bars[:], 0.0, None, ALU.is_equal))
                nc.vector.tensor_tensor(right_sums[:, 0, 0:C1], unbroken[:, END, 0:C1], unbroken[:, WHOLE, 1:], ALU.mult)
                dve.wait_ge(ends_turned, 2 * DMA)
                link(nc.vector.tensor_tensor(right_sums[:, 1, 0:C1], unbroken[:, END, 0:C1], turned_sums[:, 1, 1:],
                                             ALU.mult))
                nc.vector.tensor_tensor_scan(scanned_sums[:], unbroken[:, INSIDE, :], turned_sums[:, 0, :], 0.0,
                                             ALU.mult, ALU.add)
                link(nc.vector.tensor_tensor_scan(more[:, 1, C1 - 1::-1], right_sums[:, 0, C1 - 1::-1],
                                                  right_sums[:, 1, C1 - 1::-1], 0.0, ALU.mult, ALU.add))
                link(nc.vector.tensor_tensor(more[:, 0, 1:], scanned_sums[:, 0:C1], unbroken[:, START, 1:], ALU.mult))
                link(nc.vector.tensor_tensor(through[:], more[:], unbroken[:, WHOLE:WHOLE + 1, :].to_broadcast([HEADS, 2, CHUNKS]),
                                             ALU.mult))
                for k in range(2):
                    ins = nc.vector.tensor_tensor(totals[:, k, :], turned_sums[:, k, :], more[:, 1 - k, :], ALU.add)
                link(ins)
                nc.vector.tensor_tensor(totals[:], totals[:], through[:], ALU.add).then_inc(totals_ready, 1)
                dve.wait_ge(enter_in, 2 * DMA)
                for k, fenced in enumerate((tail_fence, head_fence)):
                    link(nc.vector.scalar_tensor_tensor(largest[:], fenced[:], end_totals[:, k:k + 1], largest[:],
                                                        ALU.add, ALU.max))
    fences.close()

    sums = ExitStack()
    node_sums = [sums.enter_context(nc.sbuf_tensor(f"node_sums1_{k}", [P, NP], F32)) for k in range(2)]
    with ExitStack() as ctx:
        sb = lambda name, shape, dt=F32: ctx.enter_context(nc.sbuf_tensor(name, shape, dt))
        ps = lambda name, shape, dt=F32: ctx.enter_context(nc.psum_tensor(name, shape, dt))
        sem = lambda name: ctx.enter_context(nc.semaphore(name))
        rows = sb("rows2", [P, QUADS, QW])
        message = sb("message", [P, QUADS, QW])
        inverse = sb("inverse", [P, P])
        alpha = sb("alpha", [P, P])
        coefs = sb("coefs", [P, QUADS, QW])
        onehot_in = sb("onehot_in", [P, QUADS, QW], BF16)
        onehot = sb("onehot", [P, QUADS, QT, P])
        tile_sums = [ps(f"tile_sums1_{i}", [P, QT, P]) for i in range(QUADS)]
        alpha_ps = ps("alpha_ps", [P, QUADS, QT * HEADS])
        rows_in = [sem(f"rows_in{q}") for q in range(QUADS)]
        inverse_made = sem("inverse_made")
        alpha_made = sem("alpha_made")
        alpha_turned = sem("alpha_turned")
        coefs_made = sem("coefs_made")
        message_made = sem("message_made")
        onehot_made = sem("onehot_made1")
        summed = sem("summed1")
        added = sem("added1")
        cleared = sem("cleared1")
        with nc.Block() as block:
            @block.sync
            def _(sp):
                def body(j, first, last):
                    for q in range(QUADS):
                        if not first:
                            sp.wait_ge(message_made, j * QUADS + q - QUADS + 1)
                            sp.wait_ge(onehot_made, j * QUADS + q - QUADS + 1)
                        sp.dma_start(rows[:, q, :], xl_edges[bass.ds(j, 1), :, q * QW:(q + 1) * QW].rearrange("a p e -> (a p) e")
                                     ).then_inc(rows_in[q], DMA)
                        sp.dma_start(onehot_in[:, q, :],
                                     onehot_edges[bass.ds(j, 1), :, q * QW:(q + 1) * QW].rearrange("a p e -> (a p) e")
                                     ).then_inc(rows_in[q], DMA)
                groups_of(sp, groups, body)

            @block.scalar
            def _(act):
                def body(j, first, last):
                    for q in range(QUADS):
                        act.wait_ge(alpha_turned, j + 1)
                        if not first:
                            act.wait_ge(message_made, j * QUADS + q - QUADS + 1)
                        nc.scalar.copy(coefs[:, q, :].rearrange("p (a b) -> p a b", b=HC),
                                       alpha_ps[:, q, :].unsqueeze(2).to_broadcast([P, QT * HEADS, HC])
                                       ).then_inc(coefs_made, 1)
                        act.wait_ge(rows_in[q], (j + 1) * 2 * DMA)
                        if not first:
                            act.wait_ge(summed, j * QUADS + q - QUADS + 1)
                        nc.scalar.copy(onehot[:, q].rearrange("p i n -> p (i n)"),
                                       onehot_in[:, q, :]).then_inc(onehot_made, 1)
                groups_of(act, groups, body)

            @block.gpsimd
            def _(pool):
                nc.gpsimd.memset(node_sums[1][:], 0.0).then_inc(cleared, 1)

                def body(j, first, last):
                    for q in range(QUADS):
                        pool.wait_ge(rows_in[q], (j + 1) * 2 * DMA)
                        pool.wait_ge(coefs_made, j * QUADS + q + 1)
                        if not first:
                            pool.wait_ge(summed, j * QUADS + q - QUADS + 1)
                        nc.gpsimd.tensor_tensor(message[:, q, :], rows[:, q, :], coefs[:, q, :],
                                                ALU.mult).then_inc(message_made, 1)
                groups_of(pool, groups, body)

            @block.tensor
            def _(pe):
                def turn(j, start):
                    pe.wait_ge(alpha_made, j + 1)
                    if not start:
                        pe.wait_ge(coefs_made, j * QUADS)
                    nc.tensor.transpose(alpha_ps[:].rearrange("p q n -> p (q n)"), alpha[:], ident[:]
                                        ).then_inc(alpha_turned, 1)

                turn(0, True)

                def body(j, first, last):
                    for q in range(QUADS):
                        pe.wait_ge(onehot_made, j * QUADS + q + 1)
                        pe.wait_ge(message_made, j * QUADS + q + 1)
                        if not first:
                            pe.wait_ge(added, (j * QUADS + q - QUADS + 1) * QT)
                        for i in range(QT):
                            mm = nc.tensor.matmul(tile_sums[q][:, i, :], message[:, q, i * P:(i + 1) * P],
                                                  onehot[:, q, i, :], start=True, stop=True)
                        mm.then_inc(summed, 1)
                        if q == 0 and not last:
                            turn(j + 1, False)
                groups_of(pe, groups, body)

            @block.vector
            def _(dve):
                def add_tile(j, q, i, base, start=False):
                    if not (start and q == 0 and i < 2):
                        dve.wait_ge(added, (j * QUADS + q) * QT + i - 1)
                    span = node_sums[i % 2][:, bass.ds(base, P)]
                    nc.vector.tensor_tensor(span, span, tile_sums[q][:, i, :], ALU.add).then_inc(added, 1)

                def invert(j, start=False):
                    if not start:
                        dve.wait_ge(alpha_made, j)
                    nc.vector.reciprocal(inverse[:], largest[:, bass.ds(j * P, P)]).then_inc(inverse_made, 1)

                def weigh(j, start=False):
                    at = bass.ds(j * P, P)
                    dve.wait_ge(inverse_made, j + 1)
                    if not start:
                        dve.wait_ge(alpha_turned, j)
                    nc.vector.tensor_tensor(alpha[:], logits[:, at], inverse[:], ALU.mult).then_inc(alpha_made, 1)

                for j in range(2):
                    invert(j, j == 0)
                    weigh(j, j == 0)
                nc.vector.memset(node_sums[0][:], 0.0).then_inc(cleared, 1)
                dve.wait_ge(cleared, 2)

                def body(j, first, ahead):
                    if ahead:
                        invert(j + 2)
                    bases = window_bases(dve, j, 0, CHUNKS)
                    for q in range(QUADS):
                        if q == 2 and ahead:
                            weigh(j + 2)
                        dve.wait_ge(summed, j * QUADS + q + 1)
                        for i in range(QT):
                            add_tile(j, q, i, bases[q * QT + i], first)

                body(0, True, True)
                with dve.Fori(1, groups - 2) as j:
                    body(j, False, True)
                for j in (groups - 2, groups - 1):
                    body(j, False, False)
                dve.wait_ge(added, tiles)


    FC = 4
    with ExitStack() as ctx:
        sb = lambda name, shape, dt=F32: ctx.enter_context(nc.sbuf_tensor(name, shape, dt))
        ps = lambda name, shape, dt=F32: ctx.enter_context(nc.psum_tensor(name, shape, dt))
        sem = lambda name: ctx.enter_context(nc.semaphore(name))
        fc = sb("fc", [P, FC * P])
        proj = sb("proj", [P, FC, P])
        a_bias = sb("a_bias", [P, P])
        ln2_col = sb("ln2_col", [P, 1])
        x1_bias = sb("x1_bias", [P, 2, QT, P])
        x2 = sb("x2", [P, 2, QT, P])
        x12 = sb("x12", [P, 2, QT, P])
        total = sb("total", [P, 2, QT, P])
        u = sb("u1", [P, 2, QT, P])
        result = sb("result", [P, 2, QT, P])
        stats = sb("stats1", [P, 2, QT, 6])
        mv = sb("mv1", [P, 2, QT, 2])
        std = sb("std1", [P, 2, QT])
        rstd = sb("rstd1", [P, 2, QT])
        hT = sb("hT1", [P, QW])
        hidden = logits[:, 0:2 * FC * QW].rearrange("p (a k e) -> p a k e", a=2, k=FC)
        a_ps = ps("a_ps", [P, QT, P])
        t_ps = ps("t_ps1", [P, QW])
        f_ps = [ps(f"f_ps{i}", [P, QW]) for i in range(FC)]
        y_ps = ps("y_ps", [P, QT, P])
        weights_in = sem("mlp_weights_in")
        fc_scaled = sem("fc_scaled")
        step = sem("dve_step1")
        merged = sem("sums_merged")
        biased = sem("x1_biased")
        row_major = sem("row_major")
        x2_made = sem("x2_made")
        var_ready = [sem(f"var_ready1_{k}") for k in range(2)]
        std_ready = [sem(f"std_ready1_{k}") for k in range(2)]
        u_ready = sem("u_ready1")
        x12_ready = sem("x12_ready")
        turned = sem("turned1")
        hT_ready = sem("hT_ready1")
        fc_ready = sem("fc_ready")
        relu_ready = sem("relu_ready")
        y_ready = sem("y_ready")
        total_ready = sem("total_ready")
        result_ready = sem("result_ready")
        out_stored = [sem(f"out_stored{i}") for i in range(2)]
        out_dram = t["out"].rearrange("(b i p) d -> b p i d", i=QT, p=P)

        def all_steps(stages):
            for s in range(-4, node_groups + 3):
                for lag, stage in stages:
                    if 0 <= s - lag < node_groups:
                        stage(s - lag)

        with nc.Block() as block:
            @block.sync
            def _(sp):
                sp.dma_start(a_bias[:], t["attn_bias"].to_broadcast([P, P])).then_inc(weights_in, DMA)
                sp.dma_start(ln2_col[:], t["ln2_w"].rearrange("o d -> d o"), allow_slow_non_contiguous=True
                             ).then_inc(weights_in, DMA)
                sp.dma_start(fc[:], t["fc_wT"]).then_inc(weights_in, DMA)
                sp.dma_start(proj[:], t["proj_wT"].rearrange("(k p) d -> p k d", p=P)).then_inc(weights_in, DMA)
                for b in range(node_groups):
                    sp.wait_ge(result_ready, b + 1)
                    sp.dma_start(out_dram[b], result[:, b % 2]).then_inc(out_stored[b % 2], DMA)
                for i in range(2):
                    sp.wait_ge(out_stored[i], (node_groups + 1 - i) // 2 * DMA)

            @block.tensor
            def _(pe):
                def turn_sums(b):
                    pe.wait_ge(merged, b + 1)
                    if b:
                        pe.wait_ge(x2_made, b)
                    for i in range(QT):
                        at = b * QW + i * P
                        mm = nc.tensor.transpose(a_ps[:, i, :], node_sums[0][:, at:at + P], ident[:])
                    mm.then_inc(row_major, 1)

                def turn_u(b):
                    pe.wait_ge(u_ready, b + 1)
                    for i in range(QT):
                        mm = nc.tensor.transpose(t_ps[:, i * P:(i + 1) * P], u[:, b % 2, i, :], ident[:])
                    mm.then_inc(turned, 1)

                def expand(b):
                    pe.wait_ge(hT_ready, b + 1)
                    for k in range(FC):
                        if b:
                            pe.wait_ge(relu_ready, FC * (b - 1) + k + 1)
                        nc.tensor.matmul(f_ps[k][:], fc[:, k * P:(k + 1) * P], hT[:], start=True,
                                         stop=True).then_inc(fc_ready, 1)

                def contract(b):
                    pe.wait_ge(relu_ready, FC * (b + 1))
                    if b:
                        pe.wait_ge(total_ready, b)
                    for i in range(QT):
                        for k in range(FC):
                            mm = nc.tensor.matmul(y_ps[:, i, :], hidden[:, b % 2, k, i * P:(i + 1) * P], proj[:, k, :],
                                                  start=(k == 0), stop=(k == FC - 1))
                    mm.then_inc(y_ready, 1)

                pe.wait_ge(weights_in, 4 * DMA)
                pe.wait_ge(fc_scaled, 1)
                all_steps([(0, turn_u), (1, contract), (0, expand), (-2, turn_sums)])

            @block.scalar
            def _(act):
                def root(b, k):
                    act.wait_ge(var_ready[k], b + 1)
                    nc.scalar.activation(std[:, k, :], mv[:, k, :, 1], ACT.Sqrt,
                                         bias=eps_col[:, 0:1]).then_inc(std_ready[k], 1)

                def copy_hT(b):
                    act.wait_ge(turned, b + 1)
                    if b:
                        act.wait_ge(fc_ready, FC * b)
                    nc.scalar.copy(hT[:], t_ps[:]).then_inc(hT_ready, 1)

                def relu(b):
                    if b >= 2:
                        act.wait_ge(y_ready, b - 1)
                    for k in range(FC):
                        act.wait_ge(fc_ready, FC * b + k + 1)
                        nc.scalar.activation(hidden[:, b % 2, k, :], f_ps[k][:], ACT.Relu).then_inc(relu_ready, 1)

                all_steps([(0, copy_hT), (-1, lambda b: root(b, 0)), (0, relu), (1, lambda b: root(b, 1))])

            @block.gpsimd
            def _(pool):
                def merge(b):
                    both = [part[:, b * QW:(b + 1) * QW] for part in node_sums]
                    nc.gpsimd.tensor_tensor(both[0], both[0], both[1], ALU.add).then_inc(merged, 1)

                def bias(b):
                    if b >= 2:
                        pool.wait_ge(x2_made, b - 1)
                    nc.gpsimd.tensor_tensor(x1_bias[:, b % 2], x1[:, b], a_bias[:].unsqueeze(1).to_broadcast([P, QT, P]),
                                            ALU.add).then_inc(biased, 1)

                def residual(b):
                    pool.wait_ge(x2_made, b + 1)
                    if b >= 2:
                        pool.wait_ge(total_ready, b - 1)
                    nc.gpsimd.tensor_tensor(x12[:, b % 2], x2[:, b % 2], x1[:, b], ALU.add).then_inc(x12_ready, 1)

                pool.wait_ge(weights_in, 4 * DMA)
                all_steps([(-3, merge), (-2, bias), (-1, residual)])

            @block.vector
            def _(dve):
                n = [0]

                def link(ins):
                    n[0] += 1
                    ins.then_inc(step, 1)
                    dve.wait_ge(step, n[0])

                def moments(k, src):
                    for i in range(QT):
                        ins = nc.vector.bn_stats(stats[:, k, i, :], src[:, i, :])
                    link(ins)
                    for i in range(QT):
                        ins = nc.vector.bn_aggr(mv[:, k, i, :], stats[:, k, i, :])
                    ins.then_inc(var_ready[k], 1)

                def scaled(b, k, out, src):
                    dve.wait_ge(std_ready[k], b + 1)
                    link(nc.vector.reciprocal(rstd[:, k, :], std[:, k, :]))
                    for i in range(QT):
                        ins = nc.vector.tensor_scalar(out[:, i, :], src[:, i, :], mv[:, k, i, 0:1], rstd[:, k, i:i + 1],
                                                      ALU.subtract, ALU.mult)
                    return ins

                def residual(b):
                    dve.wait_ge(row_major, b + 1)
                    dve.wait_ge(biased, b + 1)
                    if b >= 2:
                        dve.wait_ge(x12_ready, b - 1)
                    nc.vector.tensor_tensor(x2[:, b % 2], a_ps[:], x1_bias[:, b % 2], ALU.add).then_inc(x2_made, 1)
                    dve.wait_ge(x2_made, b + 1)
                    moments(0, x2[:, b % 2])

                def norm0(b):
                    if b >= 2:
                        dve.wait_ge(turned, b - 1)
                    scaled(b, 0, u[:, b % 2], x2[:, b % 2]).then_inc(u_ready, 1)

                def add_mlp(b):
                    dve.wait_ge(y_ready, b + 1)
                    dve.wait_ge(x12_ready, b + 1)
                    nc.vector.tensor_tensor(total[:, b % 2], y_ps[:], x12[:, b % 2], ALU.add).then_inc(total_ready, 1)
                    dve.wait_ge(total_ready, b + 1)
                    moments(1, total[:, b % 2])

                def norm1(b):
                    if b >= 2:
                        dve.wait_ge(out_stored[b % 2], b // 2 * DMA)
                    scaled(b, 1, result[:, b % 2], total[:, b % 2]).then_inc(result_ready, 1)

                dve.wait_ge(weights_in, 4 * DMA)
                nc.vector.tensor_scalar(fc[:], fc[:], ln2_col[:, 0:1], None, ALU.mult).then_inc(fc_scaled, 1)
                all_steps([(-1, residual), (2, norm1), (-1, norm0), (1, add_mlp)])
    sums.close()
    attention.close()
    persistent.close()


def kernel(x, src, dst, edge_attr_128, **w):
    import numpy as np
    import concourse.bacc as bacc
    from concourse.bass_utils import run_bass_kernel_spmd

    x, src, dst, attr = (np.asarray(a) for a in (x, src, dst, edge_attr_128))
    w = {k: np.asarray(v) for k, v in w.items()}
    N, D = x.shape
    E = src.shape[0]
    groups, node_groups = sizes(N, E)
    EP, NP, tiles = groups * CHUNKS * P, node_groups * QW, groups * CHUNKS

    def edges(a, fill):
        full = np.full((EP,) + a.shape[1:], fill, a.dtype)
        full[:E] = a
        return full.reshape((CHUNKS, groups, P) + a.shape[1:])

    def row(a):
        return np.ascontiguousarray(a.reshape(1, -1))

    def turned(a):
        return np.ascontiguousarray(a.T)

    srcs, dsts = edges(src, 0), edges(dst, N)
    xp = np.zeros((NP, D), x.dtype)
    xp[:N] = x
    beside = np.full((EP + 2,), -1, dst.dtype)
    beside[1:-1] = dsts.reshape(-1)
    halo = np.lib.stride_tricks.as_strided(beside, (groups, CHUNKS, P + 2), [n * beside.itemsize
                                                                             for n in (P, groups * P, 1)])
    arrays = {
        "x": xp,
        "dst_halo": np.ascontiguousarray(halo),
        "xT": turned(xp),
        "src_cols": np.ascontiguousarray(srcs.transpose(2, 1, 0)).reshape(P, tiles),
        "dst_cols": np.ascontiguousarray(dsts.transpose(2, 1, 0)).reshape(P, tiles),
        "dst_rows": np.ascontiguousarray(dsts.transpose(1, 0, 2)).reshape(tiles, P),
        "first_dst": np.ascontiguousarray(dsts[:, :, 0].T).reshape(1, tiles),
        "dst_nat": beside,
        "attrT": np.ascontiguousarray(edges(attr, 0).transpose(1, 3, 0, 2)).reshape(groups, D, CHUNKS * P),
        "Wqk": w["L0_gnn_Wqk"], "Wv": w["L0_gnn_Wv"], "Wo": w["L0_gnn_Wo"],
        "bqk": row(w["L0_gnn_bqk"]), "bv": row(w["L0_gnn_bv"]), "bo": row(w["L0_gnn_bo"]),
        "gamma": row(w["L0_gnn_gamma"]), "beta": row(w["L0_gnn_beta"]),
        "ln1_w": row(w["L1_gnn_ln1_w"]), "ln2_w": row(w["L1_gnn_ln2_w"]),
        "lin_l_wT": turned(w["L1_gnn_lin_l_w"]), "lin_r_wT": turned(w["L1_gnn_lin_r_w"]),
        "lin_l_b": row(w["L1_gnn_lin_l_b"]), "lin_r_b": row(w["L1_gnn_lin_r_b"]),
        "lin_edge_wT": turned(w["L1_gnn_lin_edge_w"]), "att": w["L1_gnn_att"],
        "attn_bias": row(w["L1_gnn_attn_bias"]),
        "fc_wT": turned(w["L1_gnn_fc_w"]), "proj_wT": turned(w["L1_gnn_proj_w"]),
    }
    nc = bacc.Bacc("TRN2", target_bir_lowering=False, num_devices=1)
    t = {k: nc.dram_tensor("in_" + k, a.shape, mybir.dt.from_np(a.dtype), kind="ExternalInput").ap()
         for k, a in arrays.items()}
    t["out"] = nc.dram_tensor("out_nodes", (NP, D), F32, kind="ExternalOutput").ap()
    build(nc, t, N, E)
    r = run_bass_kernel_spmd(nc, [{"in_" + k: a for k, a in arrays.items()}], core_ids=[0])
    return r.results[0]["out_nodes"][:N]
```
